# Optimizing a Trainium2 kernel written in Bass

```python
import numpy as np
import jax
import jax.numpy as jnp

def _softmax(x, axis=-1):
    return jax.nn.softmax(x, axis=axis)

def _gelu(x):
    return jax.nn.gelu(x, approximate=True)

def _silu(x):
    return jax.nn.silu(x)

def _sigmoid(x):
    return jax.nn.sigmoid(x)

def _layernorm(x, axis=-1, eps=1e-05):
    m = jnp.mean(x, axis=axis, keepdims=True)
    v = jnp.var(x, axis=axis, keepdims=True)
    return (x - m) / jnp.sqrt(v + eps)

def _scatter_add(tgt, idx, src, axis=0):
    return tgt.at[idx].add(src)

def _segment_sum(src, seg, n):
    return jax.ops.segment_sum(src, seg, n)
kernel_name = 'mk_lm_tower_d2_tok_ids768_r4_d96c30'

def setup_inputs(seed: int=0):
    np.random.seed(seed)
    _w = jnp.asarray

    def _rec_inputs():
        import jax
        import jax.numpy as jnp
        _rk = jax.random.key(seed)
        x = jax.random.randint(jax.random.fold_in(_rk, 1), (16, 256), 0, 31993, jnp.int32)
        return x
    x = _rec_inputs()

    def _L0_tok_setup():
        import jax, jax.numpy as jnp
        import numpy as np
        B, S, D, L, K, V = (8, 256, 192, 4, 4, 8000)
        N = D
        EPS = 1e-05

        def _layernorm(x, g, b):
            m = jnp.mean(x, axis=-1, keepdims=True)
            v = jnp.mean(jnp.square(x - m), axis=-1, keepdims=True)
            return (x - m) * jax.lax.rsqrt(v + EPS) * g + b

        def _dwconv_causal(u, w, b):
            lhs = u.transpose(0, 2, 1)
            rhs = w[:, None, :]
            out = jax.lax.conv_general_dilated(lhs, rhs, window_strides=(1,), padding=[(K - 1, 0)], dimension_numbers=('NCH', 'OIH', 'NCH'), feature_group_count=D)
            return out.transpose(0, 2, 1) + b

        def _selective_scan(u, delta, Bm, Cm):
            decay = jnp.exp(-delta)
            inp = u * Bm
            h0 = jnp.zeros((u.shape[0], N), u.dtype)
            xs = (decay.transpose(1, 0, 2), inp.transpose(1, 0, 2), Cm.transpose(1, 0, 2))

            def step(h, x):
                d, i, c = x
                h = h * d + i
                return (h, jnp.sum(h * c, axis=-1))
            _, ys = jax.lax.scan(step, h0, xs)
            return ys.T[..., None]

        def _block(x, g, bt, Wi, bi, cw, cb, wd, bd_, wB, bB_, wC, bC_, wo, bo):
            h = _layernorm(x, g, bt)
            uv = h @ Wi.T + bi
            u, v = (uv[..., :D], uv[..., D:])
            uc = _dwconv_causal(u, cw, cb)
            delta = jax.nn.softplus(uc @ wd.T + bd_)
            Bm = uc @ wB.T + bB_
            Cm = uc @ wC.T + bC_
            y = _selective_scan(uc, delta, Bm, Cm)
            y = y * jax.nn.sigmoid(v)
            return x + (y @ wo.T + bo)
        key = jax.random.key(seed)
        ks = jax.random.split(key, 12)
        rn = lambda k, shp, s=0.02: jax.random.normal(k, shp, jnp.float32) * s
        return dict(tokens=jax.random.randint(ks[0], (B, S), 0, V), embedding=rn(ks[1], (V, D)), pos_enc=rn(ks[2], (256, D)), ln_g=jnp.ones((L, D), jnp.float32), ln_b=jnp.zeros((L, D), jnp.float32), Win=rn(ks[3], (L, 2 * D, D)), b_in=jnp.zeros((L, 2 * D), jnp.float32), convw=rn(ks[4], (L, D, K), 0.1), convb=jnp.zeros((L, D), jnp.float32), Wd=rn(ks[5], (L, N, D)), bd=jnp.zeros((L, N), jnp.float32), WB=rn(ks[6], (L, N, D)), bB=jnp.zeros((L, N), jnp.float32), WC=rn(ks[7], (L, N, D)), bC=jnp.zeros((L, N), jnp.float32), Wout=rn(ks[8], (L, D, D)), bout=jnp.zeros((L, D), jnp.float32))
    _L0_tok_all = _L0_tok_setup()
    _L0_tok_in = {k: v for k, v in _L0_tok_all.items() if k in ('embedding', 'pos_enc', 'ln_g', 'ln_b', 'Win', 'b_in', 'convw', 'convb', 'Wd', 'bd', 'WB', 'bB', 'WC', 'bC', 'Wout', 'bout')}
    del _L0_tok_all

    def _L0_attn_setup():
        import jax, jax.numpy as jnp
        import numpy as np
        D_MODEL = 192
        H = 6
        DQK = 128
        DV = 64
        SCALE_BASE = 512.0

        def _xpos(x, sign):
            B, T, Hn, d = x.shape
            half = d // 2
            pos = jnp.arange(T, dtype=jnp.float32)
            inv_freq = 1.0 / 10000.0 ** (jnp.arange(half, dtype=jnp.float32) / half)
            angles = pos[:, None] * inv_freq[None, :]
            zeta = (jnp.arange(half, dtype=jnp.float32) + half) / d
            decay = zeta[None, :] ** (sign * pos[:, None] / SCALE_BASE)
            cos_a = (jnp.cos(angles) * decay)[None, :, None, :]
            sin_a = (jnp.sin(angles) * decay)[None, :, None, :]
            x1, x2 = (x[..., :half], x[..., half:])
            return jnp.concatenate([x1 * cos_a - x2 * sin_a, x1 * sin_a + x2 * cos_a], axis=-1)

        def _decay_mask(T):
            gammas = jnp.array([1.0 - 2.0 ** (-(5 + h)) for h in range(H)], dtype=jnp.float32)
            i = jnp.arange(T, dtype=jnp.float32)
            diff = i[:, None] - i[None, :]
            causal = (diff >= 0).astype(jnp.float32)
            D = gammas[:, None, None] ** jnp.clip(diff, 0.0)[None] * causal[None]
            row = jnp.clip(jnp.sum(D, axis=-1, keepdims=True), 1e-06)
            return D / jnp.sqrt(row)
        key = jax.random.key(seed)
        ks = jax.random.split(key, 6)
        B, T = (2, 512)

        def xavier(k, shape):
            lim = float(np.sqrt(6.0 / (shape[0] + shape[1])))
            return jax.random.uniform(k, shape, jnp.float32, -lim, lim)
        return {'x': jax.random.normal(ks[0], (B, T, D_MODEL), jnp.float32), 'Wq': xavier(ks[1], (D_MODEL, H * DQK)), 'Wk': xavier(ks[2], (D_MODEL, H * DQK)), 'Wv': xavier(ks[3], (D_MODEL, H * DV)), 'Wg': xavier(ks[4], (D_MODEL, H * DV)), 'Wo': xavier(ks[5], (H * DV, D_MODEL)), 'gn_weight': jnp.ones((H * DV,), jnp.float32), 'gn_bias': jnp.zeros((H * DV,), jnp.float32)}
    _L0_attn_all = _L0_attn_setup()
    _L0_attn_in = {k: v for k, v in _L0_attn_all.items() if k in ('Wq', 'Wk', 'Wv', 'Wg', 'Wo', 'gn_weight', 'gn_bias')}
    del _L0_attn_all

    def _L0_ffn_setup():
        import jax, jax.numpy as jnp
        import numpy as np
        EPS_NORM = 1e-05
        RMS_EPS = 1e-05

        def _l2_normalize(v):
            n = jnp.sqrt(jnp.sum(v * v, axis=-1, keepdims=True))
            return v / jnp.maximum(n, EPS_NORM)

        def _rms_norm(x, weight, eps):
            ms = jnp.mean(x * x, axis=-1, keepdims=True)
            return x * jax.lax.rsqrt(ms + eps) * weight
        key = jax.random.key(seed)
        ks = jax.random.split(key, 6)
        B, T, D = (8, 1024, 192)
        S, F = (64, 768)
        x = jax.random.normal(ks[0], (B, T, D), dtype=jnp.float32)
        slots = 0.02 * jax.random.normal(ks[1], (S, D), dtype=jnp.float32)
        scale = jnp.ones((S,), dtype=jnp.float32)
        fc1_weight = 0.02 * jax.random.normal(ks[2], (S, D, F), dtype=jnp.float32)
        fc1_bias = jnp.zeros((S, F), dtype=jnp.float32)
        fc2_weight = 0.02 * jax.random.normal(ks[3], (S, F, D), dtype=jnp.float32)
        fc2_bias = jnp.zeros((S, D), dtype=jnp.float32)
        norm_weight = jnp.ones((D,), dtype=jnp.float32)
        return {'x': x, 'slots': slots, 'scale': scale, 'fc1_weight': fc1_weight, 'fc1_bias': fc1_bias, 'fc2_weight': fc2_weight, 'fc2_bias': fc2_bias, 'norm_weight': norm_weight}
    _L0_ffn_all = _L0_ffn_setup()
    _L0_ffn_in = {k: v for k, v in _L0_ffn_all.items() if k in ('slots', 'scale', 'fc1_weight', 'fc1_bias', 'fc2_weight', 'fc2_bias', 'norm_weight')}
    del _L0_ffn_all

    def _L1_attn_setup():
        import jax, jax.numpy as jnp
        import numpy as np
        import math
        DIM = 192
        NUM_HEADS = 12

        def _xavier_uniform(key, out_f, in_f):
            a = math.sqrt(6.0 / (in_f + out_f))
            return jax.random.uniform(key, (out_f, in_f), jnp.float32, -a, a)
        key = jax.random.key(seed)
        k_x, k_qw, k_qB, k_pw, k_pB = jax.random.split(key, 5)
        B, N = (16, 256)
        x = jax.random.normal(k_x, (B, N, DIM), jnp.float32)
        qkv_w = _xavier_uniform(k_qw, 3 * DIM, DIM)
        qkv_b = jnp.zeros((3 * DIM,), jnp.float32)
        qkv_B = jax.random.normal(k_qB, (3 * DIM, DIM), jnp.float32) * math.sqrt(1.0 / DIM)
        proj_w = _xavier_uniform(k_pw, DIM, DIM)
        proj_b = jnp.zeros((DIM,), jnp.float32)
        proj_B = jax.random.normal(k_pB, (DIM, DIM), jnp.float32) * math.sqrt(1.0 / DIM)
        return {'x': x, 'qkv_w': qkv_w, 'qkv_b': qkv_b, 'qkv_B': qkv_B, 'proj_w': proj_w, 'proj_b': proj_b, 'proj_B': proj_B}
    _L1_attn_all = _L1_attn_setup()
    _L1_attn_in = {k: v for k, v in _L1_attn_all.items() if k in ('qkv_w', 'qkv_b', 'qkv_B', 'proj_w', 'proj_b', 'proj_B')}
    del _L1_attn_all

    def _L1_ffn_setup():
        import jax, jax.numpy as jnp
        import numpy as np
        ATOM = {'vm': 0, 'im': 1, 'cm': 2, 'sc': 3, 'cc': 4}
        TASK_PAIRS = [('vm', 'sc'), ('vm', 'cc'), ('im', 'sc'), ('im', 'cc'), ('cm', 'sc'), ('cm', 'cc')]
        SRC_IDX = np.array([[ATOM[l], ATOM[r]] for l, r in TASK_PAIRS], dtype=np.int32)
        DST_IDX = np.array([[ATOM[r], ATOM[l]] for l, r in TASK_PAIRS], dtype=np.int32)
        NCLS = 6
        NATOMS = 5

        def _l2norm(x, eps=1e-12):
            return x / jnp.clip(jnp.linalg.norm(x, axis=-1, keepdims=True), eps)
        key = jax.random.key(seed)
        ks = jax.random.split(key, 12)
        B, NPATCH, D, H = (64, 197, 192, 768)
        std = 0.02
        x = jax.random.normal(ks[0], (B, NCLS + NPATCH, D), dtype=jnp.float32)
        fc1_w = jax.random.normal(ks[1], (H, D), dtype=jnp.float32) * std
        fc1_b = jnp.zeros((H,), jnp.float32)
        fc2_w = jax.random.normal(ks[2], (D, H), dtype=jnp.float32) * std
        fc2_b = jnp.zeros((D,), jnp.float32)
        gate_pair = jax.random.normal(ks[3], (NCLS, 2, D), dtype=jnp.float32) * std
        atom_in_w = jax.random.normal(ks[4], (NATOMS, H, D), dtype=jnp.float32) * std
        atom_in_b = jax.random.normal(ks[5], (NATOMS, H), dtype=jnp.float32) * std
        atom_out_w = jax.random.normal(ks[6], (NATOMS, D, H), dtype=jnp.float32) * std
        atom_out_b = jax.random.normal(ks[7], (NATOMS, D), dtype=jnp.float32) * std
        balance_bias = jnp.zeros((NCLS, 2), jnp.float32)
        return {'x': x, 'fc1_w': fc1_w, 'fc1_b': fc1_b, 'fc2_w': fc2_w, 'fc2_b': fc2_b, 'gate_pair': gate_pair, 'atom_in_w': atom_in_w, 'atom_in_b': atom_in_b, 'atom_out_w': atom_out_w, 'atom_out_b': atom_out_b, 'balance_bias': balance_bias}
    _L1_ffn_all = _L1_ffn_setup()
    _L1_ffn_in = {k: v for k, v in _L1_ffn_all.items() if k in ('fc1_w', 'fc1_b', 'fc2_w', 'fc2_b', 'gate_pair', 'atom_in_w', 'atom_in_b', 'atom_out_w', 'atom_out_b', 'balance_bias')}
    del _L1_ffn_all
    return {'x': x, 'L0_tok_embedding': _L0_tok_in['embedding'], 'L0_tok_pos_enc': _L0_tok_in['pos_enc'], 'L0_tok_ln_g': _L0_tok_in['ln_g'], 'L0_tok_ln_b': _L0_tok_in['ln_b'], 'L0_tok_Win': _L0_tok_in['Win'], 'L0_tok_b_in': _L0_tok_in['b_in'], 'L0_tok_convw': _L0_tok_in['convw'], 'L0_tok_convb': _L0_tok_in['convb'], 'L0_tok_Wd': _L0_tok_in['Wd'], 'L0_tok_bd': _L0_tok_in['bd'], 'L0_tok_WB': _L0_tok_in['WB'], 'L0_tok_bB': _L0_tok_in['bB'], 'L0_tok_WC': _L0_tok_in['WC'], 'L0_tok_bC': _L0_tok_in['bC'], 'L0_tok_Wout': _L0_tok_in['Wout'], 'L0_tok_bout': _L0_tok_in['bout'], 'L0_attn_Wq': _L0_attn_in['Wq'], 'L0_attn_Wk': _L0_attn_in['Wk'], 'L0_attn_Wv': _L0_attn_in['Wv'], 'L0_attn_Wg': _L0_attn_in['Wg'], 'L0_attn_Wo': _L0_attn_in['Wo'], 'L0_attn_gn_weight': _L0_attn_in['gn_weight'], 'L0_attn_gn_bias': _L0_attn_in['gn_bias'], 'L0_ffn_slots': _L0_ffn_in['slots'], 'L0_ffn_scale': _L0_ffn_in['scale'], 'L0_ffn_fc1_weight': _L0_ffn_in['fc1_weight'], 'L0_ffn_fc1_bias': _L0_ffn_in['fc1_bias'], 'L0_ffn_fc2_weight': _L0_ffn_in['fc2_weight'], 'L0_ffn_fc2_bias': _L0_ffn_in['fc2_bias'], 'L0_ffn_norm_weight': _L0_ffn_in['norm_weight'], 'L1_attn_qkv_w': _L1_attn_in['qkv_w'], 'L1_attn_qkv_b': _L1_attn_in['qkv_b'], 'L1_attn_qkv_B': _L1_attn_in['qkv_B'], 'L1_attn_proj_w': _L1_attn_in['proj_w'], 'L1_attn_proj_b': _L1_attn_in['proj_b'], 'L1_attn_proj_B': _L1_attn_in['proj_B'], 'L1_ffn_fc1_w': _L1_ffn_in['fc1_w'], 'L1_ffn_fc1_b': _L1_ffn_in['fc1_b'], 'L1_ffn_fc2_w': _L1_ffn_in['fc2_w'], 'L1_ffn_fc2_b': _L1_ffn_in['fc2_b'], 'L1_ffn_gate_pair': _L1_ffn_in['gate_pair'], 'L1_ffn_atom_in_w': _L1_ffn_in['atom_in_w'], 'L1_ffn_atom_in_b': _L1_ffn_in['atom_in_b'], 'L1_ffn_atom_out_w': _L1_ffn_in['atom_out_w'], 'L1_ffn_atom_out_b': _L1_ffn_in['atom_out_b'], 'L1_ffn_balance_bias': _L1_ffn_in['balance_bias']}

def reference(x, L0_tok_embedding, L0_tok_pos_enc, L0_tok_ln_g, L0_tok_ln_b, L0_tok_Win, L0_tok_b_in, L0_tok_convw, L0_tok_convb, L0_tok_Wd, L0_tok_bd, L0_tok_WB, L0_tok_bB, L0_tok_WC, L0_tok_bC, L0_tok_Wout, L0_tok_bout, L0_attn_Wq, L0_attn_Wk, L0_attn_Wv, L0_attn_Wg, L0_attn_Wo, L0_attn_gn_weight, L0_attn_gn_bias, L0_ffn_slots, L0_ffn_scale, L0_ffn_fc1_weight, L0_ffn_fc1_bias, L0_ffn_fc2_weight, L0_ffn_fc2_bias, L0_ffn_norm_weight, L1_attn_qkv_w, L1_attn_qkv_b, L1_attn_qkv_B, L1_attn_proj_w, L1_attn_proj_b, L1_attn_proj_B, L1_ffn_fc1_w, L1_ffn_fc1_b, L1_ffn_fc2_w, L1_ffn_fc2_b, L1_ffn_gate_pair, L1_ffn_atom_in_w, L1_ffn_atom_in_b, L1_ffn_atom_out_w, L1_ffn_atom_out_b, L1_ffn_balance_bias):
    import jax
    import jax.numpy as jnp

    def _L0_tok_ref(tokens, embedding, pos_enc, ln_g, ln_b, Win, b_in, convw, convb, Wd, bd, WB, bB, WC, bC, Wout, bout):
        import jax, jax.numpy as jnp
        import numpy as np
        B, S, D, L, K, V = (8, 256, 192, 4, 4, 8000)
        N = D
        EPS = 1e-05

        def _layernorm(x, g, b):
            m = jnp.mean(x, axis=-1, keepdims=True)
            v = jnp.mean(jnp.square(x - m), axis=-1, keepdims=True)
            return (x - m) * jax.lax.rsqrt(v + EPS) * g + b

        def _dwconv_causal(u, w, b):
            lhs = u.transpose(0, 2, 1)
            rhs = w[:, None, :]
            out = jax.lax.conv_general_dilated(lhs, rhs, window_strides=(1,), padding=[(K - 1, 0)], dimension_numbers=('NCH', 'OIH', 'NCH'), feature_group_count=D)
            return out.transpose(0, 2, 1) + b

        def _selective_scan(u, delta, Bm, Cm):
            decay = jnp.exp(-delta)
            inp = u * Bm
            h0 = jnp.zeros((u.shape[0], N), u.dtype)
            xs = (decay.transpose(1, 0, 2), inp.transpose(1, 0, 2), Cm.transpose(1, 0, 2))

            def step(h, x):
                d, i, c = x
                h = h * d + i
                return (h, jnp.sum(h * c, axis=-1))
            _, ys = jax.lax.scan(step, h0, xs)
            return ys.T[..., None]

        def _block(x, g, bt, Wi, bi, cw, cb, wd, bd_, wB, bB_, wC, bC_, wo, bo):
            h = _layernorm(x, g, bt)
            uv = h @ Wi.T + bi
            u, v = (uv[..., :D], uv[..., D:])
            uc = _dwconv_causal(u, cw, cb)
            delta = jax.nn.softplus(uc @ wd.T + bd_)
            Bm = uc @ wB.T + bB_
            Cm = uc @ wC.T + bC_
            y = _selective_scan(uc, delta, Bm, Cm)
            y = y * jax.nn.sigmoid(v)
            return x + (y @ wo.T + bo)
        x = embedding[tokens] + pos_enc[:S][None]
        for l in range(L):
            x = _block(x, ln_g[l], ln_b[l], Win[l], b_in[l], convw[l], convb[l], Wd[l], bd[l], WB[l], bB[l], WC[l], bC[l], Wout[l], bout[l])
        return x

    def _L0_attn_ref(x, Wq, Wk, Wv, Wg, Wo, gn_weight, gn_bias):
        import jax, jax.numpy as jnp
        import numpy as np
        D_MODEL = 192
        H = 6
        DQK = 128
        DV = 64
        SCALE_BASE = 512.0

        def _xpos(x, sign):
            B, T, Hn, d = x.shape
            half = d // 2
            pos = jnp.arange(T, dtype=jnp.float32)
            inv_freq = 1.0 / 10000.0 ** (jnp.arange(half, dtype=jnp.float32) / half)
            angles = pos[:, None] * inv_freq[None, :]
            zeta = (jnp.arange(half, dtype=jnp.float32) + half) / d
            decay = zeta[None, :] ** (sign * pos[:, None] / SCALE_BASE)
            cos_a = (jnp.cos(angles) * decay)[None, :, None, :]
            sin_a = (jnp.sin(angles) * decay)[None, :, None, :]
            x1, x2 = (x[..., :half], x[..., half:])
            return jnp.concatenate([x1 * cos_a - x2 * sin_a, x1 * sin_a + x2 * cos_a], axis=-1)

        def _decay_mask(T):
            gammas = jnp.array([1.0 - 2.0 ** (-(5 + h)) for h in range(H)], dtype=jnp.float32)
            i = jnp.arange(T, dtype=jnp.float32)
            diff = i[:, None] - i[None, :]
            causal = (diff >= 0).astype(jnp.float32)
            D = gammas[:, None, None] ** jnp.clip(diff, 0.0)[None] * causal[None]
            row = jnp.clip(jnp.sum(D, axis=-1, keepdims=True), 1e-06)
            return D / jnp.sqrt(row)
        B, T, _ = x.shape
        Q = (x @ Wq).reshape(B, T, H, DQK)
        K = (x @ Wk).reshape(B, T, H, DQK)
        V = (x @ Wv).reshape(B, T, H, DV)
        Q = _xpos(Q, 1.0)
        K = _xpos(K, -1.0)
        scores = jnp.einsum('bihd,bjhd->bhij', Q, K) * DQK ** (-0.5)
        scores = scores * _decay_mask(T)[None]
        out = jnp.einsum('bhij,bjhv->bihv', scores, V)
        concat = out.reshape(B, T, H * DV)
        g = concat.transpose(0, 2, 1).reshape(B, H, DV, T)
        mean = jnp.mean(g, axis=(2, 3), keepdims=True)
        var = jnp.var(g, axis=(2, 3), keepdims=True)
        g = (g - mean) / jnp.sqrt(var + 1e-05)
        g = g.reshape(B, H * DV, T) * gn_weight[None, :, None] + gn_bias[None, :, None]
        normed = g.transpose(0, 2, 1)
        gate = jax.nn.silu(x @ Wg)
        return normed * gate @ Wo

    def _L0_ffn_ref(x, slots, scale, fc1_weight, fc1_bias, fc2_weight, fc2_bias, norm_weight):
        import jax, jax.numpy as jnp
        import numpy as np
        EPS_NORM = 1e-05
        RMS_EPS = 1e-05

        def _l2_normalize(v):
            n = jnp.sqrt(jnp.sum(v * v, axis=-1, keepdims=True))
            return v / jnp.maximum(n, EPS_NORM)

        def _rms_norm(x, weight, eps):
            ms = jnp.mean(x * x, axis=-1, keepdims=True)
            return x * jax.lax.rsqrt(ms + eps) * weight
        xn = _rms_norm(x, norm_weight, RMS_EPS)
        tok = _l2_normalize(xn)
        sl = _l2_normalize(slots) * scale[:, None]
        logits = jnp.einsum('sd,btd->bst', sl, tok)
        dispatch_w = jax.nn.softmax(logits, axis=-1)
        combine_w = jax.nn.softmax(logits, axis=-2)
        y = jnp.einsum('btd,bst->bsd', xn, dispatch_w)
        y = jnp.einsum('sio,bsi->bso', fc1_weight, y) + fc1_bias
        y = jax.nn.gelu(y, approximate=False)
        y = jnp.einsum('sio,bsi->bso', fc2_weight, y) + fc2_bias
        out = jnp.einsum('bsd,bst->btd', y, combine_w)
        return out

    def _L1_attn_ref(x, qkv_w, qkv_b, qkv_B, proj_w, proj_b, proj_B):
        import jax, jax.numpy as jnp
        import numpy as np
        import math
        DIM = 192
        NUM_HEADS = 12

        def _xavier_uniform(key, out_f, in_f):
            a = math.sqrt(6.0 / (in_f + out_f))
            return jax.random.uniform(key, (out_f, in_f), jnp.float32, -a, a)
        B, N, C = x.shape
        hd = C // NUM_HEADS
        scale = hd ** (-0.5)
        qkv = x @ qkv_w.T + qkv_b
        qkv = qkv.reshape(B, N, 3, NUM_HEADS, hd).transpose(2, 0, 3, 1, 4)
        q, k, v = (qkv[0], qkv[1], qkv[2])
        attn = jnp.einsum('bhnd,bhmd->bhnm', q, k) * scale
        attn = jax.nn.softmax(attn, axis=-1)
        out = jnp.einsum('bhnm,bhmd->bhnd', attn, v)
        out = out.transpose(0, 2, 1, 3).reshape(B, N, C)
        return out @ proj_w.T + proj_b

    def _L1_ffn_ref(x, fc1_w, fc1_b, fc2_w, fc2_b, gate_pair, atom_in_w, atom_in_b, atom_out_w, atom_out_b, balance_bias):
        import jax, jax.numpy as jnp
        import numpy as np
        ATOM = {'vm': 0, 'im': 1, 'cm': 2, 'sc': 3, 'cc': 4}
        TASK_PAIRS = [('vm', 'sc'), ('vm', 'cc'), ('im', 'sc'), ('im', 'cc'), ('cm', 'sc'), ('cm', 'cc')]
        SRC_IDX = np.array([[ATOM[l], ATOM[r]] for l, r in TASK_PAIRS], dtype=np.int32)
        DST_IDX = np.array([[ATOM[r], ATOM[l]] for l, r in TASK_PAIRS], dtype=np.int32)
        NCLS = 6
        NATOMS = 5

        def _l2norm(x, eps=1e-12):
            return x / jnp.clip(jnp.linalg.norm(x, axis=-1, keepdims=True), eps)
        src = jnp.asarray(SRC_IDX)
        dst = jnp.asarray(DST_IDX)
        D = x.shape[-1]
        H = atom_in_w.shape[1]
        cls_tokens = x[:, :NCLS]
        patch_tokens = x[:, NCLS:]
        patch_out = jax.nn.gelu(patch_tokens @ fc1_w.T + fc1_b, approximate=False) @ fc2_w.T + fc2_b
        gate_in = _l2norm(cls_tokens.astype(jnp.float32))
        gate_w = _l2norm(gate_pair.astype(jnp.float32))
        gate_logits = jnp.einsum('bnd,nrd->bnr', gate_in, gate_w) + balance_bias[None]
        route_probs = jax.nn.softmax(gate_logits, axis=-1)
        chosen_route = jnp.argmax(route_probs, axis=-1)
        hid_all = jax.nn.gelu(jnp.einsum('bnd,ahd->bnah', cls_tokens, atom_in_w) + atom_in_b[None, None], approximate=False)
        sh_pair = hid_all[:, jnp.arange(NCLS)[:, None], src, :]
        route_out_w = atom_out_w[dst.reshape(-1)].reshape(NCLS, 2, D, H)
        route_candidates = jnp.einsum('bnrh,nrdh->bnrd', sh_pair, route_out_w) + atom_out_b[dst][None]
        chosen_w = jnp.take_along_axis(route_probs, chosen_route[..., None], axis=-1)
        chosen_cand = jnp.take_along_axis(route_candidates, chosen_route[:, :, None, None], axis=2)[:, :, 0]
        cls_out = chosen_cand * chosen_w.astype(chosen_cand.dtype)
        return jnp.concatenate([cls_out, patch_out], axis=1)
    h = _L0_tok_ref(x, L0_tok_embedding, L0_tok_pos_enc, L0_tok_ln_g, L0_tok_ln_b, L0_tok_Win, L0_tok_b_in, L0_tok_convw, L0_tok_convb, L0_tok_Wd, L0_tok_bd, L0_tok_WB, L0_tok_bB, L0_tok_WC, L0_tok_bC, L0_tok_Wout, L0_tok_bout)
    h = h + _L0_attn_ref(_layernorm(h, axis=-1), L0_attn_Wq, L0_attn_Wk, L0_attn_Wv, L0_attn_Wg, L0_attn_Wo, L0_attn_gn_weight, L0_attn_gn_bias)
    h = h + _L0_ffn_ref(_layernorm(h, axis=-1), L0_ffn_slots, L0_ffn_scale, L0_ffn_fc1_weight, L0_ffn_fc1_bias, L0_ffn_fc2_weight, L0_ffn_fc2_bias, L0_ffn_norm_weight)
    h = h + _L1_attn_ref(_layernorm(h, axis=-1), L1_attn_qkv_w, L1_attn_qkv_b, L1_attn_qkv_B, L1_attn_proj_w, L1_attn_proj_b, L1_attn_proj_B)
    h = h + _L1_ffn_ref(_layernorm(h, axis=-1), L1_ffn_fc1_w, L1_ffn_fc1_b, L1_ffn_fc2_w, L1_ffn_fc2_b, L1_ffn_gate_pair, L1_ffn_atom_in_w, L1_ffn_atom_in_b, L1_ffn_atom_out_w, L1_ffn_atom_out_b, L1_ffn_balance_bias)
    return h

_drawn_inputs = setup_inputs


def setup_inputs(seed=0):
    import zlib

    import numpy as np

    out = dict(_drawn_inputs(seed))
    spreads = {'L0_tok_ln_g': (1.0, 0.6),
     'L0_tok_ln_b': (0.0, 0.8),
     'L0_tok_b_in': (0.0, 0.1),
     'L0_tok_convb': (0.0, 0.1),
     'L0_tok_bd': (0.0, 0.8),
     'L0_tok_bB': (0.0, 0.1),
     'L0_tok_bC': (0.0, 0.1),
     'L0_tok_bout': (0.0, 0.1),
     'L0_attn_gn_weight': (1.0, 0.2),
     'L0_attn_gn_bias': (0.0, 0.1),
     'L0_ffn_scale': (1.0, 0.6),
     'L0_ffn_fc1_bias': (0.0, 0.8),
     'L0_ffn_fc2_bias': (0.0, 0.387),
     'L0_ffn_norm_weight': (1.0, 0.6),
     'L1_attn_qkv_b': (0.0, 0.1),
     'L1_attn_proj_b': (0.0, 0.1),
     'L1_ffn_fc1_b': (0.0, 0.281),
     'L1_ffn_fc2_b': (0.0, 0.1),
     'L1_ffn_balance_bias': (0.0, 0.8)}
    factors = {'L0_tok_Wd': 38.644,
     'L0_ffn_slots': 8.0,
     'L0_ffn_fc1_weight': 3.512,
     'L0_ffn_fc2_weight': 3.36,
     'L1_ffn_gate_pair': 32.238,
     'L1_ffn_atom_in_w': 6.766,
     'L1_ffn_atom_in_b': 8.0,
     'L1_ffn_atom_out_w': 6.609,
     'L1_ffn_atom_out_b': 26.803}
    for name, (base, spread) in spreads.items():
        noise = np.random.default_rng([zlib.crc32(name.encode()), seed]).standard_normal(out[name].shape)
        drawn = base * np.exp(spread * noise) if base else spread * noise
        out[name] = jnp.asarray(drawn.astype(out[name].dtype))
    for name, factor in factors.items():
        out[name] = (out[name] * factor).astype(out[name].dtype)
    return out
```

```python
from contextlib import ExitStack

import concourse.bass as bass
import numpy as np
from concourse import mybir

F32 = mybir.dt.float32
I32 = mybir.dt.int32
ALU = mybir.AluOpType
ACT = mybir.ActivationFunctionType
AX_X = mybir.AxisListType.X

P = 128
B, S, D = 16, 256, 192
V = 8000
L = 4
TAPS = 4
HD = D // 2
TILES = B * S // P
GT = 4
NG = TILES // GT
GB = 2
N = GT * P
EPS = 1e-5

NVEC = 26
V_G, V_BT, V_BU, V_BV, V_CW, V_CB, V_BD, V_BB, V_BC = 0, 2, 4, 6, 8, 16, 18, 20, 22
V_NBD = 24

H0, DQK, DV = 6, 128, 64
HV = H0 * DV
NCH = HV // P
MW = S + P

SLOTS, FF = 64, 768
FC = FF // P
RING = 4

H1, HD1 = 12, 16
HG = 3
QG = H1 // HG
HR = 32
UN = GB * QG
QT = HG * HR

NCLS, NATOMS = 6, 5
CT_N = NCLS * B


def build(nc, A, out, slot_out):
    ctx = ExitStack()
    with ctx:
        def sb(name, shape, dt=F32):
            return ctx.enter_context(nc.sbuf_tensor(name, shape, dt))

        def sem(name):
            return ctx.enter_context(nc.semaphore(name))

        banks = ctx.enter_context(nc.psum_tensor("banks", [P, 8, 512], F32))
        X = sb("X", [P, TILES, D])
        tok_i = sb("tok_i", [P, TILES], I32)
        tok_neg = sb("tok_neg", [P, TILES], I32)
        tok_fix = sb("tok_fix", [P, TILES], I32)
        pos = sb("pos", [P, 2, D])
        ident = sb("ident", [P, P])
        own_rows = sb("rows_of_each_head", [QT, HG])
        mhalf = sb("mhalf", [P, 8])
        st = sb("st", [P, GT, 6])
        mv = sb("mv", [P, GT, 2])
        vare = sb("vare", [P, GT])
        rstd = sb("rstd", [P, GT])
        wait_slot = sb("wait_slot", [P, 1])
        xn = sb("xn", [P, GT, D])
        hT = sb("hT", [HD, 2, N])

        w_arena = sb("w_arena", [P, 12960])
        arena = sb("arena", [P, 16384])

        def carve(area, start):
            at = [start]

            def take(parts, *shape):
                n = int(np.prod(shape))
                v = area[0:parts, at[0]:at[0] + n]
                at[0] += n
                assert at[0] <= area.shape[1], (at[0], area.shape)
                names = "abcd"[:len(shape)]
                if len(shape) == 1:
                    return v
                return v.rearrange("p (" + " ".join(names) + ") -> p " + " ".join(names),
                                   **{n_: s_ for n_, s_ in zip(names[1:], shape[1:])})
            return take

        tw = carve(w_arena, 0)
        win = tw(HD, 2, 2 * D)
        wzbc = tw(HD, 2, 3 * D)
        wout = tw(HD, 2, D)
        vec = tw(HD, L, NVEC)
        boutb = tw(P, L, D)
        ta = carve(arena, 0)
        upad = [ta(HD, 2, GB, S + TAPS - 1) for _ in range(2)]
        uc = ta(HD, 2, N)
        sv = [ta(HD, 2, N) for _ in range(2)]
        dec = ta(HD, 2, N)
        Bs = ta(HD, 2, N)
        Cs = ta(HD, 2, N)
        inp = ta(HD, 2, N)
        hs = ta(HD, 2, N)
        hc = ta(HD, 2, N)
        hsum = ta(HD, N)
        ysum = ta(P, GT)

        rw = carve(w_arena, 3200)
        wq = rw(HD, 2, H0 * DQK)
        wk = rw(HD, 2, H0 * DQK)
        wv = rw(HD, 2, HV)
        wg = rw(HD, 2, HV)
        wo = rw(P, NCH, D)
        rot_cos = [rw(P, S) for _ in range(2)]
        rot_sin = [rw(P, S) for _ in range(2)]
        mask = rw(P, H0, MW)
        blk = rw(P, P)
        gnw = rw(P, NCH)
        gnb = rw(P, NCH)
        ra = carve(arena, 0)
        qk = [[ra(P, N) for _ in range(2)] for _ in range(2)]
        swp = [ra(P, N) for _ in range(2)]
        vt = ra(P, GT, HV)
        gate = ra(P, NCH, N)
        pm = [ra(P, GB, MW) for _ in range(2)]
        oT = ra(P, NCH, N)
        ng = ra(P, NCH, N)
        gst = ra(P, 2 * NCH, 6)
        gmv = ra(P, 2 * NCH, 2)
        gs = ra(P, 2 * NCH, 2)
        gmsq = ra(P, 2 * NCH)
        gvar = ra(P, 2 * NCH)
        grs = ra(P, 2 * NCH)
        gsc = ra(P, 2 * NCH)
        gmb = ra(P, 2 * NCH)
        gbi = ra(P, 2 * NCH)

        cw = carve(w_arena, 11856)
        slots = cw(SLOTS, D)
        slot_scale = cw(SLOTS, 1)
        normw = cw(P, D)
        b1 = cw(P, SLOTS, FC)
        b2 = cw(SLOTS, D)
        slT = sb("slT", [HD, 2, SLOTS])
        sln2 = sb("sln2", [SLOTS, 2])
        slT_junk = sb("slots_squared", [SLOTS, D])
        ring1 = [sb(f"ring1_{r}", [HD, 2, FF]) for r in range(RING)]
        ring2 = [sb(f"ring2_{r}", [P, FC, D]) for r in range(RING)]
        ca = carve(arena, 0)
        CT = ca(SLOTS, B * S)
        YT = ca(HD, 2, SLOTS, B)
        xw = [ca(P, GT, D) for _ in range(2)]
        tokn = ca(P, GT, D)
        sq = ca(P, GT, D)
        n2 = ca(P, GT)
        n2c = ca(P, GT)
        rn = ca(P, GT)
        mx = ca(SLOTS, GB)
        nmx = ca(SLOTS, GB)
        E_ = ca(SLOTS, N)
        den = ca(SLOTS, GB)
        rden = ca(SLOTS, GB)
        cmx = ca(P, GT)
        Cl = ca(P, GT, SLOTS)
        csum = ca(P, GT)
        crec = ca(P, GT)
        eT = ca(P, GT, SLOTS)
        yv = ca(SLOTS, GB, D)
        ca = carve(arena, B * S + 2 * SLOTS * B)
        y2all = ca(SLOTS, B, D)
        ys = [ca(HD, 2, B) for _ in range(2)]
        hraw = [ca(B, FF) for _ in range(2)]
        fo = ca(B, RING, D)
        hb = [ca(P, FC * B) for _ in range(2)]
        gl = [ca(P, FC * B) for _ in range(2)]
        CTs = ca(SLOTS, N)
        y2 = ca(SLOTS, GB, D)

        aw = carve(w_arena, 0)
        wqk = aw(HD, 2, 2 * QG * QT)
        wv1 = aw(HD, 2, D)
        wp1 = aw(HD, 2, D)
        qkb = aw(QT, 2 * QG)
        vb1 = aw(P, D)
        pb1 = aw(P, D)
        assert 2 * 2 * QG * QT + 4 * D + 2 * QG + 2 * D <= 3200
        da = carve(arena, 0)
        qkT = [[da(QT, N) for _ in range(2 * QG)] for _ in range(2)]
        va = [da(P, GT, H1, HD1 + 1) for _ in range(2)]
        pT = [da(P, HG, 2, S) for _ in range(2)]
        mt = da(P, 2, QT)
        smx = da(P, HG, 2)
        qa = da(QT, S)
        kd = [da(QT, HG, S) for _ in range(2)]
        ssum = da(P, 2, H1)
        ao = da(P, 2, D)
        aoT = da(HD, 2, S)

        fw = carve(w_arena, 3200)
        w1f = fw(HD, 2, FF)
        w2f = fw(P, FC, D)
        b1f = fw(P, FC)
        b2f = fw(P, D)
        atom_in = [ring1[a][:, :, :] for a in range(RING)] + [fw(HD, 2, FF)]
        atom_out = [ring2[a][:, :, :] for a in range(RING)] + [fw(P, FC, D)]
        atom_b1 = fw(P, NATOMS, FC)
        atom_b2 = fw(HD, NATOMS, 2)
        gates = fw(CT_N, 2, D)
        balance = fw(CT_N, 2)
        ea = carve(arena, 0)
        hid = [ea(P, FC, N) for _ in range(2)]
        cls_x = ea(CT_N, D)
        cls_n = ea(CT_N, D)
        cls_T = ea(HD, 2, CT_N)
        cls_h = [ea(P, FC, CT_N) for _ in range(2)]
        cand = [ea(HD, 2, CT_N) for _ in range(2)]
        gprod = ea(CT_N, 2, D)
        csq = ea(CT_N, 3, D)
        cst = ea(CT_N, 6)
        cmv = ea(CT_N, 2)
        cpw = ea(CT_N, 4)
        crs = ea(CT_N, 4)
        dots = ea(CT_N, 2)
        lg1 = ea(CT_N, 2)
        lmax = ea(CT_N, 1)
        prob = ea(CT_N, 2)
        psum_ = ea(CT_N, 2)
        pick = ea(CT_N, 2)
        fin = [ea(CT_N, D) for _ in range(2)]

        s_idx = sem("idx_loaded")
        s_pos = sem("pos_loaded")
        s_const = sem("constants_ready")
        s_fix = sem("token_ids_clamped")
        s_gath = [sem(f"rows_gathered_{g}") for g in range(NG)]
        s_emb = sem("embedding_ready")
        s_win = sem("win_loaded")
        s_wzbc = sem("wzbc_loaded")
        s_wout = sem("wout_loaded")
        s_vec = sem("vec_loaded")
        s_nbd = sem("negated_bd_ready")
        s_pads = sem("conv_pads_zero")
        s_stat = sem("ln_stat_step")
        s_var = sem("ln_var_ready")
        s_rstd = sem("ln_rstd_ready")
        s_xn = sem("ln_xn_ready")
        s_tr = sem("transposed_in_psum")
        s_hT = sem("hT_evacuated")
        s_uvp = sem("uv_in_psum")
        s_uve = sem("uv_evacuated")
        s_zp = sem("zbc_in_psum")
        s_ze = sem("zbc_evacuated")
        s_reset = sem("decay_reset")
        s_inp = sem("scan_input_ready")
        s_scan = sem("scan_done")
        s_hc = sem("hc_ready")
        s_conv = sem("conv_step")
        s_wop = sem("wo_in_psum")
        s_hsum = sem("hc_halves_added")
        s_yp = sem("y_products_transposed")
        s_ysum = sem("y_ready")
        s_bout = sem("bout_added")
        s_res = sem("residual_updated")
        s_rw = sem("retention_weights_loaded")
        s_qkp = sem("qk_in_psum")
        s_rot = sem("rotary_products_ready")
        s_radd = sem("rotary_sum_ready")
        s_vgp = sem("vg_in_psum")
        s_vge = sem("vg_evacuated")
        s_sp = sem("scores_in_psum")
        s_pm = sem("masked_scores_ready")
        s_pv = sem("pv_in_psum")
        s_oT = sem("oT_evacuated")
        s_gn = sem("groupnorm_step")
        s_gstat = sem("groupnorm_stats_in_psum")
        s_grs = sem("groupnorm_rstd_ready")
        s_ng = sem("gated_norm_ready")
        s_rop = sem("retention_out_in_psum")
        s_rres = sem("retention_residual_updated")
        s_cw = sem("mixture_weights_loaded")
        s_sl = sem("slots_step")
        s_slq = sem("slots_square_sum")
        s_slr = sem("slots_rnorm")
        s_slp = sem("slots_transposed")
        s_slT = sem("slots_evacuated")
        s_xw = sem("weighted_norm_ready")
        s_n2 = sem("token_square_sums")
        s_n2c = sem("token_square_sums_bounded")
        s_rn = sem("token_rnorm_ready")
        s_tokn = sem("unit_tokens_ready")
        s_lt = sem("logits_in_psum")
        s_mx = sem("dispatch_max_ready")
        s_nmx = sem("dispatch_max_negated")
        s_E = sem("dispatch_exp_ready")
        s_cmx = sem("combine_max_ready")
        s_sub = sem("combine_shifted")
        s_cexp = sem("combine_exp_ready")
        s_csum = sem("combine_sum_ready")
        s_cn = sem("combine_ready")
        s_tre = sem("dispatch_transposed")
        s_trc = sem("combine_transposed")
        s_eT = sem("dispatch_evacuated")
        s_CT = sem("combine_evacuated")
        s_y = sem("slot_inputs_in_psum")
        s_rden = sem("dispatch_reciprocal_ready")
        s_yv = sem("slot_inputs_ready")
        s_trY = sem("slot_inputs_transposed")
        s_YT = sem("slot_inputs_evacuated")
        s_w1 = [sem(f"fc1_loaded_{r}") for r in range(RING)]
        s_w2 = [sem(f"fc2_loaded_{r}") for r in range(RING)]
        s_fc1 = sem("fc1_in_psum")
        s_ys = sem("slot_input_copied")
        s_hr = sem("fc1_evacuated")
        s_ht = sem("fc1_transposed")
        s_y2d = sem("slot_outputs_moved")
        s_y2a = sem("slot_outputs_back")
        s_hb = sem("fc1_biased")
        s_gl = sem("gelu_ready")
        s_fc2 = sem("fc2_in_psum")
        s_y2c = sem("fc2_evacuated")
        s_cp = sem("combine_operands_copied")
        s_y2 = sem("slot_outputs_ready")
        s_co = sem("mixture_out_in_psum")
        s_cres = sem("mixture_residual_updated")
        s_aw = sem("attention_weights_loaded")
        s_qb = sem("query_bias_scaled")
        s_da = sem("attention_buffers_set")
        s_jp = sem("shared_bank_filled")
        s_je = sem("shared_bank_emptied")
        s_kd = sem("keys_set_apart")
        s_p1 = sem("scores_for_max_in_psum")
        s_smx = sem("score_max_ready")
        s_neg = sem("score_max_negated")
        s_p2 = sem("shifted_scores_in_psum")
        s_ex = sem("probabilities_ready")
        s_av = sem("attention_values_in_psum")
        s_sr = sem("probability_sum_inverted")
        s_ao = sem("attention_out_ready")
        s_pb = sem("projection_bias_added")
        s_fw = sem("ffn_weights_loaded")
        s_atom = sem("atom_weights_loaded")
        s_clsg = sem("class_rows_gathered")
        s_cls = sem("class_step")
        s_csq = sem("class_square_sums")
        s_crs = sem("class_powers_ready")
        s_cexp2 = sem("route_exp_ready")
        s_clT = sem("class_transposed")
        s_clTe = sem("class_transposed_evacuated")
        s_ain = sem("atom_hidden_in_psum")
        s_ag = sem("atom_gelu_ready")
        s_aout = sem("atom_out_in_psum")
        s_cand = sem("candidate_ready")
        s_candT = sem("candidates_transposed")
        s_fin = sem("class_rows_ready")
        s_f1 = sem("ffn_hidden_in_psum")
        s_gf = sem("ffn_gelu_ready")
        s_f2 = sem("ffn_out_in_psum")
        s_b2f = sem("ffn_bias_added")
        s_eres = sem("ffn_residual_updated")
        s_out = sem("output_written")

        def wait(eng, s_, v):
            if not isinstance(v, int) or v > 0:
                eng.wait_ge(s_, v)

        def ln_stats(dve, q, t0, mul=1.0, add=EPS):
            for i in range(GT):
                dve.bn_stats(st[:, i, :], X[:, t0 + i, :]).then_inc(s_stat, 1)
            dve.wait_ge(s_stat, q * (2 * GT) + GT)
            dve.memset(wait_slot[:, :], 0.0)
            for i in range(GT):
                dve.bn_aggr(mv[:, i, :], st[:, i, :]).then_inc(s_stat, 1)
            dve.wait_ge(s_stat, q * (2 * GT) + 2 * GT)
            dve.tensor_scalar(vare[:, :], mv[:, :, 1], mul, add, ALU.mult, ALU.add).then_inc(s_var, 1)

        def ln_rstd(pool, q):
            pool.wait_ge(s_var, q + 1)
            pool.tensor_tensor(rstd[:, :], vare[:, :], mhalf[:, 0:GT], ALU.pow).then_inc(s_rstd, 1)

        def ln_apply(dve, q, t0, free=None):
            dve.wait_ge(s_rstd, q + 1)
            dve.wait_ge(*(free or (s_tr, q * 2)))
            for i in range(GT):
                dve.tensor_scalar(xn[:, i, :], X[:, t0 + i, :], mv[:, i, 0:1], rstd[:, i:i + 1],
                                  ALU.subtract, ALU.mult).then_inc(s_xn, 1)

        def transpose_group(pe, q, tq=None):
            pe.wait_ge(s_xn, (q + 1) * GT)
            pe.wait_ge(s_hT, (q if tq is None else tq) * 2)
            for k in range(2):
                for i in range(GT):
                    ins = pe.transpose(banks[0:HD, k, i * P:(i + 1) * P], xn[:, i, k * HD:(k + 1) * HD], ident[:, :])
                ins.then_inc(s_tr, 1)

        def flip(pe, o, x, idn, first):
            if first:
                return pe.matmul(o, x, idn, start=True, stop=True)
            return pe.transpose(o, x, idn)

        block = ctx.enter_context(nc.Block())

        NT = L * NG

        def run_tok(eng, body):
            for j in range(-2, NG - 2):
                body(j, j % 2, {d for d in range(-2, 3) if 0 <= j - d < NT})
            with eng.Fori((NG - 2) // 2, (NT - 2) // 2) as i:
                for h in range(2):
                    body(2 * i + h, h, set(range(-2, 3)))
            for j in range(NT - 2, NT + 2):
                body(j, j % 2, {d for d in range(-2, 3) if 0 <= j - d < NT})

        RET_W = 13 * 16
        GN_VAR = 12 + 2 + 3
        GN_STEPS = GN_VAR + 3 + 6
        TOK_DONE = NT * GT

        def run_groups(eng, body):
            body(0, True, False)
            with eng.Fori(1, NG - 1) as g:
                body(g, True, True)
            body(NG - 1, True, True)
            body(NG, False, True)

        CW = 5 * 16
        Q_MIX = NT + NG
        AW = 6 * 16
        Q_ATT = Q_MIX + NG
        JOBS_FIRST = 2 + 2 * QG + GT + 2
        JOBS = 2 * UN + UN + 2

        CLS_VAR, CLS_NORMS = 3, 7
        FW = 10 * 16
        ATOMS_W = 8 * 16
        Q_FFN = Q_ATT + NG
        ATOM_ROLE = [(0, slice(2 * a, 2 * a + 2)) for a in range(3)] + [(1, slice(a, NCLS, 2)) for a in range(2)]

        def classes(x, which):
            return x.rearrange("p (n b) -> p n b", n=NCLS)[:, which, :]

        def group_jobs(first, more, more2):
            jobs = {}
            for u in range(UN):
                if more:
                    jobs[u, 0] = ("qk", u)
                extra = {0: ("v", 0), 1: ("v", 1), 2: ("aoT", 1), 3: ("proj", 1),
                         4: ("v", 2), 5: ("v", 3), 6: ("aoT", 0), 7: ("proj", 0)}[u]
                if not (extra[0] == "v" and not more) and not (u in (2, 3) and first):
                    jobs[u, 1] = extra
                jobs[u, 2] = ("max", u)
            if more2:
                jobs[UN - 1, 3] = ("hT", 0)
                jobs[UN, 3] = ("hT", 1)
            return {k: (*v, n) for n, (k, v) in enumerate(jobs.items())}

        def run_attention(eng, body):
            def base(g):
                return JOBS_FIRST + JOBS * g - 2
            body(0, 0, JOBS_FIRST, group_jobs(True, True, True))
            with eng.Fori(0, (NG - 4) // 2) as k:
                body(2 * k + 1, 1, base(2 * k + 1), group_jobs(False, True, True))
                body(2 * k + 2, 0, base(2 * k + 2), group_jobs(False, True, True))
            body(NG - 3, 1, base(NG - 3), group_jobs(False, True, True))
            body(NG - 2, 0, base(NG - 2), group_jobs(False, True, False))
            body(NG - 1, 1, base(NG - 1) - 2, group_jobs(False, False, False))

        JOBS_TAIL = JOBS_FIRST + JOBS * (NG - 1) - 4 + UN + 4

        def run_mix(body):
            def run(eng):
                body(0, 0, True, False)
                with eng.Fori(0, (NG - 2) // 2) as k:
                    body(2 * k + 1, 1, True, True)
                    body(2 * k + 2, 0, True, True)
                body(NG - 1, 1, True, True)
                body(NG, 0, False, True)
            return run

        def run_slots(eng, body):
            for r in range(RING):
                body(r, r, 0)
            with eng.Fori(1, SLOTS // RING) as k:
                for r in range(RING):
                    body(RING * k + r, r, k)

        def run_combine(eng, body):
            body(0, True, False)
            with eng.Fori(1, NG) as g:
                body(g, True, True)
            body(NG, False, True)

        @block.sync
        def _(sp):
            sp.dma_start(tok_i[:, :], A["tok_idx"]).then_inc(s_idx, 16)
            sp.dma_start(vec[:, :, 0:V_NBD], A["vec"]).then_inc(s_vec, 16)
            sp.dma_start(win, A["win"][0]).then_inc(s_win, 16)
            sp.dma_start(pos[:, :, :], A["pos"]).then_inc(s_pos, 16)
            sp.dma_start(boutb, A["bout"].rearrange("(o l) d -> o l d", o=1).broadcast_to((P, L, D))).then_inc(s_vec, 16)
            sp.dma_start(wzbc, A["wzbc"][0]).then_inc(s_wzbc, 16)
            sp.dma_start(wout, A["wout"][0]).then_inc(s_wout, 16)
            for dst, name in ((wq, "rq"), (wk, "rk"), (wv, "rv"), (wg, "rg"), (wo, "ro"), (rot_cos[0], "cos_q"),
                              (rot_sin[0], "sin_q"), (rot_cos[1], "cos_k"), (rot_sin[1], "sin_k"), (mask, "mask"),
                              (blk, "blk"), (gnw, "gnw"), (gnb, "gnb")):
                sp.dma_start(dst, A[name]).then_inc(s_rw, 16)
            for dst, name in ((slots, "slots"), (slot_scale, "slot_scale"), (b1, "b1"), (b2, "b2")):
                sp.dma_start(dst, A[name]).then_inc(s_cw, 16)
            sp.dma_start(normw, A["normw"].rearrange("(o d) -> o d", o=1).broadcast_to((P, D))).then_inc(s_cw, 16)
            for r in range(RING):
                sp.dma_start(ring1[r][:, :, :], A["fc1"][r]).then_inc(s_w1[r], 16)
                sp.dma_start(ring2[r][:, :, :], A["fc2"][r]).then_inc(s_w2[r], 16)
            for l in range(1, L):
                sp.wait_ge(s_uvp, l * NG * 4)
                sp.dma_start(win, A["win"][l]).then_inc(s_win, 16)
                sp.wait_ge(s_zp, l * NG * 6)
                sp.dma_start(wzbc, A["wzbc"][l]).then_inc(s_wzbc, 16)
                sp.wait_ge(s_wop, l * NG)
                sp.dma_start(wout, A["wout"][l]).then_inc(s_wout, 16)
            for dst, name in ((wqk, "wqk"), (wv1, "wv1"), (wp1, "wp1"), (qkb, "qkb")):
                sp.wait_ge(s_res, TOK_DONE)
                sp.dma_start(dst, A[name]).then_inc(s_aw, 16)
            for dst, name in ((vb1, "vb1"), (pb1, "pb1")):
                sp.dma_start(dst, A[name].rearrange("(o d) -> o d", o=1).broadcast_to((P, D))).then_inc(s_aw, 16)
            sp.wait_ge(s_rres, 2 * NG)
            for dst, name in ((w1f, "w1f"), (w2f, "w2f"), (b1f, "b1f"), (atom_b1, "atom_b1"), (atom_b2, "atom_b2"),
                              (gates, "gates"), (balance, "balance")):
                sp.dma_start(dst, A[name]).then_inc(s_fw, 16)
            sp.dma_start(b2f, A["b2f"].rearrange("(o d) -> o d", o=1).broadcast_to((P, D))).then_inc(s_fw, 16)
            sp.dma_start(atom_in[RING], A["atom_in"][RING]).then_inc(s_fw, 16)
            sp.dma_start(atom_out[RING], A["atom_out"][RING]).then_inc(s_fw, 16)
            with sp.Fori(1, SLOTS // RING) as k:
                for r in range(RING):
                    n = RING * k + r
                    sp.wait_ge(s_fc1, n - RING + 1)
                    sp.dma_start(ring1[r][:, :, :], A["fc1"][bass.ds(n, 1)].rearrange("o p k f -> p (o k) f")
                                 ).then_inc(s_w1[r], 16)
                    sp.wait_ge(s_fc2, n - RING + 1)
                    sp.dma_start(ring2[r][:, :, :], A["fc2"][bass.ds(n, 1)].rearrange("o p c d -> p (o c) d")
                                 ).then_inc(s_w2[r], 16)
            sp.wait_ge(s_y2d, SLOTS // RING * 16)
            sp.dma_start(y2all, slot_out).then_inc(s_y2a, 16)
            for a in range(RING):
                sp.wait_ge(s_fc2, SLOTS)
                sp.dma_start(atom_in[a], A["atom_in"][a]).then_inc(s_atom, 16)
                sp.dma_start(atom_out[a], A["atom_out"][a]).then_inc(s_atom, 16)
            sp.wait_ge(s_je, JOBS_TAIL + 2)
            for n in range(NCLS):
                sp.dma_start(cls_x[n * B:(n + 1) * B, :], X[n:n + 1, ::2, :]).then_inc(s_clsg, 16)
            rows_out = out.rearrange("(t p) d -> p t d", p=P)
            with sp.Fori(0, NG) as g:
                sp.wait_ge(s_eres, 2 * g + 2)
                for t in range(GT):
                    lo = NCLS if t % 2 == 0 else 0
                    sp.dma_start(rows_out[lo:, bass.ds(g * GT + t, 1), :],
                                 X[lo:, bass.ds(g * GT + t, 1), :]).then_inc(s_out, 16)
            sp.wait_ge(s_fin, 2)
            for n in range(NCLS):
                sp.dma_start(out.rearrange("(b t) d -> t b d", b=B)[n], fin[1][n * B:(n + 1) * B, :]).then_inc(s_out, 16)
            sp.wait_ge(s_out, 16 * (TILES + NCLS))

        @block.gpsimd
        def _(pool):
            pool.memset(ident[:, :], 0.0).then_inc(s_const, 1)
            pool.memset(mhalf[:, :], -0.5).then_inc(s_const, 1)
            pool.memset(own_rows[:, :], 0.0).then_inc(s_const, 1)
            for h in range(HG):
                pool.wait_ge(s_const, 3 + h)
                pool.memset(own_rows[h * HR:(h + 1) * HR, h:h + 1], 1.0).then_inc(s_const, 1)
            pool.wait_ge(s_const, 3 + HG)
            pool.affine_select(out=ident[:, :], in_=ident[:, :], compare_op=ALU.not_equal, fill=1.0, base=0,
                               pattern=[[-1, P]], channel_multiplier=1).then_inc(s_const, 1)
            pool.wait_ge(s_fix, 4)
            def gather(g):
                for t in range(g * GT, (g + 1) * GT):
                    pool.indirect_dma_start(X[:, t, :], None, A["emb"],
                                            bass.IndirectOffsetOnAxis(ap=tok_fix[:, t:t + 1], axis=0)
                                            ).then_inc(s_gath[g], 16)
            gather(0)
            gather(1)
            pool.wait_ge(s_sl, 1)
            pool.tensor_tensor(sln2[:, 1:2], sln2[:, 0:1], mhalf[0:SLOTS, 0:1], ALU.pow).then_inc(s_slr, 1)

            def step(j, par, on):
                if 2 in on:
                    pool.wait_ge(s_hc, j - 1)
                    wait(pool, s_yp, j - 2)
                    pool.tensor_tensor(hsum, hc[:, 0, :], hc[:, 1, :], ALU.add).then_inc(s_hsum, 1)
                if isinstance(j, int) and j + 4 < NG:
                    gather(j + 4)
                if -2 in on:
                    ln_rstd(pool, j + 2)
                    q = j + 2
                    pool.wait_ge(s_xn, (q + 1) * GT)
                    if isinstance(q, int) and q == 0:
                        pool.wait_ge(s_vec, 32)
                    xg = X[:, bass.ds(q % NG * GT, GT), :]
                    bb = boutb[:, bass.ds(q // NG, 1), :].broadcast_to((P, GT, D))
                    pool.tensor_tensor(xg, xg, bb, ALU.add).then_inc(s_bout, 1)
            run_tok(pool, step)

            def ret(g, cur, prev):
                if cur:
                    for h in range(H0):
                        for w in range(2):
                            n = 12 * g + 2 * h + w
                            pool.wait_ge(s_rot, 3 * n + 3)
                            pool.tensor_tensor(qk[w][h % 2], qk[w][h % 2], swp[w], ALU.add).then_inc(s_radd, 1)
                        if h == 1 and prev:
                            pool.wait_ge(s_gn, GN_STEPS * (g - 1) + GN_VAR)
                            pool.tensor_tensor(grs, gvar, mhalf[:, 0:2 * NCH], ALU.pow).then_inc(s_grs, 1)
                        if h == 4 and not (isinstance(g, int) and g == NG - 1):
                            ln_rstd(pool, NT + g + 1)
                else:
                    pool.wait_ge(s_gn, GN_STEPS * (g - 1) + GN_VAR)
                    pool.tensor_tensor(grs, gvar, mhalf[:, 0:2 * NCH], ALU.pow).then_inc(s_grs, 1)
            ln_rstd(pool, NT)
            run_groups(pool, ret)

            def mix(i, par, cur, prev):
                if cur:
                    ln_rstd(pool, Q_MIX + i)
                    pool.wait_ge(s_n2c, i + 1)
                    pool.tensor_tensor(rn, n2c, mhalf[:, 0:GT], ALU.pow).then_inc(s_rn, 1)
            run_mix(mix)(pool)

            def add_bias(g, q0, bias, done):
                pool.wait_ge(s_xn, GT * (q0 + g + 1))
                xg = X[:, bass.ds(g * GT, GT), :]
                pool.tensor_tensor(xg, xg, bias.rearrange("p (o d) -> p o d", o=1).broadcast_to((P, GT, D)),
                                   ALU.add).then_inc(done, 1)

            def att(g, par, base, jobs):
                for u in range(UN):
                    U = UN * g + u
                    pool.wait_ge(s_je, base)
                    wait(pool, s_p2, U - 1)
                    k = qkT[par][QG + u % QG][:, (u // QG) * S:(u // QG + 1) * S]
                    pool.tensor_tensor(kd[u % 2], k.rearrange("p (o s) -> p o s", o=1).broadcast_to((QT, HG, S)),
                                       own_rows[:, :].rearrange("p (h o) -> p h o", o=1).broadcast_to((QT, HG, S)),
                                       ALU.mult).then_inc(s_kd, 1)
                    if u == 3 and (UN - 1, 3) in jobs:
                        ln_rstd(pool, Q_ATT + g + 2)
                    if u == 4 and (UN - 1, 3) in jobs:
                        add_bias(g + 2, Q_ATT, pb1, s_pb)
            pool.wait_ge(s_cres, 2 * NG)
            pool.wait_ge(s_aw, AW)
            for g in range(2):
                ln_rstd(pool, Q_ATT + g)
                add_bias(g, Q_ATT, pb1, s_pb)
            run_attention(pool, att)

            pool.wait_ge(s_fw, FW)
            pool.wait_ge(s_clsg, 16 * NCLS)
            for g in range(2):
                ln_rstd(pool, Q_FFN + g)
                add_bias(g, Q_FFN, b2f, s_b2f)
            for n, sl in enumerate((slice(0, 1), slice(1, 4))):
                pool.wait_ge(s_cls, (CLS_VAR, CLS_NORMS)[n])
                pool.tensor_tensor(crs[:, sl], cpw[:, sl], mhalf[0:CT_N, sl], ALU.pow).then_inc(s_crs, 1)
            with pool.Fori(2, NG) as g:
                ln_rstd(pool, Q_FFN + g)
                add_bias(g, Q_FFN, b2f, s_b2f)

        @block.vector
        def _(dve):
            dve.wait_ge(s_idx, 16)
            dve.tensor_scalar(tok_neg[:, :], tok_i[:, :], 0.0, float(V), ALU.is_lt, ALU.mult).then_inc(s_fix, 1)
            dve.wait_ge(s_fix, 1)
            dve.tensor_tensor(tok_fix[:, :], tok_neg[:, :], tok_i[:, :], ALU.add).then_inc(s_fix, 1)
            dve.wait_ge(s_fix, 2)
            dve.tensor_scalar(tok_neg[:, :], tok_fix[:, :], float(V - 1), 0.0, ALU.min, ALU.max).then_inc(s_fix, 1)
            dve.wait_ge(s_fix, 3)
            dve.tensor_copy(tok_fix[:, :], tok_neg[:, :]).then_inc(s_fix, 1)
            for u in upad:
                dve.memset(u[:, :, :, 0:TAPS - 1], 0.0).then_inc(s_pads, 1)
            dve.wait_ge(s_vec, 32)
            dve.tensor_scalar(vec[:, :, V_NBD:V_NBD + 2], vec[:, :, V_BD:V_BD + 2], -1.0, None,
                              ALU.mult).then_inc(s_nbd, 1)
            dve.wait_ge(s_cw, CW)
            dve.wait_ge(s_slq, 1)
            dve.tensor_scalar(sln2[:, 0:1], sln2[:, 0:1], 1e-10, None, ALU.max).then_inc(s_sl, 1)
            dve.wait_ge(s_slr, 1)
            dve.tensor_scalar(slots, slots, sln2[:, 1:2], slot_scale, ALU.mult, ALU.mult).then_inc(s_sl, 1)
            dve.wait_ge(s_pos, 16)

            def scan_part(j):
                dve.wait_ge(s_ze, 6 * j + 2)
                d4 = dec.rearrange("p k (b t) -> p (k b) t", b=GB)
                dve.memset(d4[:, :, 0:1], 0.0).then_inc(s_reset, 1)
                dve.wait_ge(s_ze, 6 * j + 4)
                dve.tensor_tensor(inp, Bs, uc, ALU.mult).then_inc(s_inp, 1)
                dve.wait_ge(s_reset, j + 1)
                dve.wait_ge(s_inp, j + 1)
                dve.tensor_tensor_scan(hs.rearrange("p k n -> p (k n)"), dec.rearrange("p k n -> p (k n)"),
                                       inp.rearrange("p k n -> p (k n)"), 0.0, ALU.mult, ALU.add).then_inc(s_scan, 1)
                dve.wait_ge(s_scan, j + 1)
                dve.wait_ge(s_ze, 6 * j + 6)
                dve.wait_ge(s_hsum, j)
                dve.tensor_tensor(hc, hs, Cs, ALU.mult).then_inc(s_hc, 1)

            def conv_part(j, par):
                lay = j // NG

                def col(c):
                    return vec[:, bass.ds(lay, 1), c:c + 1].rearrange("p a b -> p (a b)")
                dve.wait_ge(s_uve, 4 * j + 2)
                dve.wait_ge(s_zp, 6 * j)
                ucv = [uc[:, k, :].rearrange("p (b t) -> p b t", b=GB) for k in range(2)]
                u = upad[par]
                for k in range(2):
                    dve.tensor_scalar(ucv[k], u[:, k, :, 3:3 + S], col(V_CW + 2 * 3 + k), col(V_CB + k),
                                      ALU.mult, ALU.add).then_inc(s_conv, 1)
                for n, tap in enumerate((2, 1, 0)):
                    for k in range(2):
                        dve.wait_ge(s_conv, 8 * j + 2 * n + k + 1)
                        dve.scalar_tensor_tensor(ucv[k], u[:, k, :, tap:tap + S], col(V_CW + 2 * tap + k), ucv[k],
                                                 ALU.mult, ALU.add).then_inc(s_conv, 1)

            def residual_part(j):
                dve.wait_ge(s_yp, j + 1)
                dve.reduce_sum(ysum, banks[:, 0, 0:GT * HD].rearrange("p (t d) -> p t d", t=GT), AX_X).then_inc(s_ysum, 1)
                dve.wait_ge(s_ysum, j + 1)
                dve.wait_ge(s_wop, j + 1)
                dve.wait_ge(s_bout, j + 1)
                for i in range(GT):
                    xt = X[:, bass.ds(j % NG * GT + i, 1), :].rearrange("p a d -> p (a d)")
                    dve.scalar_tensor_tensor(xt, banks[:, 2 + i // 2, (i % 2) * D:(i % 2 + 1) * D],
                                             ysum[:, i:i + 1], xt,
                                             ALU.mult, ALU.add).then_inc(s_res, 1)

            def step(j, par, on):
                if 2 in on:
                    scan_part(j - 2)
                if 1 in on:
                    conv_part(j - 1, 1 - par)
                if 2 in on:
                    residual_part(j - 2)
                if -2 in on:
                    q = j + 2
                    if isinstance(q, int) and q < NG:
                        dve.wait_ge(s_gath[q], 16 * GT)
                        for b in range(GB):
                            xb = X[:, q * GT + 2 * b:q * GT + 2 * b + 2, :]
                            dve.tensor_tensor(xb, xb, pos[:, :, :], ALU.add).then_inc(s_emb, 1)
                        dve.wait_ge(s_emb, (q + 1) * GB)
                    else:
                        dve.wait_ge(s_res, (q - NG + 1) * GT)
                    ln_stats(dve, q, q % NG * GT)
                    ln_apply(dve, q, q % NG * GT)
            run_tok(dve, step)

            def rotary(g, h, w):
                n = 12 * g + 2 * h + w
                head = H0 * g + h
                dst = qk[w][h % 2]
                ps = banks[:, 2 + w, :]
                dve.wait_ge(s_qkp, n + 1)
                if not isinstance(g, int) or head >= 2:
                    dve.wait_ge(s_sp, 2 * (head - 1))
                if not isinstance(g, int) or n >= 2:
                    dve.wait_ge(s_radd, n - 1)

                def v(x):
                    return x.rearrange("p (b t) -> p b t", b=GB)

                def tab(x):
                    return x.rearrange("p (o t) -> p o t", o=1).broadcast_to((x.shape[0], GB, S))
                dve.tensor_tensor(v(dst), v(ps), tab(rot_cos[w]), ALU.mult).then_inc(s_rot, 1)
                for lo, hi in ((0, 64), (64, 0)):
                    dve.tensor_tensor(v(swp[w][lo:lo + 64, :]), v(ps[hi:hi + 64, :]), tab(rot_sin[w][hi:hi + 64, :]),
                                      ALU.mult).then_inc(s_rot, 1)

            def apply_mask(g, h):
                head = H0 * g + h
                for b in range(GB):
                    dve.wait_ge(s_sp, 2 * head + b + 1)
                    if not isinstance(g, int) or head >= 2:
                        dve.wait_ge(s_pv, head - 1)
                    dve.tensor_tensor(pm[h % 2][:, b, :], banks[:, 6 + b, 0:MW], mask[:, h, :],
                                      ALU.mult).then_inc(s_pm, 1)

            def gn_stats(g):
                base = GN_STEPS * g
                for c in range(NCH):
                    for b in range(GB):
                        dve.wait_ge(s_oT, NCH * g + c + 1)
                        dve.bn_stats(gst[:, 2 * c + b, :], oT[:, c, b * S:(b + 1) * S]).then_inc(s_gn, 1)
                dve.wait_ge(s_gn, base + 6)
                dve.memset(wait_slot[:, :], 0.0)
                for n in range(2 * NCH):
                    dve.bn_aggr(gmv[:, n, :], gst[:, n, :]).then_inc(s_gn, 1)
                dve.wait_ge(s_gn, base + 12)
                dve.tensor_tensor(gmsq, gmv[:, :, 0], gmv[:, :, 0], ALU.mult).then_inc(s_gn, 1)
                dve.wait_ge(s_gn, base + 13)
                dve.tensor_tensor(gmv[:, :, 1], gmv[:, :, 1], gmsq, ALU.add).then_inc(s_gn, 1)

            def gn_var(g):
                base = GN_STEPS * g + 14
                dve.wait_ge(s_gstat, g + 1)
                dve.tensor_copy(gs, banks[:, 0, 400:400 + 4 * NCH].rearrange("p (n s) -> p n s", s=2)).then_inc(s_gn, 1)
                dve.wait_ge(s_gn, base + 1)
                dve.tensor_tensor(gmsq, gs[:, :, 0], gs[:, :, 0], ALU.mult).then_inc(s_gn, 1)
                dve.wait_ge(s_gn, base + 2)
                dve.scalar_tensor_tensor(gvar, gs[:, :, 1], EPS, gmsq, ALU.add, ALU.subtract).then_inc(s_gn, 1)

            def gn_apply(g):
                base = GN_STEPS * g + GN_VAR

                def pair(x):
                    return x.rearrange("p (c b) -> p c b", b=GB)

                def per_c(x):
                    return x.rearrange("p (c o) -> p c o", o=1).broadcast_to((P, NCH, GB))
                dve.wait_ge(s_grs, g + 1)
                dve.tensor_tensor(pair(gsc), pair(grs), per_c(gnw), ALU.mult).then_inc(s_gn, 1)
                dve.wait_ge(s_gn, base + 1)
                dve.tensor_tensor(gmb, gs[:, :, 0], gsc, ALU.mult).then_inc(s_gn, 1)
                dve.wait_ge(s_gn, base + 2)
                dve.tensor_tensor(pair(gbi), per_c(gnb), pair(gmb), ALU.subtract).then_inc(s_gn, 1)
                dve.wait_ge(s_gn, base + 3)
                dve.wait_ge(s_rop, g)
                for c in range(NCH):
                    for b in range(GB):
                        n = 2 * c + b
                        dve.tensor_scalar(ng[:, c, b * S:(b + 1) * S], oT[:, c, b * S:(b + 1) * S], gsc[:, n:n + 1],
                                          gbi[:, n:n + 1], ALU.mult, ALU.add).then_inc(s_gn, 1)
                dve.wait_ge(s_gn, base + 9)
                dve.wait_ge(s_vge, 7 * g + 7)
                dve.tensor_tensor(ng, ng, gate, ALU.mult).then_inc(s_ng, 1)

            def ret_residual(g):
                dve.wait_ge(s_rop, g + 1)
                for i in range(2):
                    xt = X[:, bass.ds(g * GT + 2 * i, 2), :]
                    dve.tensor_tensor(xt, banks[:, i, 0:2 * D].rearrange("p (t d) -> p t d", t=2), xt,
                                      ALU.add).then_inc(s_rres, 1)

            def ret(g, cur, prev):
                for h in range(H0):
                    if cur:
                        rotary(g, h, 0)
                        rotary(g, h, 1)
                        if h >= 1:
                            apply_mask(g, h - 1)
                    if prev and h == 0:
                        gn_stats(g - 1)
                    if prev and h == 1:
                        gn_var(g - 1)
                    if prev and h == 2:
                        gn_apply(g - 1)
                    if prev and h == 4:
                        ret_residual(g - 1)
                    if cur and h == 4 and not (isinstance(g, int) and g == NG - 1):
                        ln_stats(dve, NT + g + 1, (g + 1) * GT)
                        ln_apply(dve, NT + g + 1, (g + 1) * GT)
                if cur:
                    apply_mask(g, H0 - 1)
            dve.wait_ge(s_res, TOK_DONE)
            ln_stats(dve, NT, 0)
            ln_apply(dve, NT, 0)
            dve.wait_ge(s_rw, RET_W)
            run_groups(dve, ret)

            def shift_logits(g):
                dve.wait_ge(s_lt, 2 * g + 1)
                dve.reduce_max(mx, banks[0:SLOTS, 2, :].rearrange("p (b t) -> p b t", b=GB), AX_X).then_inc(s_mx, 1)
                dve.wait_ge(s_mx, g + 1)
                wait(dve, s_E, 2 * g)
                dve.tensor_scalar(nmx, mx, -1.0, None, ALU.mult).then_inc(s_nmx, 1)
                dve.wait_ge(s_lt, 2 * g + 2)
                lg = banks[:, 3, 0:GT * SLOTS].rearrange("p (t s) -> p t s", t=GT)
                dve.reduce_max(cmx, lg, AX_X).then_inc(s_cmx, 1)
                dve.wait_ge(s_cmx, g + 1)
                wait(dve, s_trc, g)
                dve.tensor_tensor(Cl, lg, per_tile(cmx, SLOTS), ALU.subtract).then_inc(s_sub, 1)

            def per_tile(x, n):
                return x.rearrange("p (t o) -> p t o", o=1).broadcast_to((P, GT, n))

            def weighted_norm(i, par):
                q = Q_MIX + i
                ln_stats(dve, q, i * GT, 1.0 + EPS, EPS * EPS)
                dve.wait_ge(s_rstd, q + 1)
                wait(dve, s_y, i - 1)
                for t in range(GT):
                    xt = X[:, bass.ds(i * GT + t, 1), :].rearrange("p a d -> p (a d)")
                    dve.tensor_scalar(xw[par][:, t, :], xt, mv[:, t, 0:1], rstd[:, t:t + 1],
                                      ALU.subtract, ALU.mult).then_inc(s_xn, 1)
                dve.wait_ge(s_xn, GT * (q + 1))
                dve.tensor_tensor(xw[par], xw[par], normw.rearrange("p (o d) -> p o d", o=1).broadcast_to((P, GT, D)),
                                  ALU.mult).then_inc(s_xw, 1)

            def combine_weights(g):
                dve.wait_ge(s_cexp, g + 1)
                dve.reduce_sum(csum, Cl, AX_X).then_inc(s_csum, 1)
                dve.wait_ge(s_csum, 2 * g + 1)
                dve.reciprocal(crec, csum).then_inc(s_csum, 1)
                dve.wait_ge(s_csum, 2 * g + 2)
                dve.tensor_tensor(Cl, Cl, per_tile(crec, SLOTS), ALU.mult).then_inc(s_cn, 1)

            def unit_tokens(i, par):
                dve.wait_ge(s_n2, GT * (i + 1))
                dve.tensor_scalar(n2c, n2, 1e-10, None, ALU.max).then_inc(s_n2c, 1)
                dve.wait_ge(s_rn, i + 1)
                dve.wait_ge(s_tr, 2 * (Q_MIX + i))
                for t in range(GT):
                    dve.tensor_scalar(tokn[:, t, :], xw[par][:, t, :], rn[:, t:t + 1], None, ALU.mult).then_inc(s_tokn, 1)

            def slot_inputs(g):
                dve.wait_ge(s_y, g + 1)
                dve.reciprocal(rden, den).then_inc(s_rden, 1)
                dve.wait_ge(s_rden, g + 1)
                wait(dve, s_trY, g)
                for b in range(GB):
                    dve.tensor_scalar(yv[:, b, :], banks[0:SLOTS, 6, b * D:(b + 1) * D], rden[:, b:b + 1], None,
                                      ALU.mult).then_inc(s_yv, 1)

            def mix(i, par, cur, prev):
                if prev:
                    shift_logits(i - 1)
                if cur:
                    weighted_norm(i, par)
                if prev:
                    combine_weights(i - 1)
                if cur:
                    unit_tokens(i, par)
                if prev:
                    slot_inputs(i - 1)
            dve.wait_ge(s_rres, 2 * NG)
            run_mix(mix)(dve)

            def bias_fc1(n, r):
                dve.wait_ge(s_ht, n + 1)
                wait(dve, s_gl, n - 1)
                dve.tensor_tensor(hb[r % 2].rearrange("p (c b) -> p c b", c=FC),
                                  banks[:, 4 + r % 2, 0:FC * B].rearrange("p (c b) -> p c b", c=FC),
                                  b1[:, bass.ds(n, 1), :].rearrange("p o c -> p c o").broadcast_to((P, FC, B)),
                                  ALU.add).then_inc(s_hb, 1)

            def slot(n, r, k):
                if not isinstance(n, int) or n >= 1:
                    bias_fc1(n - 1, (r - 1) % RING)
                dve.wait_ge(s_fc1, n + 1)
                wait(dve, s_ht, n - 1)
                dve.tensor_copy(hraw[r % 2], banks[0:B, 2 * (r % 2):2 * (r % 2) + 2, :].rearrange("p a n -> p (a n)")
                                [:, 0:FF]).then_inc(s_hr, 1)
            run_slots(dve, slot)
            bias_fc1(SLOTS - 1, RING - 1)

            def combine(g, cur, prev):
                if prev:
                    dve.wait_ge(s_co, g)
                    for i in range(2):
                        xt = X[:, bass.ds((g - 1) * GT + 2 * i, 2), :]
                        dve.tensor_tensor(xt, banks[:, i, 0:2 * D].rearrange("p (t d) -> p t d", t=2), xt,
                                          ALU.add).then_inc(s_cres, 1)
                if cur:
                    wait(dve, s_co, g)
                    dve.tensor_tensor(y2, y2all[:, bass.ds(g * GB, GB), :],
                                      b2.rearrange("p (o d) -> p o d", o=1).broadcast_to((SLOTS, GB, D)),
                                      ALU.add).then_inc(s_y2, 1)
            dve.wait_ge(s_y2a, 16)
            run_combine(dve, combine)

            def job_wait(n):
                dve.wait_ge(s_jp, n + 1)

            def values(par, t, n):
                job_wait(n)
                dve.tensor_tensor(va[par][:, t, :, 0:HD1], banks[:, 6, 0:D].rearrange("p (h d) -> p h d", h=H1),
                                  vb1.rearrange("p (h d) -> p h d", h=H1), ALU.add).then_inc(s_je, 1)

            def norm_stats(g):
                ln_stats(dve, Q_ATT + g, g * GT)

            def norm_apply(g, *free):
                ln_apply(dve, Q_ATT + g, g * GT, free)

            def att_residual(g, b, n):
                job_wait(n)
                dve.wait_ge(s_pb, g + 1)
                xt = X[:, bass.ds(g * GT + 2 * b, 2), :]
                dve.tensor_tensor(xt, banks[:, 6, 0:2 * D].rearrange("p (t d) -> p t d", t=2), xt,
                                  ALU.add).then_inc(s_je, 1)

            def normalise(n_b):
                dve.wait_ge(s_av, QG * (n_b + 1))
                o = banks[:, 7, 0:2 * H1 * (HD1 + 1)].rearrange("p (n h e) -> p n h e", n=2, h=H1)
                dve.reciprocal(ssum, o[:, :, :, HD1]).then_inc(s_sr, 1)
                dve.wait_ge(s_sr, n_b + 1)
                dve.tensor_tensor(ao.rearrange("p n (h d) -> p (n h) d", h=H1),
                                  banks[:, 7, 0:2 * H1 * (HD1 + 1)].rearrange("p (m e) -> p m e", e=HD1 + 1)[:, :, 0:HD1],
                                  ssum.rearrange("p n (h o) -> p (n h) o", o=1).broadcast_to((P, 2 * H1, HD1)),
                                  ALU.mult).then_inc(s_ao, 1)

            def att(g, par, base, jobs):
                for u in range(UN):
                    U = UN * g + u
                    dve.wait_ge(s_p1, U + 1)
                    dve.reduce_max(smx, banks[:, 0:HG, :].rearrange("p h (n m) -> p h n m", n=2), AX_X).then_inc(s_smx, 1)
                    dve.wait_ge(s_smx, U + 1)
                    dve.tensor_scalar(mt.rearrange("p n (h r) -> p n h r", r=HR)[:, :, :, HD1],
                                      smx.rearrange("p h n -> p n h"), -1.0, None, ALU.mult).then_inc(s_neg, 1)
                    if (u, 1) in jobs:
                        kind, item, n = jobs[u, 1]
                        if kind == "v":
                            values(1 - par, item, base + n)
                        elif kind == "proj":
                            att_residual(g - item, item, base + n)
                    if u == 5:
                        normalise(GB * g)
                    if u == 1 and not (isinstance(g, int) and g == 0):
                        normalise(GB * g - 1)
                    if u == 3 and (UN - 1, 3) in jobs:
                        norm_stats(g + 2)
                    if u == 4 and (UN - 1, 3) in jobs:
                        norm_apply(g + 2, s_jp, base)
                    _, _, n = jobs[u, 2]
                    job_wait(base + n)
                    wait(dve, s_p2, U)
                    dve.tensor_tensor(qa, qkT[par][u % QG][:, (u // QG) * S:(u // QG + 1) * S], banks[0:QT, 6, 0:S],
                                      ALU.add).then_inc(s_je, 1)
            dve.wait_ge(s_cres, 2 * NG)
            dve.memset(mt, 0.0).then_inc(s_da, 1)
            for v in va:
                dve.memset(v[:, :, :, HD1:], 1.0).then_inc(s_da, 1)
            norm_stats(0)
            norm_apply(0, s_tr, 2 * Q_ATT)
            dve.wait_ge(s_aw, AW)
            dve.tensor_scalar(qkb[:, 0:QG], qkb[:, 0:QG], HD1 ** -0.5, None, ALU.mult).then_inc(s_qb, 1)
            dve.wait_ge(s_da, 3)
            for t in range(GT):
                values(0, t, 2 + 2 * QG + t)
            norm_stats(1)
            norm_apply(1, s_jp, 2)
            run_attention(dve, att)
            normalise(GB * NG - 1)
            att_residual(NG - 1, 1, JOBS_TAIL + 1)

            def ffn_norm(g):
                ln_stats(dve, Q_FFN + g, g * GT)
                if isinstance(g, int) and g == 0:
                    ln_apply(dve, Q_FFN, 0, (s_jp, JOBS_TAIL))
                else:
                    ln_apply(dve, Q_FFN + g, g * GT, (s_tr, 2 * (Q_ATT + g)))

            cls_n_done = [0]

            def cls_link(ins):
                cls_n_done[0] += 1
                ins.then_inc(s_cls, 1)
                dve.wait_ge(s_cls, cls_n_done[0])

            def over(x, n):
                return x.rearrange("p (s o) -> p s o", o=1).broadcast_to((CT_N, x.shape[1], n))

            def class_norm():
                dve.wait_ge(s_clsg, 16 * NCLS)
                cls_link(dve.bn_stats(cst, cls_x))
                cls_link(dve.bn_aggr(cmv, cst))
                cls_link(dve.tensor_scalar(cpw[:, 0:1], cmv[:, 1:2], EPS, None, ALU.add))
                assert cls_n_done[0] == CLS_VAR
                dve.wait_ge(s_crs, 1)
                cls_link(dve.tensor_scalar(cls_n, cls_x, cmv[:, 0:1], crs[:, 0:1], ALU.subtract, ALU.mult))

            def class_route():
                one = cls_n.rearrange("p (o d) -> p o d", o=1).broadcast_to((CT_N, 2, D))
                cls_link(dve.tensor_tensor(gprod, gates, one, ALU.mult))
                cls_link(dve.reduce_sum(dots, gprod, AX_X))
                dve.wait_ge(s_csq, 3)
                cls_link(dve.tensor_scalar(cpw[:, 1:4], cpw[:, 1:4], 1e-24, None, ALU.max))
                assert cls_n_done[0] == CLS_NORMS
                dve.wait_ge(s_crs, 2)
                cls_link(dve.tensor_scalar(dots, dots, crs[:, 1:2], None, ALU.mult))
                cls_link(dve.tensor_tensor(dots, dots, crs[:, 2:4], ALU.mult))
                cls_link(dve.tensor_tensor(lg1, dots, balance, ALU.add))
                cls_link(dve.reduce_max(lmax, lg1, AX_X))
                cls_link(dve.tensor_scalar(lg1, lg1, lmax, None, ALU.subtract))
                dve.wait_ge(s_cexp2, 1)
                cls_link(dve.reduce_sum(psum_[:, 0:1], prob, AX_X))
                cls_link(dve.reciprocal(psum_[:, 1:2], psum_[:, 0:1]))
                cls_link(dve.tensor_scalar(prob, prob, psum_[:, 1:2], None, ALU.mult))
                cls_link(dve.tensor_tensor(pick[:, 1:2], prob[:, 1:2], prob[:, 0:1], ALU.is_gt))
                cls_link(dve.tensor_scalar(pick[:, 0:1], pick[:, 1:2], -1.0, 1.0, ALU.mult, ALU.add))
                cls_link(dve.tensor_tensor(pick, pick, prob, ALU.mult))

            def class_out():
                for a in range(NATOMS):
                    role, which = ATOM_ROLE[a]
                    w = len(range(NCLS)[which]) * B
                    dve.wait_ge(s_aout, a + 1)
                    for k in range(2):
                        dve.tensor_scalar(classes(cand[1 - role][:, k, :], which),
                                          banks[0:HD, 6 + a % 2, k * w:(k + 1) * w].rearrange("p (n b) -> p n b", b=B),
                                          atom_b2[:, a, k:k + 1], None, ALU.add).then_inc(s_cand, 1)
                for r in range(2):
                    dve.wait_ge(s_candT, 1)
                    wait(dve, s_fin, r)
                    dve.scalar_tensor_tensor(fin[r], banks[0:CT_N, 7, r * D:(r + 1) * D], pick[:, r:r + 1],
                                             fin[0] if r else cls_x, ALU.mult, ALU.add).then_inc(s_fin, 1)

            def ffn(g, par, cur, prev):
                if cur and not (isinstance(g, int) and g == NG - 1):
                    ffn_norm(g + 1)
                if prev:
                    dve.wait_ge(s_f2, g)
                    dve.wait_ge(s_b2f, g)
                    for i in range(2):
                        xt = X[:, bass.ds((g - 1) * GT + 2 * i, 2), :]
                        dve.tensor_tensor(xt, banks[:, 6 + i, 0:2 * D].rearrange("p (t d) -> p t d", t=2), xt,
                                          ALU.add).then_inc(s_eres, 1)
                if isinstance(g, int) and g == 0:
                    class_norm()
                    class_route()
                if isinstance(g, int) and g == NG - 1:
                    class_out()
            dve.wait_ge(s_je, JOBS_TAIL + 2)
            ffn_norm(0)
            dve.wait_ge(s_fw, FW)
            run_mix(ffn)(dve)

        @block.scalar
        def _(act):
            act.wait_ge(s_cw, CW)
            act.activation(slT_junk[:, :], slots, ACT.Square, accum_out=sln2[:, 0:1]).then_inc(s_slq, 1)
            act.wait_ge(s_slp, 1)
            act.activation(slT[:, :, :], banks[0:HD, 0, 0:2 * SLOTS].rearrange("p (k s) -> p k s", k=2),
                           ACT.Identity).then_inc(s_slT, 1)
            act.wait_ge(s_nbd, 1)
            act.wait_ge(s_pads, 2)

            def col(lay, c):
                return vec[:, bass.ds(lay, 1), c:c + 1].rearrange("p a b -> p (a b)")

            def step(j, par, on):
                if 0 in on:
                    if not isinstance(j, int) or j >= 2:
                        act.wait_ge(s_conv, 8 * (j - 1))
                    for k in range(2):
                        act.wait_ge(s_uvp, 4 * j + k + 1)
                        act.activation(upad[par][:, k, :, TAPS - 1:],
                                       banks[0:HD, 4 + k, :].rearrange("p (b t) -> p b t", b=GB),
                                       ACT.Identity, bias=col(j // NG, V_BU + k), scale=1.0).then_inc(s_uve, 1)
                    if not isinstance(j, int) or j >= 2:
                        act.wait_ge(s_wop, j - 1)
                    for k in range(2):
                        act.wait_ge(s_uvp, 4 * j + k + 3)
                        act.activation(sv[par][:, k, :], banks[0:HD, 6 + k, :], ACT.Sigmoid,
                                       bias=col(j // NG, V_BV + k), scale=1.0).then_inc(s_uve, 1)
                if -1 in on:
                    q = j + 1
                    act.wait_ge(s_uvp, 4 * q)
                    for k in range(2):
                        act.wait_ge(s_tr, 2 * q + k + 1)
                        act.activation(hT[:, k, :], banks[0:HD, k, :], ACT.Identity,
                                       bias=col(q // NG, V_BT + k), scale=col(q // NG, V_G + k)).then_inc(s_hT, 1)
                if 1 in on:
                    q = j - 1
                    for n, (dst, c, free) in enumerate(((dec, V_NBD, s_scan), (Bs, V_BB, s_inp), (Cs, V_BC, s_hc))):
                        act.wait_ge(free, q)
                        for k in range(2):
                            act.wait_ge(s_zp, 6 * q + 2 * n + k + 1)
                            act.activation(dst[:, k, :], banks[0:HD, 4 + (2 * n + k) % 4, :],
                                           ACT.Sigmoid if n == 0 else ACT.Identity,
                                           bias=col(q // NG, c + k), scale=-1.0 if n == 0 else 1.0).then_inc(s_ze, 1)
            run_tok(act, step)

            def plain_hT(q, free, value):
                act.wait_ge(free, value)
                for k in range(2):
                    act.wait_ge(s_tr, 2 * q + k + 1)
                    act.activation(hT[:, k, :], banks[0:HD, k, :], ACT.Identity).then_inc(s_hT, 1)

            def ret(g, cur, prev):
                if not cur:
                    return
                act.wait_ge(s_pv, H0 * g)
                for i in range(GT):
                    act.wait_ge(s_vgp, 7 * g + i + 1)
                    act.activation(vt[:, i, :], banks[:, 4, 0:HV], ACT.Identity).then_inc(s_vge, 1)
                act.wait_ge(s_ng, g)
                for c in range(NCH):
                    act.wait_ge(s_vgp, 7 * g + GT + c + 1)
                    act.activation(gate[:, c, :], banks[:, 4, :], ACT.Silu).then_inc(s_vge, 1)
                    if c != 1:
                        act.wait_ge(s_pv, H0 * g + (2 if c == 0 else 4))
                        act.activation(oT[:, c // 2, :], banks[:, 5, :], ACT.Identity).then_inc(s_oT, 1)
                if not (isinstance(g, int) and g == NG - 1):
                    plain_hT(NT + g + 1, s_qkp, 12 * (g + 1))
                act.wait_ge(s_pv, H0 * g + 6)
                act.activation(oT[:, 2, :], banks[:, 5, :], ACT.Identity).then_inc(s_oT, 1)
            plain_hT(NT, s_uvp, 4 * NT)
            act.wait_ge(s_res, TOK_DONE)
            run_groups(act, ret)

            def mix(i, par, cur, prev):
                g = i - 1
                if prev:
                    act.wait_ge(s_nmx, g + 1)
                    wait(act, s_tre, g)
                    wait(act, s_yv, 2 * g)
                    for b in range(GB):
                        act.activation(E_[:, b * S:(b + 1) * S], banks[0:SLOTS, 2, b * S:(b + 1) * S], ACT.Exp,
                                       bias=nmx[:, b:b + 1], scale=1.0, accum_out=den[:, b:b + 1]).then_inc(s_E, 1)
                    act.wait_ge(s_sub, g + 1)
                    act.activation(Cl, Cl, ACT.Exp).then_inc(s_cexp, 1)
                if cur:
                    act.wait_ge(s_xw, i + 1)
                    wait(act, s_n2c, i)
                    wait(act, s_n2, GT * i)
                    for t in range(GT):
                        act.activation(sq[:, t, :], xw[par][:, t, :], ACT.Square, accum_out=n2[:, t:t + 1]).then_inc(s_n2, 1)
                if prev:
                    act.wait_ge(s_tre, g + 1)
                    wait(act, s_y, g)
                    act.activation(eT, banks[:, 4, 0:GT * SLOTS].rearrange("p (t s) -> p t s", t=GT),
                                   ACT.Identity).then_inc(s_eT, 1)
                    act.wait_ge(s_trc, g + 1)
                    act.activation(CT[:, bass.ds(g * N, N)], banks[0:SLOTS, 5, :], ACT.Identity).then_inc(s_CT, 1)
                if cur:
                    if isinstance(i, int) and i == 0:
                        plain_hT(Q_MIX, s_qkp, 12 * NG)
                    else:
                        plain_hT(Q_MIX + i, s_lt, 2 * i)
                if prev:
                    act.wait_ge(s_trY, g + 1)
                    for b in range(GB):
                        act.activation(YT[:, :, :, bass.ds(g * GB + b, 1)].rearrange("p k s o -> p k (s o)"),
                                       banks[0:HD, 7, b * 2 * SLOTS:(b + 1) * 2 * SLOTS]
                                       .rearrange("p (k s) -> p k s", k=2), ACT.Identity).then_inc(s_YT, 1)
            act.wait_ge(s_rres, 2 * NG)
            run_mix(mix)(act)

            def copy_input(n, r):
                wait(act, s_fc1, n - 1)
                act.activation(ys[r % 2], YT[:, :, bass.ds(n, 1), :].rearrange("p k o b -> p k (o b)"),
                               ACT.Identity).then_inc(s_ys, 1)

            def finish_slot(n, r, k):
                act.wait_ge(s_hb, n + 1)
                wait(act, s_fc2, n - 1)
                act.activation(gl[r % 2], hb[r % 2], ACT.Gelu).then_inc(s_gl, 1)
                act.wait_ge(s_fc2, n + 1)
                if r == 0:
                    wait(act, s_y2d, 16 * k)
                act.activation(fo[:, r, :], banks[0:B, 6 + r % 2, 0:D], ACT.Identity).then_inc(s_y2c, 1)
                if r == RING - 1:
                    act.wait_ge(s_y2c, n + 1)
                    act.dma_start(slot_out[bass.ds(RING * k, RING)].rearrange("s b d -> b s d"), fo
                                  ).then_inc(s_y2d, 16)

            def slot(n, r, k):
                copy_input(n, r)
                if not (isinstance(n, int) and n == 0):
                    finish_slot(n - 1, (r - 1) % RING, k if r else k - 1)
            act.wait_ge(s_YT, GB * NG)
            run_slots(act, slot)
            finish_slot(SLOTS - 1, RING - 1, SLOTS // RING - 1)

            def combine(g, cur, prev):
                if cur:
                    wait(act, s_co, g)
                    act.activation(CTs, CT[:, bass.ds(g * N, N)], ACT.Identity).then_inc(s_cp, 1)
            run_combine(act, combine)

            def half_hT(k, n):
                act.wait_ge(s_jp, n + 1)
                act.activation(hT[:, k, :], banks[0:HD, 6, :], ACT.Identity).then_inc(s_je, 1)

            def qk_out(par, i, n):
                w, c = i % 2, i // 2
                act.wait_ge(s_jp, n + 1)
                m = w * QG + c
                act.activation(qkT[par][m], banks[0:QT, 6, :], ACT.Identity, bias=qkb[:, m:m + 1],
                               scale=1.0 if w else HD1 ** -0.5).then_inc(s_je, 1)

            def exps(U, par):
                act.wait_ge(s_p2, U + 1)
                wait(act, s_av, U - 1)
                act.activation(pT[par].rearrange("p h m n -> p h (m n)"), banks[:, 3:3 + HG, :],
                               ACT.Exp).then_inc(s_ex, 1)

            def att(g, par, base, jobs):
                for u in range(UN):
                    if (u, 0) in jobs:
                        _, item, n = jobs[u, 0]
                        qk_out(1 - par, item, base + n)
                    if (u, 1) in jobs and jobs[u, 1][0] == "aoT":
                        act.wait_ge(s_jp, base + jobs[u, 1][2] + 1)
                        act.activation(aoT, banks[0:HD, 6, :].rearrange("p (k n) -> p k n", k=2),
                                       ACT.Identity).then_inc(s_je, 1)
                    if u or not isinstance(g, int) or g:
                        exps(UN * g + u - 1, (u + 1) % 2)
                for k in range(2):
                    if (UN - 1 + k, 3) in jobs:
                        half_hT(k, base + jobs[UN - 1 + k, 3][2])
            act.wait_ge(s_cres, 2 * NG)
            act.wait_ge(s_qb, 1)
            for k in range(2):
                half_hT(k, k)
            for i in range(2 * QG):
                qk_out(0, i, 2 + i)
            for k in range(2):
                half_hT(k, JOBS_FIRST - 2 + k)
            run_attention(act, att)
            exps(UN * NG - 1, 1)
            act.wait_ge(s_jp, JOBS_TAIL + 1)
            act.activation(aoT, banks[0:HD, 6, :].rearrange("p (k n) -> p k n", k=2), ACT.Identity).then_inc(s_je, 1)

            def ffn(g, par, cur, prev):
                if cur:
                    wait(act, s_f2, g - 1)
                    for c in range(FC):
                        act.wait_ge(s_f1, FC * g + c + 1)
                        act.activation(hid[par][:, c, :], banks[:, 2 + (FC * par + c) % 4, :], ACT.Gelu,
                                       bias=b1f[:, c:c + 1], scale=1.0).then_inc(s_gf, 1)
                    if not (isinstance(g, int) and g == NG - 1):
                        plain_hT(Q_ATT + g + 1, s_f1, FC * (g + 1))
                if isinstance(g, int) and g == 0:
                    act.wait_ge(s_cls, CLS_VAR + 1)
                    act.activation(csq[:, 0, :], cls_n, ACT.Square, accum_out=cpw[:, 1:2]).then_inc(s_csq, 1)
                    for r in range(2):
                        act.activation(csq[:, 1 + r, :], gates[:, r, :], ACT.Square,
                                       accum_out=cpw[:, 2 + r:3 + r]).then_inc(s_csq, 1)
                    act.wait_ge(s_clT, 1)
                    act.activation(cls_T, banks[0:HD, 6, 0:2 * CT_N].rearrange("p (k n) -> p k n", k=2),
                                   ACT.Identity).then_inc(s_clTe, 1)
                    for a in range(NATOMS):
                        role, which = ATOM_ROLE[a]
                        w = len(range(NCLS)[which]) * B
                        act.wait_ge(s_ain, a + 1)
                        for c in range(FC):
                            act.activation(classes(cls_h[role][:, c, :], which),
                                           banks[:, 7 - a % 2, c * w:(c + 1) * w].rearrange("p (n b) -> p n b", b=B),
                                           ACT.Gelu, bias=atom_b1[:, a, c:c + 1], scale=1.0).then_inc(s_ag, 1)
                    act.wait_ge(s_cls, CLS_NORMS + 5)
                    act.activation(prob, lg1, ACT.Exp).then_inc(s_cexp2, 1)
            act.wait_ge(s_je, JOBS_TAIL + 2)
            act.wait_ge(s_fw, FW)
            plain_hT(Q_ATT, s_jp, JOBS_TAIL)
            run_mix(ffn)(act)

        @block.tensor
        def _(pe):
            pe.wait_ge(s_const, 4 + HG)
            pe.wait_ge(s_sl, 2)
            for k in range(2):
                ins = pe.transpose(banks[0:HD, 0, k * SLOTS:(k + 1) * SLOTS], slots[:, k * HD:(k + 1) * HD],
                                   ident[0:SLOTS, 0:SLOTS])
            ins.then_inc(s_slp, 1)
            pe.wait_ge(s_slT, 1)

            def two_halves(o, w, x):
                pe.matmul(o, w(0), x(0), start=True, stop=False)
                return pe.matmul(o, w(1), x(1), start=False, stop=True)

            def wo_part(j, par):
                pe.wait_ge(s_wout, (j // NG + 1) * 16)
                pe.wait_ge(s_uve, 4 * j + 4)
                pe.wait_ge(s_res, GT * j)
                for i in range(GT):
                    ins = two_halves(banks[:, 2 + i // 2, (i % 2) * D:(i % 2 + 1) * D],
                                     lambda k: sv[par][:, k, i * P:(i + 1) * P], lambda k: wout[:, k, :])
                ins.then_inc(s_wop, 1)

            def y_part(j, transposed):
                pe.wait_ge(s_hsum, j + 1)
                if transposed:
                    pe.wait_ge(s_hT, 2 * (j + 4))
                for i in range(GT):
                    ins = pe.transpose(banks[:, 0, i * HD:(i + 1) * HD], hsum[:, i * P:(i + 1) * P], ident[0:HD, 0:HD])
                ins.then_inc(s_yp, 1)

            def uv_part(j):
                pe.wait_ge(s_win, (j // NG + 1) * 16)
                pe.wait_ge(s_hT, 2 * j + 2)
                for c in range(4):
                    if not isinstance(j, int) or j >= 2:
                        pe.wait_ge(s_ze, 6 * (j - 2) + (5, 6, 3, 4)[c])
                    two_halves(banks[0:HD, 4 + c, :], lambda k: win[:, k, c * HD:(c + 1) * HD],
                               lambda k: hT[:, k, :]).then_inc(s_uvp, 1)

            def zbc_part(j, uv_between, between):
                pe.wait_ge(s_wzbc, (j // NG + 1) * 16)
                pe.wait_ge(s_conv, 8 * j + 8)
                for c in range(6):
                    if c == 2:
                        between()
                    if c >= 4:
                        pe.wait_ge(s_ze, 6 * j + c - 3)
                    elif uv_between:
                        pe.wait_ge(s_uve, 4 * (j + 1) + c + 1)
                    else:
                        pe.wait_ge(s_ze, 6 * (j - 1) + (5, 6, 3, 4)[c])
                    two_halves(banks[0:HD, 4 + c % 4, :], lambda k: wzbc[:, k, c * HD:(c + 1) * HD],
                               lambda k: uc[:, k, :]).then_inc(s_zp, 1)

            def step(j, par, on):
                if 2 in on:
                    wo_part(j - 2, par)
                if 0 in on:
                    uv_part(j)
                if -1 in on:
                    wait(pe, s_ysum, j - 2)
                    transpose_group(pe, j + 1)

                def y_between():
                    if 2 in on:
                        y_part(j - 2, -1 in on)
                if 1 in on:
                    zbc_part(j - 1, 0 in on, y_between)
                else:
                    y_between()
            run_tok(pe, step)

            def vg(g, n):
                pe.wait_ge(s_vge, 7 * g + n)
                if n < GT:
                    two_halves(banks[:, 4, 0:HV], lambda k: hT[:, k, n * P:(n + 1) * P],
                               lambda k: wv[:, k, :]).then_inc(s_vgp, 1)
                else:
                    c = n - GT
                    two_halves(banks[:, 4, :], lambda k: wg[:, k, c * P:(c + 1) * P],
                               lambda k: hT[:, k, :]).then_inc(s_vgp, 1)

            def qk_item(g, h, w):
                n = 12 * g + 2 * h + w
                if not isinstance(g, int) or n >= 2:
                    pe.wait_ge(s_rot, 3 * (n - 1))
                two_halves(banks[:, 2 + w, :], lambda k: (wq, wk)[w][:, k, h * P:(h + 1) * P],
                           lambda k: hT[:, k, :]).then_inc(s_qkp, 1)

            def scores(g, h):
                head = H0 * g + h
                q, k = qk[0][h % 2], qk[1][h % 2]
                pe.wait_ge(s_radd, 2 * (head + 1))
                for b in range(GB):
                    if not isinstance(g, int) or head >= 1:
                        pe.wait_ge(s_pm, 2 * (head - 1) + b + 1)
                    pe.matmul(banks[:, 6 + b, 0:S], k[:, b * S:b * S + P], q[:, b * S:(b + 1) * S],
                              start=True, stop=True)
                    pe.matmul(banks[:, 6 + b, S:MW], k[:, b * S + P:(b + 1) * S], q[:, b * S + P:(b + 1) * S],
                              start=True, stop=True).then_inc(s_sp, 1)

            def pv(g, h):
                head = H0 * g + h
                if h % 2 == 0:
                    pe.wait_ge(s_oT, NCH * g + h // 2)
                pe.wait_ge(s_pm, 2 * head + 2)
                pe.wait_ge(s_vge, 7 * g + GT)
                r = (h % 2) * DV
                for b in range(GB):
                    pe.matmul(banks[r:r + DV, 5, b * S:(b + 1) * S], vt[:, 2 * b, h * DV:(h + 1) * DV],
                              pm[h % 2][:, b, 0:S], start=True, stop=False)
                    ins = pe.matmul(banks[r:r + DV, 5, b * S + P:(b + 1) * S], vt[:, 2 * b + 1, h * DV:(h + 1) * DV],
                                    pm[h % 2][:, b, S:MW], start=False, stop=True)
                ins.then_inc(s_pv, 1)

            def gn_sums(g):
                pe.wait_ge(s_gn, GN_STEPS * g + 14)
                pe.wait_ge(s_hT, 2 * (NT + g + 1) if not isinstance(g, int) or g < NG - 1 else 2 * (NT + NG))
                pe.matmul(banks[:, 0, 400:400 + 4 * NCH], blk, gmv.rearrange("p n s -> p (n s)"),
                          start=True, stop=True).then_inc(s_gstat, 1)

            def ret_out(g):
                pe.wait_ge(s_ng, g + 1)
                for i in range(GT):
                    for c in range(NCH):
                        ins = pe.matmul(banks[:, i // 2, (i % 2) * D:(i % 2 + 1) * D], ng[:, c, i * P:(i + 1) * P],
                                        wo[:, c, :], start=c == 0, stop=c == NCH - 1)
                ins.then_inc(s_rop, 1)

            def ret(g, cur, prev):
                if cur:
                    pe.wait_ge(s_hT, 2 * (NT + g) + 2)
                for h in range(H0):
                    if cur:
                        for w in range(2):
                            if 2 * h + w < GT:
                                vg(g, 2 * h + w)
                            elif w == 0 and h >= 3:
                                vg(g, GT + h - 3)
                            qk_item(g, h, w)
                    if prev and h == 0:
                        gn_sums(g - 1)
                    if cur and h >= 2:
                        pv(g, h - 2)
                    if cur and h >= 1:
                        scores(g, h - 1)
                    if prev and h == 3:
                        ret_out(g - 1)
                if cur:
                    pv(g, H0 - 2)
                    scores(g, H0 - 1)
                    if not (isinstance(g, int) and g == NG - 1):
                        pe.wait_ge(s_rres, 2 * g)
                        transpose_group(pe, NT + g + 1)
                    pv(g, H0 - 1)
            pe.wait_ge(s_rw, RET_W)
            pe.wait_ge(s_ysum, NT)
            transpose_group(pe, NT)
            run_groups(pe, ret)

            def mix(i, par, cur, prev):
                g = i - 1
                if prev:
                    pe.wait_ge(s_E, 2 * g + 2)
                    wait(pe, s_eT, g)
                    for t in range(GT):
                        ins = flip(pe, banks[:, 4, t * SLOTS:(t + 1) * SLOTS], E_[:, t * P:(t + 1) * P],
                                   ident[0:SLOTS, 0:SLOTS], t == 0)
                    ins.then_inc(s_tre, 1)
                    pe.wait_ge(s_cn, g + 1)
                    wait(pe, s_CT, g)
                    for t in range(GT):
                        ins = flip(pe, banks[0:SLOTS, 5, t * P:(t + 1) * P], Cl[:, t, :], ident[:, :], t == 0)
                    ins.then_inc(s_trc, 1)
                    pe.wait_ge(s_eT, g + 1)
                    wait(pe, s_yv, 2 * g)
                    for b in range(GB):
                        ins = two_halves(banks[0:SLOTS, 6, b * D:(b + 1) * D], lambda k: eT[:, 2 * b + k, :],
                                         lambda k: xw[1 - par][:, 2 * b + k, :])
                    ins.then_inc(s_y, 1)
                if cur:
                    pe.wait_ge(s_tokn, GT * (i + 1))
                    pe.wait_ge(s_hT, 2 * (Q_MIX + i))
                    for k in range(2):
                        for t in range(GT):
                            ins = pe.transpose(banks[0:HD, k, t * P:(t + 1) * P], tokn[:, t, k * HD:(k + 1) * HD],
                                               ident[:, :])
                        ins.then_inc(s_tr, 1)
                    pe.wait_ge(s_hT, 2 * (Q_MIX + i) + 2)
                    wait(pe, s_E, 2 * i)
                    two_halves(banks[0:SLOTS, 2, :], lambda k: slT[:, k, :], lambda k: hT[:, k, :]).then_inc(s_lt, 1)
                    wait(pe, s_sub, i)
                    for t in range(GT):
                        ins = two_halves(banks[:, 3, t * SLOTS:(t + 1) * SLOTS],
                                         lambda k: hT[:, k, t * P:(t + 1) * P], lambda k: slT[:, k, :])
                    ins.then_inc(s_lt, 1)
                if prev:
                    pe.wait_ge(s_yv, 2 * g + 2)
                    wait(pe, s_YT, 2 * g)
                    for b in range(GB):
                        for k in range(2):
                            c = (2 * b + k) * SLOTS
                            ins = flip(pe, banks[0:HD, 7, c:c + SLOTS], yv[:, b, k * HD:(k + 1) * HD],
                                       ident[0:SLOTS, 0:SLOTS], b + k == 0)
                    ins.then_inc(s_trY, 1)
            pe.wait_ge(s_rres, 2 * NG)
            run_mix(mix)(pe)

            def fc1(n, r, k):
                pe.wait_ge(s_w1[r], 16 * (k + 1))
                pe.wait_ge(s_ys, n + 1)
                wait(pe, s_hr, n - 1)
                for a, w in ((0, 512), (1, FF - 512)):
                    ins = two_halves(banks[0:B, 2 * (r % 2) + a, 0:w], lambda h: ys[r % 2][:, h, :],
                                     lambda h: ring1[r][:, h, 512 * a:512 * a + w])
                ins.then_inc(s_fc1, 1)

            def transpose_hidden(n, r):
                wait(pe, s_hb, n - 1)
                pe.wait_ge(s_hr, n + 1)
                for c in range(FC):
                    ins = flip(pe, banks[:, 4 + r % 2, c * B:(c + 1) * B], hraw[r % 2][:, c * P:(c + 1) * P],
                               ident[0:B, 0:B], c == 0)
                ins.then_inc(s_ht, 1)

            def fc2(n, r, k):
                pe.wait_ge(s_w2[r], 16 * (k + 1))
                wait(pe, s_y2c, n - 1)
                pe.wait_ge(s_gl, n + 1)
                for c in range(FC):
                    ins = pe.matmul(banks[0:B, 6 + r % 2, 0:D], gl[r % 2][:, c * B:(c + 1) * B], ring2[r][:, c, :],
                                    start=c == 0, stop=c == FC - 1)
                ins.then_inc(s_fc2, 1)

            def slot(n, r, k):
                if isinstance(n, int) and n == 0:
                    fc1(n, r, k)
                    return
                before = (r - 1) % RING
                transpose_hidden(n - 1, before)
                fc1(n, r, k)
                fc2(n - 1, before, k if r else k - 1)
            pe.wait_ge(s_YT, GB * NG)
            run_slots(pe, slot)
            transpose_hidden(SLOTS - 1, RING - 1)
            fc2(SLOTS - 1, RING - 1, SLOTS // RING - 1)

            def combine(g, cur, prev):
                if prev:
                    pe.wait_ge(s_y2, g)
                    pe.wait_ge(s_cp, g)
                    wait(pe, s_cres, 2 * (g - 1))
                    for t in range(GT):
                        ins = pe.matmul(banks[:, t // 2, (t % 2) * D:(t % 2 + 1) * D], CTs[:, t * P:(t + 1) * P],
                                        y2[:, t // 2, :], start=True, stop=True)
                    ins.then_inc(s_co, 1)
            run_combine(pe, combine)

            def task(n):
                wait(pe, s_je, n)

            def half_transpose(q, k, n):
                task(n)
                pe.wait_ge(s_xn, GT * (q + 1))
                for t in range(GT):
                    ins = pe.transpose(banks[0:HD, 6, t * P:(t + 1) * P], xn[:, t, k * HD:(k + 1) * HD], ident[:, :])
                ins.then_inc(s_jp, 1)

            def qk_in(i, n):
                task(n)
                m = ((i % 2) * QG + i // 2) * QT
                two_halves(banks[0:QT, 6, :], lambda k: wqk[:, k, m:m + QT], lambda k: hT[:, k, :]).then_inc(s_jp, 1)

            def v_in(t, n):
                task(n)
                two_halves(banks[:, 6, 0:D], lambda k: hT[:, k, t * P:(t + 1) * P],
                           lambda k: wv1[:, k, :]).then_inc(s_jp, 1)

            def ao_transpose(n_b, n):
                pe.wait_ge(s_ao, n_b + 1)
                task(n)
                for k in range(2):
                    for t in range(2):
                        ins = pe.transpose(banks[0:HD, 6, k * S + t * P:k * S + (t + 1) * P],
                                           ao[:, t, k * HD:(k + 1) * HD], ident[:, :])
                ins.then_inc(s_jp, 1)

            def project(n):
                task(n)
                for t in range(2):
                    ins = two_halves(banks[:, 6, t * D:(t + 1) * D], lambda k: aoT[:, k, t * P:(t + 1) * P],
                                     lambda k: wp1[:, k, :])
                ins.then_inc(s_jp, 1)

            def both_scores(u, par, first):
                b, c = u // QG, u % QG
                q, k = qkT[par][c], kd[u % 2]
                for m in range(2):
                    for h in range(HG):
                        if first:
                            ins = pe.matmul(banks[:, h, m * S:(m + 1) * S], q[:, b * S + m * P:b * S + (m + 1) * P],
                                            k[:, h, :], start=True, stop=True)
                        else:
                            ins = pe.matmul(banks[:, HG + h, m * S:(m + 1) * S], k[:, h, m * P:(m + 1) * P], qa,
                                            start=True, stop=True)
                ins.then_inc(s_p1 if first else s_p2, 1)

            def second(U, u, par, shifted):
                pe.wait_ge(s_je, shifted)
                wait(pe, s_ex, U)
                both_scores(u, par, False)

            def values_out(U, u, par):
                b, c = u // QG, u % QG
                pe.wait_ge(s_ex, U + 1)
                if c == 0:
                    wait(pe, s_ao, U // QG if isinstance(U, int) else (U - u) // QG + b)
                for n in range(2):
                    for h in range(HG):
                        o = (n * H1 + HG * c + h) * (HD1 + 1)
                        for m in range(2):
                            ins = pe.matmul(banks[:, 7, o:o + HD1 + 1], pT[u % 2][:, h, m, n * P:(n + 1) * P],
                                            va[par][:, 2 * b + m, HG * c + h, :], start=m == 0, stop=m == 1)
                ins.then_inc(s_av, 1)

            def run_job(g, base, job):
                kind, item, n = job
                n = base + n
                if kind == "qk":
                    qk_in(item, n)
                elif kind == "v":
                    v_in(item, n)
                elif kind == "aoT":
                    ao_transpose(GB * g - 1 if item else GB * g, n)
                elif kind == "proj":
                    project(n)
                elif kind == "hT":
                    half_transpose(Q_ATT + g + 2, item, n)

            def att(g, par, base, jobs):
                for u in range(UN):
                    U = UN * g + u
                    wait(pe, s_smx, U)
                    pe.wait_ge(s_kd, U + 1)
                    both_scores(u, par, True)
                    if (u, 0) in jobs:
                        run_job(g, base, jobs[u, 0])
                    if u >= 2 or not isinstance(g, int) or g:
                        values_out(U - 2, (u - 2) % UN, par if u >= 2 else 1 - par)
                    if (u, 1) in jobs:
                        run_job(g, base, jobs[u, 1])
                    if u >= 1 or not isinstance(g, int) or g:
                        second(U - 1, (u - 1) % UN, par if u >= 1 else 1 - par,
                               base + jobs[u - 1, 2][2] + 1 if u else base)
                    task(base + jobs[u, 2][2])
                    pe.wait_ge(s_neg, U + 1)
                    for m in range(2):
                        ins = pe.transpose(banks[0:QT, 6, m * P:(m + 1) * P], mt[:, m, :], ident[:, :])
                    ins.then_inc(s_jp, 1)
                for k in range(2):
                    if (UN - 1 + k, 3) in jobs:
                        run_job(g, base, jobs[UN - 1 + k, 3])
            pe.wait_ge(s_aw, AW)
            pe.wait_ge(s_cres, 2 * NG)
            for k in range(2):
                half_transpose(Q_ATT, k, k)
            for i in range(2 * QG):
                qk_in(i, 2 + i)
            for t in range(GT):
                v_in(t, 2 + 2 * QG + t)
            for k in range(2):
                half_transpose(Q_ATT + 1, k, JOBS_FIRST - 2 + k)
            run_attention(pe, att)
            last = UN * NG
            values_out(last - 2, UN - 2, 1)
            second(last - 1, UN - 1, 1, JOBS_TAIL)
            values_out(last - 1, UN - 1, 1)
            ao_transpose(GB * NG - 1, JOBS_TAIL)
            project(JOBS_TAIL + 1)
            def ffn(g, par, cur, prev):
                if cur:
                    pe.wait_ge(s_hT, 2 * (Q_ATT + g) + 2)
                    for c in range(FC):
                        wait(pe, s_gf, FC * g + c - 3)
                        two_halves(banks[:, 2 + (FC * par + c) % 4, :], lambda k: w1f[:, k, c * P:(c + 1) * P],
                                   lambda k: hT[:, k, :]).then_inc(s_f1, 1)
                    if not (isinstance(g, int) and g == NG - 1):
                        transpose_group(pe, Q_FFN + g + 1, Q_ATT + g + 1)
                if prev:
                    pe.wait_ge(s_gf, FC * g)
                    wait(pe, s_eres, 2 * (g - 1))
                    if isinstance(g, int) and g == 1:
                        pe.wait_ge(s_ag, FC * NATOMS)
                    if isinstance(g, int) and g == NG:
                        pe.wait_ge(s_fin, 2)
                    for t in range(GT):
                        for c in range(FC):
                            ins = pe.matmul(banks[:, 6 + t // 2, (t % 2) * D:(t % 2 + 1) * D],
                                            hid[1 - par][:, c, t * P:(t + 1) * P], w2f[:, c, :],
                                            start=c == 0, stop=c == FC - 1)
                    ins.then_inc(s_f2, 1)
                if isinstance(g, int) and g == 0:
                    class_in()
                if isinstance(g, int) and g == NG - 1:
                    class_candidates()

            def class_in():
                pe.wait_ge(s_cls, CLS_VAR + 1)
                for k in range(2):
                    ins = pe.transpose(banks[0:HD, 6, k * CT_N:(k + 1) * CT_N], cls_n[:, k * HD:(k + 1) * HD],
                                       ident[0:CT_N, 0:CT_N])
                ins.then_inc(s_clT, 1)
                pe.wait_ge(s_clTe, 1)
                pe.wait_ge(s_atom, ATOMS_W)
                for a in range(NATOMS):
                    which = ATOM_ROLE[a][1]
                    w = len(range(NCLS)[which]) * B
                    wait(pe, s_ag, FC * (a - 1))
                    for c in range(FC):
                        ins = two_halves(banks[:, 7 - a % 2, c * w:(c + 1) * w].rearrange("p (n b) -> p n b", b=B),
                                         lambda k: atom_in[a][:, k, c * P:(c + 1) * P],
                                         lambda k: classes(cls_T[:, k, :], which))
                    ins.then_inc(s_ain, 1)

            def class_candidates():
                pe.wait_ge(s_ag, FC * NATOMS)
                pe.wait_ge(s_eres, 2 * (NG - 1))
                for a in range(NATOMS):
                    role, which = ATOM_ROLE[a]
                    w = len(range(NCLS)[which]) * B
                    wait(pe, s_cand, 2 * (a - 1))
                    for k in range(2):
                        for c in range(FC):
                            ins = pe.matmul(banks[0:HD, 6 + a % 2, k * w:(k + 1) * w].rearrange("p (n b) -> p n b", b=B),
                                            atom_out[a][:, c, k * HD:(k + 1) * HD],
                                            classes(cls_h[1 - role][:, c, :], which), start=c == 0, stop=c == FC - 1)
                    ins.then_inc(s_aout, 1)
                pe.wait_ge(s_cand, 2 * NATOMS)
                for r in range(2):
                    for k in range(2):
                        ins = pe.transpose(banks[0:CT_N, 7, r * D + k * HD:r * D + (k + 1) * HD], cand[r][:, k, :],
                                           ident[0:HD, 0:HD])
                ins.then_inc(s_candT, 1)

            pe.wait_ge(s_je, JOBS_TAIL + 2)
            pe.wait_ge(s_fw, FW)
            transpose_group(pe, Q_FFN, Q_ATT)
            run_mix(ffn)(pe)


def halves(w):
    w = np.swapaxes(np.asarray(w), -1, -2)
    return np.ascontiguousarray(np.moveaxis(w.reshape(*w.shape[:-2], 2, HD, w.shape[-1]), -3, -2))


def columns(v):
    v = np.asarray(v)
    return np.moveaxis(v.reshape(*v.shape[:-1], -1, HD), -1, 0)


def rows(w, n):
    return w.reshape(-1, n, w.shape[1]).transpose(1, 0, 2)


def head_rows(w, extra=0):
    w = w.reshape(H1, HD1, -1)
    full = np.zeros((H1, HR, w.shape[2]), w.dtype)
    full[:, :HD1] = w
    full[:, HD1] = extra
    return full.reshape(H1 * HR, -1)


def retention_tables():
    f = np.float32
    half = DQK // 2
    t = np.arange(S, dtype=f)
    angles = t[:, None] * (f(1) / f(10000) ** (np.arange(half, dtype=f) / f(half)))[None, :]
    zeta = (np.arange(half, dtype=f) + f(half)) / f(DQK)
    tables = {}
    for name, sign in (("q", f(1)), ("k", f(-1))):
        decay = zeta[None, :] ** (sign * t[:, None] / f(512))
        cos, sin = (np.cos(angles) * decay).T, (np.sin(angles) * decay).T
        tables["cos_" + name] = np.concatenate([cos, cos])
        tables["sin_" + name] = np.concatenate([sin, -sin])
    gammas = np.array([1.0 - 2.0 ** (-(5 + h)) for h in range(H0)], f)
    diff = t[:, None] - t[None, :]
    m = gammas[:, None, None] ** np.maximum(diff, f(0))[None] * (diff >= 0).astype(f)[None]
    m = m / np.sqrt(np.maximum(m.sum(-1, keepdims=True, dtype=f), f(1e-6))) * f(DQK ** -0.5)
    keys = m.transpose(2, 0, 1)
    tables["mask"] = np.concatenate([keys[:P], keys[P:, :, P:]], axis=2).astype(f)
    tables["blk"] = np.kron(np.eye(P // DV, dtype=f), np.full((DV, DV), 1 / DV, f))
    return tables


def kernel(**a):
    import concourse.bacc as bacc
    from concourse.bass_utils import run_bass_kernel_spmd

    a = {k: np.asarray(v) for k, v in a.items()}
    t = {k[len("L0_tok_"):]: v for k, v in a.items() if k.startswith("L0_tok_")}
    data = {
        "tok_idx": a["x"].reshape(TILES, P).T,
        "emb": t["embedding"],
        "pos": t["pos_enc"].reshape(2, P, D).transpose(1, 0, 2),
        "win": halves(t["Win"]),
        "wzbc": halves(np.concatenate([t["Wd"], t["WB"], t["WC"]], axis=1)),
        "wout": halves(t["Wout"]),
        "vec": np.concatenate([columns(v) for v in (
            t["ln_g"], t["ln_b"], t["b_in"], *[t["convw"][:, :, k] for k in range(TAPS)], t["convb"],
            t["bd"], t["bB"], t["bC"])], axis=2),
        "bout": t["bout"],
    }
    r = {k[len("L0_attn_"):]: v for k, v in a.items() if k.startswith("L0_attn_")}
    data.update(rq=rows(r["Wq"], HD), rk=rows(r["Wk"], HD), rv=rows(r["Wv"], HD), rg=rows(r["Wg"], HD),
                ro=rows(r["Wo"], P), gnw=r["gn_weight"].reshape(NCH, P).T, gnb=r["gn_bias"].reshape(NCH, P).T,
                **retention_tables())
    f = {k[len("L0_ffn_"):]: v for k, v in a.items() if k.startswith("L0_ffn_")}
    data.update(slots=f["slots"], slot_scale=f["scale"][:, None], normw=f["norm_weight"], b2=f["fc2_bias"],
                b1=f["fc1_bias"].reshape(SLOTS, FC, P).transpose(2, 0, 1),
                fc1=f["fc1_weight"].reshape(SLOTS, 2, HD, FF).transpose(0, 2, 1, 3),
                fc2=f["fc2_weight"].reshape(SLOTS, FC, P, D).transpose(0, 2, 1, 3))
    m = {k[len("L1_attn_"):]: v for k, v in a.items() if k.startswith("L1_attn_")}
    wq, wk, wv = np.split(m["qkv_w"], 3)
    bq, bk, bv = np.split(m["qkv_b"], 3)
    data.update(wqk=halves(np.concatenate([head_rows(wq), head_rows(wk)])), wv1=halves(wv), wp1=halves(m["proj_w"]),
                qkb=np.concatenate([head_rows(bq), head_rows(bk, 1)]).reshape(2 * QG, QT).T, vb1=bv, pb1=m["proj_b"])
    e = {k[len("L1_ffn_"):]: v for k, v in a.items() if k.startswith("L1_ffn_")}
    data.update(w1f=halves(e["fc1_w"]), w2f=rows(e["fc2_w"].T, P), b1f=e["fc1_b"].reshape(FC, P).T, b2f=e["fc2_b"],
                atom_in=halves(e["atom_in_w"]),
                atom_out=e["atom_out_w"].transpose(0, 2, 1).reshape(NATOMS, FC, P, D).transpose(0, 2, 1, 3),
                atom_b1=e["atom_in_b"].reshape(NATOMS, FC, P).transpose(2, 0, 1),
                atom_b2=e["atom_out_b"].reshape(NATOMS, 2, HD).transpose(2, 0, 1),
                gates=np.repeat(e["gate_pair"], B, axis=0), balance=np.repeat(e["balance_bias"], B, axis=0))
    nc = bacc.Bacc("TRN2", target_bir_lowering=False, num_devices=1)
    data = {f"in_{k}": np.ascontiguousarray(v) for k, v in data.items()}
    A = {k[3:]: nc.dram_tensor(k, v.shape, mybir.dt.from_np(v.dtype), kind="ExternalInput").ap()
         for k, v in data.items()}
    out = nc.dram_tensor("out", (B * S, D), F32, kind="ExternalOutput").ap()
    slot_out = nc.dram_tensor("slot_out", (SLOTS, B, D), F32, kind="Internal").ap()
    build(nc, A, out, slot_out)
    r = run_bass_kernel_spmd(nc, [data], core_ids=[0])
    return r.results[0]["out"].reshape(B, S, D)
```

```python
from contextlib import ExitStack

import concourse.bass as bass
import numpy as np
from concourse import mybir

F32 = mybir.dt.float32
I32 = mybir.dt.int32
ALU = mybir.AluOpType
ACT = mybir.ActivationFunctionType
AX_X = mybir.AxisListType.X

P = 128
B, S, D = 16, 256, 192
V = 8000
L = 4
TAPS = 4
HD = D // 2
TILES = B * S // P
GT = 4
NG = TILES // GT
GB = GT * P // S
N = GT * P
EPS = 1e-5

NVEC = 26
V_G, V_BT, V_BU, V_BV, V_CW, V_CB, V_BD, V_BB, V_BC = 0, 2, 4, 6, 8, 16, 18, 20, 22
V_NBD = 24

H0, DQK, DV = 6, 128, 64
HV = H0 * DV
NCH = HV // P
MW = S + P

SLOTS, FF = 64, 768
FC = FF // P
RING = 4

H1, HD1 = 12, 16
HG = 3
QG = H1 // HG
UN = GB * QG
QT = HD
TH = QT // HD1
QC = H1 // TH

NCLS, NATOMS = 6, 5
CT_N = NCLS * B


def build(nc, A, out, slot_out):
    ctx = ExitStack()
    with ctx:
        def sb(name, shape, dt=F32):
            return ctx.enter_context(nc.sbuf_tensor(name, shape, dt))

        def sem(name):
            return ctx.enter_context(nc.semaphore(name))

        banks = ctx.enter_context(nc.psum_tensor("banks", [P, 8, 512], F32))
        X = sb("X", [P, TILES, D])
        tok_i = sb("tok_i", [P, TILES], I32)
        tok_neg = sb("tok_neg", [P, TILES], I32)
        tok_fix = sb("tok_fix", [P, TILES], I32)
        pos = sb("pos", [P, 2, D])
        ident = sb("ident", [P, P])
        own_rows = sb("rows_of_each_head", [QT, TH])
        mhalf = sb("mhalf", [P, 8])
        st = sb("st", [P, GT, 6])
        mv = sb("mv", [P, GT, 2])
        vare = sb("vare", [P, GT])
        rstd = sb("rstd", [P, GT])
        wait_slot = sb("wait_slot", [P, 1])
        xn = sb("xn", [P, GT, D])
        hT = sb("hT", [HD, 2, N])

        w_arena = sb("w_arena", [P, 12960])
        arena = sb("arena", [P, 16384])

        def carve(area, start):
            at = [start]

            def take(parts, *shape):
                n = int(np.prod(shape))
                v = area[0:parts, at[0]:at[0] + n]
                at[0] += n
                assert at[0] <= area.shape[1], (at[0], area.shape)
                names = "abcd"[:len(shape)]
                if len(shape) == 1:
                    return v
                return v.rearrange("p (" + " ".join(names) + ") -> p " + " ".join(names),
                                   **{n_: s_ for n_, s_ in zip(names[1:], shape[1:])})
            return take

        tw = carve(w_arena, 0)
        win = tw(HD, 2, 2 * D)
        wzbc = tw(HD, 2, 3 * D)
        wout = tw(HD, 2, D)
        vec = tw(HD, L, NVEC)
        boutb = tw(P, L, D)
        ta = carve(arena, 0)
        upad = [ta(HD, 2, GB, S + TAPS - 1) for _ in range(2)]
        uc = ta(HD, 2, N)
        sv = [ta(HD, 2, N) for _ in range(2)]
        dec = ta(HD, 2, N)
        Bs = ta(HD, 2, N)
        Cs = ta(HD, 2, N)
        inp = ta(HD, 2, N)
        hs = ta(HD, 2, N)
        hc = ta(HD, 2, N)
        hsum = ta(HD, N)
        ysum = ta(P, GT)

        rw = carve(w_arena, 3200)
        wq = rw(HD, 2, H0 * DQK)
        wk = rw(HD, 2, H0 * DQK)
        wv = rw(HD, 2, HV)
        wg = rw(HD, 2, HV)
        wo = rw(P, NCH, D)
        rot_cos = [rw(P, S) for _ in range(2)]
        rot_sin = [rw(P, S) for _ in range(2)]
        mask = rw(P, H0, MW)
        blk = rw(P, P)
        gnw = rw(P, NCH)
        gnb = rw(P, NCH)
        ra = carve(arena, 0)
        qk = [[ra(P, N) for _ in range(2)] for _ in range(2)]
        swp = [ra(P, N) for _ in range(2)]
        vt = ra(P, GT, HV)
        gate = ra(P, NCH, N)
        pm = [ra(P, GB, MW) for _ in range(2)]
        oT = ra(P, NCH, N)
        ng = ra(P, NCH, N)
        gst = ra(P, 2 * NCH, 6)
        gmv = ra(P, 2 * NCH, 2)
        gs = ra(P, 2 * NCH, 2)
        gmsq = ra(P, 2 * NCH)
        gvar = ra(P, 2 * NCH)
        grs = ra(P, 2 * NCH)
        gsc = ra(P, 2 * NCH)
        gmb = ra(P, 2 * NCH)
        gbi = ra(P, 2 * NCH)

        cw = carve(w_arena, 11856)
        slots = cw(SLOTS, D)
        slot_scale = cw(SLOTS, 1)
        normw = cw(P, D)
        b1 = cw(P, SLOTS, FC)
        b2 = cw(SLOTS, D)
        warm = sb("exponential_of_a_constant", [P, 1])
        slT = sb("slT", [HD, 2, SLOTS])
        sln2 = sb("sln2", [SLOTS, 2])
        slT_junk = sb("slots_squared", [SLOTS, D])
        ring1 = [sb(f"ring1_{r}", [HD, 2, FF]) for r in range(RING)]
        ring2 = [sb(f"ring2_{r}", [P, FC, D]) for r in range(RING)]
        ca = carve(arena, 0)
        CT = ca(SLOTS, B * S)
        YT = ca(HD, 2, SLOTS, B)
        xw = [ca(P, GT, D) for _ in range(2)]
        tokn = ca(P, GT, D)
        sq = ca(P, GT, D)
        n2 = ca(P, GT)
        n2c = ca(P, GT)
        rn = ca(P, GT)
        mx = ca(SLOTS, GB)
        nmx = ca(SLOTS, GB)
        E_ = ca(SLOTS, N)
        den = ca(SLOTS, GB)
        rden = ca(SLOTS, GB)
        cmx = ca(P, GT)
        Cl = ca(P, GT, SLOTS)
        csum = ca(P, GT)
        crec = ca(P, GT)
        eT = ca(P, GT, SLOTS)
        yv = ca(SLOTS, GB, D)
        ca = carve(arena, B * S + 2 * SLOTS * B)
        y2all = ca(SLOTS, B, D)
        ys = [ca(HD, 2, B) for _ in range(2)]
        hraw = [ca(B, FF) for _ in range(2)]
        fo = ca(B, RING, D)
        hb = [ca(P, FC * B) for _ in range(2)]
        gl = [ca(P, FC * B) for _ in range(2)]
        CTs = [ca(SLOTS, N) for _ in range(2)]
        y2 = [ca(SLOTS, GB, D) for _ in range(2)]

        aw = carve(w_arena, 0)
        wqk = aw(HD, 2, 2 * QC * QT)
        wv1 = aw(HD, 2, D)
        wp1 = aw(HD, 2, D)
        qkb = aw(QT, 2 * QC)
        vb1 = aw(P, D)
        pb1 = aw(P, D)
        assert 2 * 2 * QC * QT + 4 * D + 2 * QC + 2 * D <= 3200
        da = carve(arena, 0)
        qkT = [[da(QT, N) for _ in range(2 * QC)] for _ in range(2)]
        va = [da(P, GT, H1 // 2, 3, HD1) for _ in range(2)]
        pT = [da(P, HG, 2, S) for _ in range(2)]
        probs = [da(P, HG, 2, S) for _ in range(2)]
        smx = da(P, HG, 2)
        neg_max = da(P, HG * 2)
        kd = [da(QT, HG, S) for _ in range(2)]
        den1 = [da(P, HG * 2) for _ in range(2)]
        rden1 = [da(P, HG * 2) for _ in range(2)]
        aoT = da(HD, 2, S)

        fw = carve(w_arena, 3200)
        w1f = fw(HD, 2, FF)
        w2f = fw(P, FC, D)
        b1f = fw(P, FC)
        b2f = fw(P, D)
        atom_in = [ring1[a][:, :, :] for a in range(RING)] + [fw(HD, 2, FF)]
        atom_out = [ring2[a][:, :, :] for a in range(RING)] + [fw(P, FC, D)]
        atom_b1 = fw(P, NATOMS, FC)
        atom_b2 = fw(HD, NATOMS, 2)
        gates = fw(CT_N, 2, D)
        balance = fw(CT_N, 2)
        ea = carve(arena, 0)
        hid = [ea(P, FC, N) for _ in range(2)]
        cls_x = ea(CT_N, D)
        cls_n = ea(CT_N, D)
        cls_T = ea(HD, 2, CT_N)
        cls_h = [ea(P, FC, CT_N) for _ in range(2)]
        cand = [ea(HD, 2, CT_N) for _ in range(2)]
        gprod = ea(CT_N, 2, D)
        csq = ea(CT_N, 3, D)
        cst = ea(CT_N, 6)
        cmv = ea(CT_N, 2)
        cpw = ea(CT_N, 4)
        crs = ea(CT_N, 4)
        dots = ea(CT_N, 2)
        lg1 = ea(CT_N, 2)
        lmax = ea(CT_N, 1)
        prob = ea(CT_N, 2)
        psum_ = ea(CT_N, 2)
        pick = ea(CT_N, 2)
        fin = [ea(CT_N, D) for _ in range(2)]

        s_idx = sem("idx_loaded")
        s_pos = sem("pos_loaded")
        s_const = sem("constants_ready")
        s_fix = sem("token_ids_clamped")
        s_gath = [sem(f"rows_gathered_{g}") for g in range(NG)]
        s_emb = sem("embedding_ready")
        s_win = sem("win_loaded")
        s_wzbc = sem("wzbc_loaded")
        s_wout = sem("wout_loaded")
        s_vec = sem("vec_loaded")
        s_nbd = sem("negated_bd_ready")
        s_pads = sem("conv_pads_zero")
        s_stat = sem("ln_stat_step")
        s_var = sem("ln_var_ready")
        s_rstd = sem("ln_rstd_ready")
        s_xn = sem("ln_xn_ready")
        s_tr = sem("transposed_in_psum")
        s_hT = sem("hT_evacuated")
        s_uvp = sem("uv_in_psum")
        s_uve = sem("uv_evacuated")
        s_zp = sem("zbc_in_psum")
        s_ze = sem("zbc_evacuated")
        s_reset = sem("decay_reset")
        s_inp = sem("scan_input_ready")
        s_scan = sem("scan_done")
        s_hc = sem("hc_ready")
        s_conv = sem("conv_step")
        s_wop = sem("wo_in_psum")
        s_hsum = sem("hc_halves_added")
        s_yp = sem("y_products_transposed")
        s_ysum = sem("y_ready")
        s_bout = sem("bout_added")
        s_res = sem("residual_updated")
        s_rw = sem("retention_weights_loaded")
        s_qkp = sem("qk_in_psum")
        s_rot = sem("rotary_products_ready")
        s_radd = sem("rotary_sum_ready")
        s_vgp = sem("vg_in_psum")
        s_vge = sem("vg_evacuated")
        s_sp = sem("scores_in_psum")
        s_pm = sem("masked_scores_ready")
        s_pv = sem("pv_in_psum")
        s_oT = sem("oT_evacuated")
        s_gn = sem("groupnorm_step")
        s_gstat = sem("groupnorm_stats_in_psum")
        s_grs = sem("groupnorm_rstd_ready")
        s_ng = sem("gated_norm_ready")
        s_rop = sem("retention_out_in_psum")
        s_rres = sem("retention_residual_updated")
        s_sw = sem("slots_loaded")
        s_cw = sem("mixture_weights_loaded")
        s_sl = sem("slots_step")
        s_slq = sem("slots_square_sum")
        s_slr = sem("slots_rnorm")
        s_slp = sem("slots_transposed")
        s_slT = sem("slots_evacuated")
        s_xw = sem("weighted_norm_ready")
        s_n2 = sem("token_square_sums")
        s_n2c = sem("token_square_sums_bounded")
        s_rn = sem("token_rnorm_ready")
        s_tokn = sem("unit_tokens_ready")
        s_lt = sem("logits_in_psum")
        s_mx = sem("dispatch_max_ready")
        s_nmx = sem("dispatch_max_negated")
        s_warm = sem("exponential_table_in")
        s_E = sem("dispatch_exp_ready")
        s_cmx = sem("combine_max_ready")
        s_sub = sem("combine_shifted")
        s_cexp = sem("combine_exp_ready")
        s_csum = sem("combine_sum_ready")
        s_cn = sem("combine_ready")
        s_tre = sem("dispatch_transposed")
        s_trc = sem("combine_transposed")
        s_eT = sem("dispatch_evacuated")
        s_CT = sem("combine_evacuated")
        s_y = sem("slot_inputs_in_psum")
        s_rden = sem("dispatch_reciprocal_ready")
        s_yv = sem("slot_inputs_ready")
        s_trY = sem("slot_inputs_transposed")
        s_YT = sem("slot_inputs_evacuated")
        s_w1 = [sem(f"fc1_loaded_{r}") for r in range(RING)]
        s_w2 = [sem(f"fc2_loaded_{r}") for r in range(RING)]
        s_fc1 = sem("fc1_in_psum")
        s_ys = sem("slot_input_copied")
        s_hr = sem("fc1_evacuated")
        s_ht = sem("fc1_transposed")
        s_y2d = sem("slot_outputs_moved")
        s_y2a = sem("slot_outputs_back")
        s_hb = sem("fc1_biased")
        s_gl = sem("gelu_ready")
        s_fc2 = sem("fc2_in_psum")
        s_y2c = sem("fc2_evacuated")
        s_cp = sem("combine_operands_copied")
        s_y2 = sem("slot_outputs_ready")
        s_co = sem("mixture_out_in_psum")
        s_cres = sem("mixture_residual_updated")
        s_aw = sem("attention_weights_loaded")
        s_qb = sem("query_bias_scaled")
        s_da = sem("attention_buffers_set")
        s_jp = sem("shared_bank_filled")
        s_je = sem("shared_bank_emptied")
        s_kd = sem("keys_set_apart")
        s_p1 = sem("softmax_scores_in_psum")
        s_smx = sem("score_max_ready")
        s_neg = sem("score_max_negated")
        s_pt = sem("probabilities_transposed")
        s_pe = sem("transposed_probabilities_evacuated")
        s_ex = sem("probabilities_ready")
        s_av = sem("attention_values_in_psum")
        s_rd = sem("probability_sums_inverted")
        s_pn = sem("probabilities_normalised")
        s_ao = sem("attention_out_ready")
        s_pb = sem("projection_bias_added")
        s_fw = sem("ffn_weights_loaded")
        s_atom = sem("atom_weights_loaded")
        s_clsg = sem("class_rows_gathered")
        s_cls = sem("class_step")
        s_csq = sem("class_square_sums")
        s_crs = sem("class_powers_ready")
        s_cexp2 = sem("route_exp_ready")
        s_clT = sem("class_transposed")
        s_clTe = sem("class_transposed_evacuated")
        s_ain = sem("atom_hidden_in_psum")
        s_ag = sem("atom_gelu_ready")
        s_aout = sem("atom_out_in_psum")
        s_cand = sem("candidate_ready")
        s_candT = sem("candidates_transposed")
        s_fin = sem("class_rows_ready")
        s_f1 = sem("ffn_hidden_in_psum")
        s_gf = sem("ffn_gelu_ready")
        s_f2 = sem("ffn_out_in_psum")
        s_b2f = sem("ffn_bias_added")
        s_eres = sem("ffn_residual_updated")
        s_out = sem("output_written")

        def wait(eng, s_, v):
            if not isinstance(v, int) or v > 0:
                eng.wait_ge(s_, v)

        def ln_stats(dve, q, t0, mul=1.0, add=EPS):
            for i in range(GT):
                dve.bn_stats(st[:, i, :], X[:, t0 + i, :]).then_inc(s_stat, 1)
            dve.wait_ge(s_stat, q * (2 * GT) + GT)
            dve.memset(wait_slot[:, :], 0.0)
            for i in range(GT):
                dve.bn_aggr(mv[:, i, :], st[:, i, :]).then_inc(s_stat, 1)
            dve.wait_ge(s_stat, q * (2 * GT) + 2 * GT)
            dve.tensor_scalar(vare[:, :], mv[:, :, 1], mul, add, ALU.mult, ALU.add).then_inc(s_var, 1)

        def ln_rstd(pool, q):
            pool.wait_ge(s_var, q + 1)
            pool.tensor_tensor(rstd[:, :], vare[:, :], mhalf[:, 0:GT], ALU.pow).then_inc(s_rstd, 1)

        def ln_apply(dve, q, t0, free=None):
            dve.wait_ge(s_rstd, q + 1)
            dve.wait_ge(*(free or (s_tr, q * 2)))
            for i in range(GT):
                dve.tensor_scalar(xn[:, i, :], X[:, t0 + i, :], mv[:, i, 0:1], rstd[:, i:i + 1],
                                  ALU.subtract, ALU.mult).then_inc(s_xn, 1)

        def transpose_group(pe, q, tq=None):
            pe.wait_ge(s_xn, (q + 1) * GT)
            pe.wait_ge(s_hT, (q if tq is None else tq) * 2)
            for k in range(2):
                for i in range(GT):
                    ins = pe.transpose(banks[0:HD, k, i * P:(i + 1) * P], xn[:, i, k * HD:(k + 1) * HD], ident[:, :])
                ins.then_inc(s_tr, 1)

        def flip(pe, o, x, idn, first):
            if first:
                return pe.matmul(o, x, idn, start=True, stop=True)
            return pe.transpose(o, x, idn)

        block = ctx.enter_context(nc.Block())

        NT = L * NG

        def run_tok(eng, body):
            for j in range(-2, NG - 2):
                body(j, j % 2, {d for d in range(-2, 3) if 0 <= j - d < NT})
            with eng.Fori((NG - 2) // 2, (NT - 2) // 2) as i:
                for h in range(2):
                    body(2 * i + h, h, set(range(-2, 3)))
            for j in range(NT - 2, NT + 2):
                body(j, j % 2, {d for d in range(-2, 3) if 0 <= j - d < NT})

        RET_W = 13 * 16
        GN_VAR = 12 + 2 + 3
        GN_STEPS = GN_VAR + 3 + 6
        TOK_DONE = NT * GT

        def run_groups(eng, body):
            body(0, True, False)
            with eng.Fori(1, NG - 1) as g:
                body(g, True, True)
            body(NG - 1, True, True)
            body(NG, False, True)

        CW = 3 * 16
        Q_MIX = NT + NG
        AW = 6 * 16
        Q_ATT = Q_MIX + NG
        JOBS_FIRST = 2 + 2 * QC + GT + 2
        JOBS = 2 * QC + GT + 2 + 2

        CLS_VAR, CLS_NORMS = 3, 7
        FW = 10 * 16
        ATOMS_W = 8 * 16
        Q_FFN = Q_ATT + NG
        ATOM_ROLE = [(0, slice(2 * a, 2 * a + 2)) for a in range(3)] + [(1, slice(a, NCLS, 2)) for a in range(2)]

        def classes(x, which):
            return x.rearrange("p (n b) -> p n b", n=NCLS)[:, which, :]

        def group_jobs(first, more, more2):
            jobs = {}
            for u in range(UN):
                if more and u % 2 == 0:
                    jobs[u, 0] = ("qk", u // 2)
                if more and u in (1, 5):
                    jobs[u, 0] = ("v", u // 4 * 2)
                    jobs[u, 1] = ("v", u // 4 * 2 + 1)
                if u == 3 and not first:
                    jobs[u, 1] = ("proj", 1)
                if u == 6:
                    jobs[u, 1] = ("proj", 0)
                if more2 and u == UN - 1:
                    jobs[u, 0] = ("hT", 0)
                    jobs[u, 1] = ("hT", 1)
            return {k: (*v, n) for n, (k, v) in enumerate(jobs.items())}

        def turn(n):
            return 6 + n % 2

        def run_attention(eng, body):
            def base(g):
                return JOBS_FIRST + JOBS * g - 1
            body(0, 0, JOBS_FIRST, group_jobs(True, True, True))
            with eng.Fori(0, (NG - 4) // 2) as k:
                body(2 * k + 1, 1, base(2 * k + 1), group_jobs(False, True, True))
                body(2 * k + 2, 0, base(2 * k + 2), group_jobs(False, True, True))
            body(NG - 3, 1, base(NG - 3), group_jobs(False, True, True))
            body(NG - 2, 0, base(NG - 2), group_jobs(False, True, False))
            body(NG - 1, 1, base(NG - 1) - 2, group_jobs(False, False, False))

        JOBS_TAIL = JOBS_FIRST + JOBS * (NG - 1) - 1 - 2 + 2

        def run_mix(body):
            def run(eng):
                body(0, 0, True, False)
                body(1, 1, True, True)
                with eng.Fori(1, (NG - 2) // 2) as k:
                    body(2 * k, 0, True, True)
                    body(2 * k + 1, 1, True, True)
                body(NG - 2, 0, True, True)
                body(NG - 1, 1, True, True)
                body(NG, 0, False, True)
            return run

        def more(i):
            return not isinstance(i, int) or i < NG - 1

        def run_slots(eng, body):
            for r in range(RING):
                body(r, r, 0)
            with eng.Fori(1, SLOTS // RING) as k:
                for r in range(RING):
                    body(RING * k + r, r, k)

        def run_combine(eng, body):
            body(0, 0, True, False)
            body(1, 1, True, True)
            with eng.Fori(1, NG // 2) as k:
                body(2 * k, 0, True, True)
                body(2 * k + 1, 1, True, True)
            body(NG, 0, False, True)

        @block.sync
        def _(sp):
            sp.dma_start(tok_i[:, :], A["tok_idx"]).then_inc(s_idx, 16)
            for dst, name in ((slots, "slots"), (slot_scale, "slot_scale")):
                sp.dma_start(dst, A[name]).then_inc(s_sw, 16)
            sp.dma_start(vec[:, :, 0:V_NBD], A["vec"]).then_inc(s_vec, 16)
            sp.dma_start(win, A["win"][0]).then_inc(s_win, 16)
            sp.dma_start(pos[:, :, :], A["pos"]).then_inc(s_pos, 16)
            sp.dma_start(boutb, A["bout"].rearrange("(o l) d -> o l d", o=1).broadcast_to((P, L, D))).then_inc(s_vec, 16)
            sp.dma_start(wzbc, A["wzbc"][0]).then_inc(s_wzbc, 16)
            sp.dma_start(wout, A["wout"][0]).then_inc(s_wout, 16)
            for dst, name in ((wq, "rq"), (wk, "rk"), (wv, "rv"), (wg, "rg"), (wo, "ro"), (rot_cos[0], "cos_q"),
                              (rot_sin[0], "sin_q"), (rot_cos[1], "cos_k"), (rot_sin[1], "sin_k"), (mask, "mask"),
                              (blk, "blk"), (gnw, "gnw"), (gnb, "gnb")):
                sp.dma_start(dst, A[name]).then_inc(s_rw, 16)
            for dst, name in ((b1, "b1"), (b2, "b2")):
                sp.dma_start(dst, A[name]).then_inc(s_cw, 16)
            sp.dma_start(normw, A["normw"].rearrange("(o d) -> o d", o=1).broadcast_to((P, D))).then_inc(s_cw, 16)
            for r in range(RING):
                sp.dma_start(ring1[r][:, :, :], A["fc1"][r]).then_inc(s_w1[r], 16)
                sp.dma_start(ring2[r][:, :, :], A["fc2"][r]).then_inc(s_w2[r], 16)
            for l in range(1, L):
                sp.wait_ge(s_uvp, l * NG * 4)
                sp.dma_start(win, A["win"][l]).then_inc(s_win, 16)
                sp.wait_ge(s_zp, l * NG * 6)
                sp.dma_start(wzbc, A["wzbc"][l]).then_inc(s_wzbc, 16)
                sp.wait_ge(s_wop, l * NG)
                sp.dma_start(wout, A["wout"][l]).then_inc(s_wout, 16)
            for dst, name in ((wqk, "wqk"), (wv1, "wv1"), (wp1, "wp1"), (qkb, "qkb")):
                sp.wait_ge(s_res, TOK_DONE)
                sp.dma_start(dst, A[name]).then_inc(s_aw, 16)
            for dst, name in ((vb1, "vb1"), (pb1, "pb1")):
                sp.dma_start(dst, A[name].rearrange("(o d) -> o d", o=1).broadcast_to((P, D))).then_inc(s_aw, 16)
            sp.wait_ge(s_rres, 2 * NG)
            for dst, name in ((w1f, "w1f"), (w2f, "w2f"), (b1f, "b1f"), (atom_b1, "atom_b1"), (atom_b2, "atom_b2"),
                              (gates, "gates"), (balance, "balance")):
                sp.dma_start(dst, A[name]).then_inc(s_fw, 16)
            sp.dma_start(b2f, A["b2f"].rearrange("(o d) -> o d", o=1).broadcast_to((P, D))).then_inc(s_fw, 16)
            sp.dma_start(atom_in[RING], A["atom_in"][RING]).then_inc(s_fw, 16)
            sp.dma_start(atom_out[RING], A["atom_out"][RING]).then_inc(s_fw, 16)
            with sp.Fori(1, SLOTS // RING) as k:
                for r in range(RING):
                    n = RING * k + r
                    sp.wait_ge(s_fc1, n - RING + 1)
                    sp.dma_start(ring1[r][:, :, :], A["fc1"][bass.ds(n, 1)].rearrange("o p k f -> p (o k) f")
                                 ).then_inc(s_w1[r], 16)
                    sp.wait_ge(s_fc2, n - RING + 1)
                    sp.dma_start(ring2[r][:, :, :], A["fc2"][bass.ds(n, 1)].rearrange("o p c d -> p (o c) d")
                                 ).then_inc(s_w2[r], 16)
            for lo, hi in ((0, SLOTS - RING), (SLOTS - RING, SLOTS)):
                sp.wait_ge(s_y2d, hi // RING * 16)
                sp.dma_start(y2all[lo:hi], slot_out[lo:hi]).then_inc(s_y2a, 16)
            for a in range(RING):
                sp.wait_ge(s_fc2, SLOTS)
                sp.dma_start(atom_in[a], A["atom_in"][a]).then_inc(s_atom, 16)
                sp.dma_start(atom_out[a], A["atom_out"][a]).then_inc(s_atom, 16)
            sp.wait_ge(s_je, JOBS_TAIL + 1)
            for n in range(NCLS):
                sp.dma_start(cls_x[n * B:(n + 1) * B, :], X[n:n + 1, ::2, :]).then_inc(s_clsg, 16)
            rows_out = out.rearrange("(t p) d -> p t d", p=P)
            with sp.Fori(0, NG) as g:
                sp.wait_ge(s_eres, 2 * g + 2)
                for t in range(GT):
                    lo = NCLS if t % 2 == 0 else 0
                    sp.dma_start(rows_out[lo:, bass.ds(g * GT + t, 1), :],
                                 X[lo:, bass.ds(g * GT + t, 1), :]).then_inc(s_out, 16)
            sp.wait_ge(s_fin, 2)
            for n in range(NCLS):
                sp.dma_start(out.rearrange("(b t) d -> t b d", b=B)[n], fin[1][n * B:(n + 1) * B, :]).then_inc(s_out, 16)
            sp.wait_ge(s_out, 16 * (TILES + NCLS))

        @block.gpsimd
        def _(pool):
            pool.memset(ident[:, :], 0.0).then_inc(s_const, 1)
            pool.memset(mhalf[:, :], -0.5).then_inc(s_const, 1)
            pool.memset(own_rows[:, :], 1.0).then_inc(s_const, 1)
            pool.wait_ge(s_const, 3)
            pool.affine_select(out=own_rows[:, :], in_=own_rows[:, :], compare_op=ALU.is_ge, fill=0.0, base=0,
                               pattern=[[-HD1, TH]], channel_multiplier=1).then_inc(s_const, 1)
            pool.wait_ge(s_const, 4)
            pool.affine_select(out=own_rows[:, :], in_=own_rows[:, :], compare_op=ALU.is_ge, fill=0.0, base=HD1 - 1,
                               pattern=[[HD1, TH]], channel_multiplier=-1).then_inc(s_const, 1)
            pool.wait_ge(s_const, 5)
            pool.affine_select(out=ident[:, :], in_=ident[:, :], compare_op=ALU.not_equal, fill=1.0, base=0,
                               pattern=[[-1, P]], channel_multiplier=1).then_inc(s_const, 1)
            pool.wait_ge(s_fix, 4)
            def gather(g):
                for t in range(g * GT, (g + 1) * GT):
                    pool.indirect_dma_start(X[:, t, :], None, A["emb"],
                                            bass.IndirectOffsetOnAxis(ap=tok_fix[:, t:t + 1], axis=0)
                                            ).then_inc(s_gath[g], 16)
            gather(0)
            pool.wait_ge(s_sl, 1)
            pool.tensor_tensor(sln2[:, 1:2], sln2[:, 0:1], mhalf[0:SLOTS, 0:1], ALU.pow).then_inc(s_slr, 1)
            gather(1)

            def step(j, par, on):
                if 2 in on:
                    pool.wait_ge(s_hc, j - 1)
                    wait(pool, s_yp, j - 2)
                    pool.tensor_tensor(hsum, hc[:, 0, :], hc[:, 1, :], ALU.add).then_inc(s_hsum, 1)
                if isinstance(j, int) and j + 4 < NG:
                    gather(j + 4)
                if -2 in on:
                    ln_rstd(pool, j + 2)
                    q = j + 2
                    pool.wait_ge(s_xn, (q + 1) * GT)
                    if isinstance(q, int) and q == 0:
                        pool.wait_ge(s_vec, 32)
                    xg = X[:, bass.ds(q % NG * GT, GT), :]
                    bb = boutb[:, bass.ds(q // NG, 1), :].broadcast_to((P, GT, D))
                    pool.tensor_tensor(xg, xg, bb, ALU.add).then_inc(s_bout, 1)
                if isinstance(j, int) and j + 2 == NT:
                    ln_rstd(pool, NT)
            run_tok(pool, step)

            def ret(g, cur, prev):
                if cur:
                    for h in range(H0):
                        for w in range(2):
                            n = 12 * g + 2 * h + w
                            pool.wait_ge(s_rot, 3 * n + 3)
                            pool.tensor_tensor(qk[w][h % 2], qk[w][h % 2], swp[w], ALU.add).then_inc(s_radd, 1)
                        if h == 1 and prev:
                            pool.wait_ge(s_gn, GN_STEPS * (g - 1) + GN_VAR)
                            pool.tensor_tensor(grs, gvar, mhalf[:, 0:2 * NCH], ALU.pow).then_inc(s_grs, 1)
                        if h == 4 and not (isinstance(g, int) and g == NG - 1):
                            ln_rstd(pool, NT + g + 1)
                else:
                    pool.wait_ge(s_gn, GN_STEPS * (g - 1) + GN_VAR)
                    pool.tensor_tensor(grs, gvar, mhalf[:, 0:2 * NCH], ALU.pow).then_inc(s_grs, 1)
            run_groups(pool, ret)

            def mix(i, par, cur, prev):
                if cur:
                    ln_rstd(pool, Q_MIX + i)
                    pool.wait_ge(s_n2c, i + 1)
                    pool.tensor_tensor(rn, n2c, mhalf[:, 0:GT], ALU.pow).then_inc(s_rn, 1)
            run_mix(mix)(pool)

            def add_bias(g, q0, bias, done):
                pool.wait_ge(s_xn, GT * (q0 + g + 1))
                xg = X[:, bass.ds(g * GT, GT), :]
                pool.tensor_tensor(xg, xg, bias.rearrange("p (o d) -> p o d", o=1).broadcast_to((P, GT, D)),
                                   ALU.add).then_inc(done, 1)

            def separate_keys(U, u, par, keys_out):
                b, c = u // QG, u % QG
                first = c * HG % TH
                pool.wait_ge(s_je, keys_out)
                wait(pool, s_p1, HG * (U - 1))
                k = qkT[par][QC + c * HG // TH][:, b * S:(b + 1) * S]
                pool.tensor_tensor(kd[u % 2], k.rearrange("p (o s) -> p o s", o=1).broadcast_to((QT, HG, S)),
                                   own_rows[:, first:first + HG].rearrange("p (h o) -> p h o", o=1)
                                   .broadcast_to((QT, HG, S)), ALU.mult).then_inc(s_kd, 1)

            def att(g, par, base, jobs):
                for u in range(UN):
                    U = UN * g + u
                    if u + 1 < UN:
                        separate_keys(U + 1, u + 1, par, base)
                    elif (UN - 2, 0) in jobs:
                        separate_keys(U + 1, 0, 1 - par, base + jobs[UN - 2, 0][2] + 1)
                    pool.wait_ge(s_rd, U + 1)
                    pr = probs[u % 2].rearrange("p h n s -> p (h n) s")
                    pool.tensor_tensor(pr, pr, rden1[u % 2].rearrange("p (a o) -> p a o", o=1).broadcast_to((P, HG * 2, S)),
                                       ALU.mult).then_inc(s_pn, 1)
                    if u == 2 and (UN - 1, 1) in jobs:
                        ln_rstd(pool, Q_ATT + g + 2)
                    if u == 4 and (UN - 1, 1) in jobs:
                        add_bias(g + 2, Q_ATT, pb1, s_pb)
            pool.wait_ge(s_aw, AW)
            for g in range(2):
                ln_rstd(pool, Q_ATT + g)
                add_bias(g, Q_ATT, pb1, s_pb)
            separate_keys(0, 0, 0, 2 + 2 * QC)
            run_attention(pool, att)

            for g in range(2):
                ln_rstd(pool, Q_FFN + g)
                if g == 0:
                    pool.wait_ge(s_fw, FW)
                    pool.wait_ge(s_clsg, 16 * NCLS)
                add_bias(g, Q_FFN, b2f, s_b2f)
            for n, sl in enumerate((slice(0, 1), slice(1, 4))):
                pool.wait_ge(s_cls, (CLS_VAR, CLS_NORMS)[n])
                pool.tensor_tensor(crs[:, sl], cpw[:, sl], mhalf[0:CT_N, sl], ALU.pow).then_inc(s_crs, 1)
            with pool.Fori(2, NG) as g:
                ln_rstd(pool, Q_FFN + g)
                add_bias(g, Q_FFN, b2f, s_b2f)

        @block.vector
        def _(dve):
            dve.wait_ge(s_idx, 16)
            dve.tensor_scalar(tok_neg[:, :], tok_i[:, :], 0.0, float(V), ALU.is_lt, ALU.mult).then_inc(s_fix, 1)
            dve.wait_ge(s_fix, 1)
            dve.tensor_tensor(tok_fix[:, :], tok_neg[:, :], tok_i[:, :], ALU.add).then_inc(s_fix, 1)
            dve.wait_ge(s_fix, 2)
            dve.tensor_scalar(tok_neg[:, :], tok_fix[:, :], float(V - 1), 0.0, ALU.min, ALU.max).then_inc(s_fix, 1)
            dve.wait_ge(s_fix, 3)
            dve.tensor_copy(tok_fix[:, :], tok_neg[:, :]).then_inc(s_fix, 1)
            for u in upad:
                dve.memset(u[:, :, :, 0:TAPS - 1], 0.0).then_inc(s_pads, 1)
            dve.wait_ge(s_vec, 32)
            dve.tensor_scalar(vec[:, :, V_NBD:V_NBD + 2], vec[:, :, V_BD:V_BD + 2], -1.0, None,
                              ALU.mult).then_inc(s_nbd, 1)
            dve.wait_ge(s_sw, 32)
            dve.wait_ge(s_slq, 1)
            dve.tensor_scalar(sln2[:, 0:1], sln2[:, 0:1], 1e-10, None, ALU.max).then_inc(s_sl, 1)
            dve.wait_ge(s_slr, 1)
            dve.tensor_scalar(slots, slots, sln2[:, 1:2], slot_scale, ALU.mult, ALU.mult).then_inc(s_sl, 1)
            dve.wait_ge(s_pos, 16)

            def scan_part(j):
                dve.wait_ge(s_ze, 6 * j + 2)
                d4 = dec.rearrange("p k (b t) -> p (k b) t", b=GB)
                dve.memset(d4[:, :, 0:1], 0.0).then_inc(s_reset, 1)
                dve.wait_ge(s_ze, 6 * j + 4)
                dve.tensor_tensor(inp, Bs, uc, ALU.mult).then_inc(s_inp, 1)
                dve.wait_ge(s_reset, j + 1)
                dve.wait_ge(s_inp, j + 1)
                dve.tensor_tensor_scan(hs.rearrange("p k n -> p (k n)"), dec.rearrange("p k n -> p (k n)"),
                                       inp.rearrange("p k n -> p (k n)"), 0.0, ALU.mult, ALU.add).then_inc(s_scan, 1)
                dve.wait_ge(s_scan, j + 1)
                dve.wait_ge(s_ze, 6 * j + 6)
                dve.wait_ge(s_hsum, j)
                dve.tensor_tensor(hc, hs, Cs, ALU.mult).then_inc(s_hc, 1)

            def conv_part(j, par):
                lay = j // NG

                def col(c):
                    return vec[:, bass.ds(lay, 1), c:c + 1].rearrange("p a b -> p (a b)")
                dve.wait_ge(s_uve, 4 * j + 2)
                dve.wait_ge(s_zp, 6 * j)
                ucv = [uc[:, k, :].rearrange("p (b t) -> p b t", b=GB) for k in range(2)]
                u = upad[par]
                for k in range(2):
                    dve.tensor_scalar(ucv[k], u[:, k, :, 3:3 + S], col(V_CW + 2 * 3 + k), col(V_CB + k),
                                      ALU.mult, ALU.add).then_inc(s_conv, 1)
                for n, tap in enumerate((2, 1, 0)):
                    for k in range(2):
                        dve.wait_ge(s_conv, 8 * j + 2 * n + k + 1)
                        dve.scalar_tensor_tensor(ucv[k], u[:, k, :, tap:tap + S], col(V_CW + 2 * tap + k), ucv[k],
                                                 ALU.mult, ALU.add).then_inc(s_conv, 1)

            def residual_part(j):
                dve.wait_ge(s_yp, j + 1)
                dve.reduce_sum(ysum, banks[:, 0, 0:GT * HD].rearrange("p (t d) -> p t d", t=GT), AX_X).then_inc(s_ysum, 1)
                dve.wait_ge(s_ysum, j + 1)
                dve.wait_ge(s_wop, j + 1)
                dve.wait_ge(s_bout, j + 1)
                for i in range(GT):
                    xt = X[:, bass.ds(j % NG * GT + i, 1), :].rearrange("p a d -> p (a d)")
                    dve.scalar_tensor_tensor(xt, banks[:, 2 + i // 2, (i % 2) * D:(i % 2 + 1) * D],
                                             ysum[:, i:i + 1], xt,
                                             ALU.mult, ALU.add).then_inc(s_res, 1)

            def step(j, par, on):
                if 2 in on:
                    scan_part(j - 2)
                if 1 in on:
                    conv_part(j - 1, 1 - par)
                if 2 in on:
                    residual_part(j - 2)
                if -2 in on:
                    q = j + 2
                    if isinstance(q, int) and q < NG:
                        dve.wait_ge(s_gath[q], 16 * GT)
                        for b in range(GB):
                            xb = X[:, q * GT + 2 * b:q * GT + 2 * b + 2, :]
                            dve.tensor_tensor(xb, xb, pos[:, :, :], ALU.add).then_inc(s_emb, 1)
                        dve.wait_ge(s_emb, (q + 1) * GB)
                    else:
                        dve.wait_ge(s_res, (q - NG + 1) * GT)
                    ln_stats(dve, q, q % NG * GT)
                    ln_apply(dve, q, q % NG * GT)
                if isinstance(j, int) and j + 2 == NT:
                    dve.wait_ge(s_res, (NT - NG + 1) * GT)
                    ln_stats(dve, NT, 0)
                    ln_apply(dve, NT, 0)
            run_tok(dve, step)

            def rotary(g, h, w):
                n = 12 * g + 2 * h + w
                head = H0 * g + h
                dst = qk[w][h % 2]
                ps = banks[:, 2 + w, :]
                dve.wait_ge(s_qkp, n + 1)
                if not isinstance(g, int) or head >= 2:
                    dve.wait_ge(s_sp, 2 * (head - 1))
                if not isinstance(g, int) or n >= 2:
                    dve.wait_ge(s_radd, n - 1)

                def v(x):
                    return x.rearrange("p (b t) -> p b t", b=GB)

                def tab(x):
                    return x.rearrange("p (o t) -> p o t", o=1).broadcast_to((x.shape[0], GB, S))
                dve.tensor_tensor(v(dst), v(ps), tab(rot_cos[w]), ALU.mult).then_inc(s_rot, 1)
                for lo, hi in ((0, 64), (64, 0)):
                    dve.tensor_tensor(v(swp[w][lo:lo + 64, :]), v(ps[hi:hi + 64, :]), tab(rot_sin[w][hi:hi + 64, :]),
                                      ALU.mult).then_inc(s_rot, 1)

            def apply_mask(g, h):
                head = H0 * g + h
                for b in range(GB):
                    dve.wait_ge(s_sp, 2 * head + b + 1)
                    if not isinstance(g, int) or head >= 2:
                        dve.wait_ge(s_pv, head - 1)
                    dve.tensor_tensor(pm[h % 2][:, b, :], banks[:, 6 + b, 0:MW], mask[:, h, :],
                                      ALU.mult).then_inc(s_pm, 1)

            def gn_stats(g):
                base = GN_STEPS * g
                for c in range(NCH):
                    for b in range(GB):
                        dve.wait_ge(s_oT, NCH * g + c + 1)
                        dve.bn_stats(gst[:, 2 * c + b, :], oT[:, c, b * S:(b + 1) * S]).then_inc(s_gn, 1)
                dve.wait_ge(s_gn, base + 6)
                dve.memset(wait_slot[:, :], 0.0)
                for n in range(2 * NCH):
                    dve.bn_aggr(gmv[:, n, :], gst[:, n, :]).then_inc(s_gn, 1)
                dve.wait_ge(s_gn, base + 12)
                dve.tensor_tensor(gmsq, gmv[:, :, 0], gmv[:, :, 0], ALU.mult).then_inc(s_gn, 1)
                dve.wait_ge(s_gn, base + 13)
                dve.tensor_tensor(gmv[:, :, 1], gmv[:, :, 1], gmsq, ALU.add).then_inc(s_gn, 1)

            def gn_var(g):
                base = GN_STEPS * g + 14
                dve.wait_ge(s_gstat, g + 1)
                dve.tensor_copy(gs, banks[:, 0, 400:400 + 4 * NCH].rearrange("p (n s) -> p n s", s=2)).then_inc(s_gn, 1)
                dve.wait_ge(s_gn, base + 1)
                dve.tensor_tensor(gmsq, gs[:, :, 0], gs[:, :, 0], ALU.mult).then_inc(s_gn, 1)
                dve.wait_ge(s_gn, base + 2)
                dve.scalar_tensor_tensor(gvar, gs[:, :, 1], EPS, gmsq, ALU.add, ALU.subtract).then_inc(s_gn, 1)

            def gn_apply(g):
                base = GN_STEPS * g + GN_VAR

                def pair(x):
                    return x.rearrange("p (c b) -> p c b", b=GB)

                def per_c(x):
                    return x.rearrange("p (c o) -> p c o", o=1).broadcast_to((P, NCH, GB))
                dve.wait_ge(s_grs, g + 1)
                dve.tensor_tensor(pair(gsc), pair(grs), per_c(gnw), ALU.mult).then_inc(s_gn, 1)
                dve.wait_ge(s_gn, base + 1)
                dve.tensor_tensor(gmb, gs[:, :, 0], gsc, ALU.mult).then_inc(s_gn, 1)
                dve.wait_ge(s_gn, base + 2)
                dve.tensor_tensor(pair(gbi), per_c(gnb), pair(gmb), ALU.subtract).then_inc(s_gn, 1)
                dve.wait_ge(s_gn, base + 3)
                for c in range(NCH):
                    for b in range(GB):
                        n = 2 * c + b
                        dve.tensor_scalar(ng[:, c, b * S:(b + 1) * S], oT[:, c, b * S:(b + 1) * S], gsc[:, n:n + 1],
                                          gbi[:, n:n + 1], ALU.mult, ALU.add).then_inc(s_gn, 1)
                dve.wait_ge(s_gn, base + 9)
                dve.wait_ge(s_vge, 7 * g + 7)
                dve.tensor_tensor(ng, ng, gate, ALU.mult).then_inc(s_ng, 1)

            def ret_residual(g):
                dve.wait_ge(s_rop, g + 1)
                for i in range(2):
                    xt = X[:, bass.ds(g * GT + 2 * i, 2), :]
                    dve.tensor_tensor(xt, banks[:, i, 0:2 * D].rearrange("p (t d) -> p t d", t=2), xt,
                                      ALU.add).then_inc(s_rres, 1)

            def ret(g, cur, prev):
                for h in range(H0):
                    if cur:
                        rotary(g, h, 0)
                        rotary(g, h, 1)
                        if h >= 1:
                            apply_mask(g, h - 1)
                    if prev and h == 0:
                        gn_stats(g - 1)
                    if prev and h == 1:
                        gn_var(g - 1)
                    if prev and h == 2:
                        gn_apply(g - 1)
                    if cur and h == 4 and not (isinstance(g, int) and g == NG - 1):
                        ln_stats(dve, NT + g + 1, (g + 1) * GT)
                        ln_apply(dve, NT + g + 1, (g + 1) * GT)
                if not cur:
                    dve.wait_ge(s_rres, 2)
                    ln_stats(dve, Q_MIX, 0, 1.0 + EPS, EPS * EPS)
                if prev:
                    ret_residual(g - 1)
                if cur:
                    apply_mask(g, H0 - 1)
            dve.wait_ge(s_res, TOK_DONE)
            dve.wait_ge(s_rw, RET_W)
            run_groups(dve, ret)

            def shift_logits(g):
                dve.wait_ge(s_lt, 2 * g + 1)
                dve.reduce_max(mx, banks[0:SLOTS, 2, :].rearrange("p (b t) -> p b t", b=GB), AX_X).then_inc(s_mx, 1)
                dve.wait_ge(s_mx, g + 1)
                wait(dve, s_E, 2 * g)
                dve.tensor_scalar(nmx, mx, -1.0, None, ALU.mult).then_inc(s_nmx, 1)
                dve.wait_ge(s_lt, 2 * g + 2)
                lg = banks[:, 3, 0:GT * SLOTS].rearrange("p (t s) -> p t s", t=GT)
                dve.reduce_max(cmx, lg, AX_X).then_inc(s_cmx, 1)
                dve.wait_ge(s_cmx, g + 1)
                wait(dve, s_trc, g)
                dve.tensor_tensor(Cl, lg, per_tile(cmx, SLOTS), ALU.subtract).then_inc(s_sub, 1)

            def per_tile(x, n):
                return x.rearrange("p (t o) -> p t o", o=1).broadcast_to((P, GT, n))

            def mix_stats(i):
                ln_stats(dve, Q_MIX + i, i * GT, 1.0 + EPS, EPS * EPS)

            def weighted_norm(i, par):
                q = Q_MIX + i
                dve.wait_ge(s_rstd, q + 1)
                wait(dve, s_y, i - 1)
                for t in range(GT):
                    xt = X[:, bass.ds(i * GT + t, 1), :].rearrange("p a d -> p (a d)")
                    dve.tensor_scalar(xw[par][:, t, :], xt, mv[:, t, 0:1], rstd[:, t:t + 1],
                                      ALU.subtract, ALU.mult).then_inc(s_xn, 1)
                dve.wait_ge(s_xn, GT * (q + 1))
                dve.tensor_tensor(xw[par], xw[par], normw.rearrange("p (o d) -> p o d", o=1).broadcast_to((P, GT, D)),
                                  ALU.mult).then_inc(s_xw, 1)

            def combine_weights(g):
                dve.wait_ge(s_cexp, g + 1)
                dve.reduce_sum(csum, Cl, AX_X).then_inc(s_csum, 1)
                dve.wait_ge(s_csum, 2 * g + 1)
                dve.reciprocal(crec, csum).then_inc(s_csum, 1)
                dve.wait_ge(s_csum, 2 * g + 2)
                dve.tensor_tensor(Cl, Cl, per_tile(crec, SLOTS), ALU.mult).then_inc(s_cn, 1)

            def clamp_squares(i):
                dve.wait_ge(s_n2, GT * (i + 1))
                dve.tensor_scalar(n2c, n2, 1e-10, None, ALU.max).then_inc(s_n2c, 1)

            def unit_tokens(i, par):
                dve.wait_ge(s_rn, i + 1)
                dve.wait_ge(s_tr, 2 * (Q_MIX + i))
                for t in range(GT):
                    dve.tensor_scalar(tokn[:, t, :], xw[par][:, t, :], rn[:, t:t + 1], None, ALU.mult).then_inc(s_tokn, 1)

            def slot_inputs(g):
                dve.wait_ge(s_y, g + 1)
                dve.reciprocal(rden, den).then_inc(s_rden, 1)
                dve.wait_ge(s_rden, g + 1)
                wait(dve, s_trY, g)
                for b in range(GB):
                    dve.tensor_scalar(yv[:, b, :], banks[0:SLOTS, 6, b * D:(b + 1) * D], rden[:, b:b + 1], None,
                                      ALU.mult).then_inc(s_yv, 1)

            def mix(i, par, cur, prev):
                if more(i):
                    mix_stats(i + 1)
                if prev:
                    combine_weights(i - 1)
                    slot_inputs(i - 1)
                if more(i):
                    weighted_norm(i + 1, 1 - par)
                    clamp_squares(i + 1)
                if cur:
                    shift_logits(i)
                if more(i):
                    unit_tokens(i + 1, 1 - par)
            dve.wait_ge(s_rres, 2 * NG)
            dve.wait_ge(s_cw, CW)
            weighted_norm(0, 0)
            clamp_squares(0)
            unit_tokens(0, 0)
            run_mix(mix)(dve)

            def bias_fc1(n, r):
                dve.wait_ge(s_ht, n + 1)
                wait(dve, s_gl, n - 1)
                dve.tensor_tensor(hb[r % 2].rearrange("p (c b) -> p c b", c=FC),
                                  banks[:, 4 + r % 2, 0:FC * B].rearrange("p (c b) -> p c b", c=FC),
                                  b1[:, bass.ds(n, 1), :].rearrange("p o c -> p c o").broadcast_to((P, FC, B)),
                                  ALU.add).then_inc(s_hb, 1)

            def slot(n, r, k):
                if not isinstance(n, int) or n >= 1:
                    bias_fc1(n - 1, (r - 1) % RING)
                dve.wait_ge(s_fc1, n + 1)
                wait(dve, s_ht, n - 1)
                dve.tensor_copy(hraw[r % 2], banks[0:B, 2 * (r % 2):2 * (r % 2) + 2, :].rearrange("p a n -> p (a n)")
                                [:, 0:FF]).then_inc(s_hr, 1)
            run_slots(dve, slot)
            bias_fc1(SLOTS - 1, RING - 1)

            def combine(g, par, cur, prev):
                if cur:
                    wait(dve, s_co, g - 1)
                    dve.tensor_tensor(y2[par], y2all[:, bass.ds(g * GB, GB), :],
                                      b2.rearrange("p (o d) -> p o d", o=1).broadcast_to((SLOTS, GB, D)),
                                      ALU.add).then_inc(s_y2, 1)
                if not cur:
                    dve.wait_ge(s_cres, 2)
                    ln_stats(dve, Q_ATT, 0)
                if prev:
                    dve.wait_ge(s_co, g)
                    for i in range(2):
                        xt = X[:, bass.ds((g - 1) * GT + 2 * i, 2), :]
                        dve.tensor_tensor(xt, banks[:, 2 * (1 - par) + i, 0:2 * D].rearrange("p (t d) -> p t d", t=2), xt,
                                          ALU.add).then_inc(s_cres, 1)
            dve.wait_ge(s_y2a, 32)
            run_combine(dve, combine)

            def job_wait(n):
                dve.wait_ge(s_jp, n + 1)

            def values(par, t, n, bank=6):
                job_wait(n)
                dve.tensor_tensor(va[par][:, t, :, ::2, :],
                                  banks[:, bank, 0:D].rearrange("p (a h d) -> p a h d", h=2, d=HD1),
                                  vb1.rearrange("p (a h d) -> p a h d", h=2, d=HD1), ALU.add).then_inc(s_je, 1)

            def norm_stats(g):
                ln_stats(dve, Q_ATT + g, g * GT)

            def norm_apply(g, *free):
                ln_apply(dve, Q_ATT + g, g * GT, free)

            def att_residual(g, b, n):
                job_wait(n)
                dve.wait_ge(s_pb, g + 1)
                xt = X[:, bass.ds(g * GT + 2 * b, 2), :]
                dve.tensor_tensor(xt, banks[:, 6, 0:2 * D].rearrange("p (t d) -> p t d", t=2), xt,
                                  ALU.add).then_inc(s_je, 1)

            def keep_transposed(U, par):
                dve.wait_ge(s_pt, U + 1)
                wait(dve, s_av, U - 1)
                dve.tensor_copy(pT[par].rearrange("p h m n -> p h (m n)"), banks[:, HG:2 * HG, :]).then_inc(s_pe, 1)

            def att(g, par, base, jobs):
                for u in range(UN):
                    U = UN * g + u
                    for h in range(HG):
                        n = HG * U + h + 1
                        dve.wait_ge(s_p1, n)
                        dve.reduce_max(smx[:, h, :], banks[:, h, :].rearrange("p (n m) -> p n m", n=2), AX_X).then_inc(s_smx, 1)
                        dve.wait_ge(s_smx, n)
                        dve.tensor_scalar(neg_max[:, 2 * h:2 * h + 2], smx[:, h, :], -1.0, None, ALU.mult).then_inc(s_neg, 1)
                    def job(k):
                        if (u, k) in jobs:
                            kind, item, n = jobs[u, k]
                            if kind == "v":
                                values(1 - par, item, base + n)
                            elif kind == "proj":
                                att_residual(g - item, item, base + n)
                    if u or not isinstance(g, int) or g:
                        keep_transposed(U - 1, (u - 1) % 2)
                    job(0)
                    dve.wait_ge(s_ex, 2 * HG * (U + 1))
                    dve.reciprocal(rden1[u % 2], den1[u % 2]).then_inc(s_rd, 1)
                    job(1)
                    if u == 2 and (UN - 1, 1) in jobs:
                        norm_stats(g + 2)
                    if u == 4 and (UN - 1, 1) in jobs:
                        norm_apply(g + 2, s_jp, base)
            norm_apply(0, s_tr, 2 * Q_ATT)
            dve.wait_ge(s_cres, 2 * NG)
            for v in va:
                dve.memset(v[:, :, :, 1, :], 0.0).then_inc(s_da, 1)
            dve.wait_ge(s_aw, AW)
            dve.tensor_scalar(qkb[:, 0:QC], qkb[:, 0:QC], HD1 ** -0.5, None, ALU.mult).then_inc(s_qb, 1)
            norm_stats(1)
            norm_apply(1, s_jp, 2)
            dve.wait_ge(s_da, 2)
            for t in range(GT):
                values(0, t, 2 + 2 * QC + t, turn(2 + 2 * QC + t))
            run_attention(dve, att)
            keep_transposed(UN * NG - 1, 1)

            def ffn_norm(g):
                ln_stats(dve, Q_FFN + g, g * GT)
                if isinstance(g, int) and g == 0:
                    ln_apply(dve, Q_FFN, 0, (s_jp, JOBS_TAIL))
                else:
                    ln_apply(dve, Q_FFN + g, g * GT, (s_tr, 2 * (Q_ATT + g)))

            cls_n_done = [0]

            def cls_link(ins):
                cls_n_done[0] += 1
                ins.then_inc(s_cls, 1)
                dve.wait_ge(s_cls, cls_n_done[0])

            def over(x, n):
                return x.rearrange("p (s o) -> p s o", o=1).broadcast_to((CT_N, x.shape[1], n))

            def class_norm():
                dve.wait_ge(s_clsg, 16 * NCLS)
                cls_link(dve.bn_stats(cst, cls_x))
                cls_link(dve.bn_aggr(cmv, cst))
                cls_link(dve.tensor_scalar(cpw[:, 0:1], cmv[:, 1:2], EPS, None, ALU.add))
                assert cls_n_done[0] == CLS_VAR
                dve.wait_ge(s_crs, 1)
                cls_link(dve.tensor_scalar(cls_n, cls_x, cmv[:, 0:1], crs[:, 0:1], ALU.subtract, ALU.mult))

            def class_route():
                one = cls_n.rearrange("p (o d) -> p o d", o=1).broadcast_to((CT_N, 2, D))
                cls_link(dve.tensor_tensor(gprod, gates, one, ALU.mult))
                cls_link(dve.reduce_sum(dots, gprod, AX_X))
                dve.wait_ge(s_csq, 3)
                cls_link(dve.tensor_scalar(cpw[:, 1:4], cpw[:, 1:4], 1e-24, None, ALU.max))
                assert cls_n_done[0] == CLS_NORMS
                dve.wait_ge(s_crs, 2)
                cls_link(dve.tensor_scalar(dots, dots, crs[:, 1:2], None, ALU.mult))
                cls_link(dve.tensor_tensor(dots, dots, crs[:, 2:4], ALU.mult))
                cls_link(dve.tensor_tensor(lg1, dots, balance, ALU.add))
                cls_link(dve.reduce_max(lmax, lg1, AX_X))
                cls_link(dve.tensor_scalar(lg1, lg1, lmax, None, ALU.subtract))
                dve.wait_ge(s_cexp2, 1)
                cls_link(dve.reduce_sum(psum_[:, 0:1], prob, AX_X))
                cls_link(dve.reciprocal(psum_[:, 1:2], psum_[:, 0:1]))
                cls_link(dve.tensor_scalar(prob, prob, psum_[:, 1:2], None, ALU.mult))
                cls_link(dve.tensor_tensor(pick[:, 1:2], prob[:, 1:2], prob[:, 0:1], ALU.is_gt))
                cls_link(dve.tensor_scalar(pick[:, 0:1], pick[:, 1:2], -1.0, 1.0, ALU.mult, ALU.add))
                cls_link(dve.tensor_tensor(pick, pick, prob, ALU.mult))

            def class_out():
                for a in range(NATOMS):
                    role, which = ATOM_ROLE[a]
                    w = len(range(NCLS)[which]) * B
                    dve.wait_ge(s_aout, a + 1)
                    for k in range(2):
                        dve.tensor_scalar(classes(cand[1 - role][:, k, :], which),
                                          banks[0:HD, 6 + a % 2, k * w:(k + 1) * w].rearrange("p (n b) -> p n b", b=B),
                                          atom_b2[:, a, k:k + 1], None, ALU.add).then_inc(s_cand, 1)
                for r in range(2):
                    dve.wait_ge(s_candT, 1)
                    wait(dve, s_fin, r)
                    dve.scalar_tensor_tensor(fin[r], banks[0:CT_N, 7, r * D:(r + 1) * D], pick[:, r:r + 1],
                                             fin[0] if r else cls_x, ALU.mult, ALU.add).then_inc(s_fin, 1)

            def ffn(g, par, cur, prev):
                if cur and not (isinstance(g, int) and g == NG - 1):
                    ffn_norm(g + 1)
                if prev:
                    dve.wait_ge(s_f2, g)
                    dve.wait_ge(s_b2f, g)
                    for i in range(2):
                        xt = X[:, bass.ds((g - 1) * GT + 2 * i, 2), :]
                        dve.tensor_tensor(xt, banks[:, 6 + i, 0:2 * D].rearrange("p (t d) -> p t d", t=2), xt,
                                          ALU.add).then_inc(s_eres, 1)
                if isinstance(g, int) and g == 0:
                    class_norm()
                    class_route()
                if isinstance(g, int) and g == NG - 1:
                    class_out()
            ffn_norm(0)
            att_residual(NG - 1, 1, JOBS_TAIL)
            dve.wait_ge(s_je, JOBS_TAIL + 1)
            dve.wait_ge(s_fw, FW)
            run_mix(ffn)(dve)

        @block.scalar
        def _(act):
            act.wait_ge(s_sw, 32)
            act.activation(slT_junk[:, :], slots, ACT.Square, accum_out=sln2[:, 0:1]).then_inc(s_slq, 1)
            act.wait_ge(s_slp, 1)
            act.activation(slT[:, :, :], banks[0:HD, 0, 0:2 * SLOTS].rearrange("p (k s) -> p k s", k=2),
                           ACT.Identity).then_inc(s_slT, 1)
            act.wait_ge(s_nbd, 1)
            act.wait_ge(s_pads, 2)

            def col(lay, c):
                return vec[:, bass.ds(lay, 1), c:c + 1].rearrange("p a b -> p (a b)")

            def step(j, par, on):
                if 0 in on:
                    if not isinstance(j, int) or j >= 2:
                        act.wait_ge(s_conv, 8 * (j - 1))
                    for k in range(2):
                        act.wait_ge(s_uvp, 4 * j + k + 1)
                        act.activation(upad[par][:, k, :, TAPS - 1:],
                                       banks[0:HD, 4 + k, :].rearrange("p (b t) -> p b t", b=GB),
                                       ACT.Identity, bias=col(j // NG, V_BU + k), scale=1.0).then_inc(s_uve, 1)
                    if not isinstance(j, int) or j >= 2:
                        act.wait_ge(s_wop, j - 1)
                    for k in range(2):
                        act.wait_ge(s_uvp, 4 * j + k + 3)
                        act.activation(sv[par][:, k, :], banks[0:HD, 6 + k, :], ACT.Sigmoid,
                                       bias=col(j // NG, V_BV + k), scale=1.0).then_inc(s_uve, 1)
                if -1 in on:
                    q = j + 1
                    act.wait_ge(s_uvp, 4 * q)
                    for k in range(2):
                        act.wait_ge(s_tr, 2 * q + k + 1)
                        act.activation(hT[:, k, :], banks[0:HD, k, :], ACT.Identity,
                                       bias=col(q // NG, V_BT + k), scale=col(q // NG, V_G + k)).then_inc(s_hT, 1)
                if 1 in on:
                    q = j - 1
                    for n, (dst, c, free) in enumerate(((dec, V_NBD, s_scan), (Bs, V_BB, s_inp), (Cs, V_BC, s_hc))):
                        act.wait_ge(free, q)
                        for k in range(2):
                            act.wait_ge(s_zp, 6 * q + 2 * n + k + 1)
                            act.activation(dst[:, k, :], banks[0:HD, 4 + (2 * n + k) % 4, :],
                                           ACT.Sigmoid if n == 0 else ACT.Identity,
                                           bias=col(q // NG, c + k), scale=-1.0 if n == 0 else 1.0).then_inc(s_ze, 1)
            run_tok(act, step)

            def plain_hT(q, free, value):
                act.wait_ge(free, value)
                for k in range(2):
                    act.wait_ge(s_tr, 2 * q + k + 1)
                    act.activation(hT[:, k, :], banks[0:HD, k, :], ACT.Identity).then_inc(s_hT, 1)

            def ret(g, cur, prev):
                if not cur:
                    return
                act.wait_ge(s_pv, H0 * g)
                for i in range(GT):
                    act.wait_ge(s_vgp, 7 * g + i + 1)
                    act.activation(vt[:, i, :], banks[:, 4, 0:HV], ACT.Identity).then_inc(s_vge, 1)
                act.wait_ge(s_ng, g)
                for c in range(NCH):
                    act.wait_ge(s_vgp, 7 * g + GT + c + 1)
                    act.activation(gate[:, c, :], banks[:, 4, :], ACT.Silu).then_inc(s_vge, 1)
                    if c != 1:
                        act.wait_ge(s_pv, H0 * g + (2 if c == 0 else 4))
                        act.activation(oT[:, c // 2, :], banks[:, 5, :], ACT.Identity).then_inc(s_oT, 1)
                if not (isinstance(g, int) and g == NG - 1):
                    plain_hT(NT + g + 1, s_qkp, 12 * (g + 1))
                act.wait_ge(s_pv, H0 * g + 6)
                act.activation(oT[:, 2, :], banks[:, 5, :], ACT.Identity).then_inc(s_oT, 1)
            plain_hT(NT, s_uvp, 4 * NT)
            act.wait_ge(s_res, TOK_DONE)
            run_groups(act, ret)

            def squares(i, par):
                act.wait_ge(s_xw, i + 1)
                wait(act, s_n2c, i)
                wait(act, s_n2, GT * i)
                for t in range(GT):
                    act.activation(sq[:, t, :], xw[par][:, t, :], ACT.Square, accum_out=n2[:, t:t + 1]).then_inc(s_n2, 1)

            def mix(i, par, cur, prev):
                g = i - 1
                if prev:
                    act.wait_ge(s_nmx, g + 1)
                    wait(act, s_tre, g)
                    wait(act, s_yv, 2 * g)
                    for b in range(GB):
                        act.activation(E_[:, b * S:(b + 1) * S], banks[0:SLOTS, 2, b * S:(b + 1) * S], ACT.Exp,
                                       bias=nmx[:, b:b + 1], scale=1.0, accum_out=den[:, b:b + 1]).then_inc(s_E, 1)
                    act.wait_ge(s_sub, g + 1)
                    act.activation(Cl, Cl, ACT.Exp).then_inc(s_cexp, 1)
                if prev:
                    act.wait_ge(s_tre, g + 1)
                    wait(act, s_y, g)
                    act.activation(eT, banks[:, 4, 0:GT * SLOTS].rearrange("p (t s) -> p t s", t=GT),
                                   ACT.Identity).then_inc(s_eT, 1)
                if cur:
                    if isinstance(i, int) and i == 0:
                        plain_hT(Q_MIX, s_qkp, 12 * NG)
                    else:
                        plain_hT(Q_MIX + i, s_lt, 2 * i)
                if prev:
                    act.wait_ge(s_trc, g + 1)
                    act.activation(CT[:, bass.ds(g * N, N)], banks[0:SLOTS, 5, :], ACT.Identity).then_inc(s_CT, 1)
                if more(i):
                    squares(i + 1, 1 - par)
                    wait(act, s_warm, i)
                    act.activation(warm[:, :], mhalf[:, 0:1], ACT.Exp).then_inc(s_warm, 1)
                if prev:
                    act.wait_ge(s_trY, g + 1)
                    for b in range(GB):
                        act.activation(YT[:, :, :, bass.ds(g * GB + b, 1)].rearrange("p k s o -> p k (s o)"),
                                       banks[0:HD, 7, b * 2 * SLOTS:(b + 1) * 2 * SLOTS]
                                       .rearrange("p (k s) -> p k s", k=2), ACT.Identity).then_inc(s_YT, 1)
            act.wait_ge(s_rres, 2 * NG)
            squares(0, 0)
            run_mix(mix)(act)

            def copy_input(n, r):
                wait(act, s_fc1, n - 1)
                act.activation(ys[r % 2], YT[:, :, bass.ds(n, 1), :].rearrange("p k o b -> p k (o b)"),
                               ACT.Identity).then_inc(s_ys, 1)

            def hidden(n, r):
                act.wait_ge(s_hb, n + 1)
                wait(act, s_fc2, n - 1)
                act.activation(gl[r % 2], hb[r % 2], ACT.Gelu).then_inc(s_gl, 1)

            def slot_output(n, r, k):
                act.wait_ge(s_fc2, n + 1)
                if r == 0:
                    wait(act, s_y2d, 16 * k)
                act.activation(fo[:, r, :], banks[0:B, 6 + r % 2, 0:D], ACT.Identity).then_inc(s_y2c, 1)
                if r == RING - 1:
                    act.wait_ge(s_y2c, n + 1)
                    act.dma_start(slot_out[bass.ds(RING * k, RING)].rearrange("s b d -> b s d"), fo
                                  ).then_inc(s_y2d, 16)

            def slot(n, r, k):
                before = (r - 2) % RING
                started = not isinstance(n, int) or n >= 2
                if started:
                    hidden(n - 2, before)
                copy_input(n, r)
                if started:
                    slot_output(n - 2, before, k if r >= 2 else k - 1)
            act.wait_ge(s_YT, GB * NG)
            run_slots(act, slot)
            for r in range(RING - 2, RING):
                hidden(SLOTS - RING + r, r)
                slot_output(SLOTS - RING + r, r, SLOTS // RING - 1)

            def combine(g, par, cur, prev):
                if cur:
                    wait(act, s_co, g - 1)
                    act.activation(CTs[par], CT[:, bass.ds(g * N, N)], ACT.Identity).then_inc(s_cp, 1)
            run_combine(act, combine)

            def half_hT(k, n):
                act.wait_ge(s_jp, n + 1)
                act.activation(hT[:, k, :], banks[0:HD, 6, :], ACT.Identity).then_inc(s_je, 1)

            def qk_out(par, i, n, bank=6):
                w, c = i % 2, i // 2
                act.wait_ge(s_jp, n + 1)
                m = w * QC + c
                act.activation(qkT[par][m], banks[0:QT, bank, :], ACT.Identity, bias=qkb[:, m:m + 1],
                               scale=1.0 if w else HD1 ** -0.5).then_inc(s_je, 1)

            def exps(U, par):
                wait(act, s_pt, U - 1)
                wait(act, s_rd, U - 1)
                for h in range(HG):
                    act.wait_ge(s_neg, HG * U + h + 1)
                    for n in range(2):
                        act.activation(probs[par][:, h, n, :], banks[:, h, n * S:(n + 1) * S], ACT.Exp,
                                       bias=neg_max[:, 2 * h + n:2 * h + n + 1], scale=1.0,
                                       accum_out=den1[par][:, 2 * h + n:2 * h + n + 1]).then_inc(s_ex, 1)

            def keep_output(n_b, used):
                act.wait_ge(s_av, QG * (n_b + 1))
                act.wait_ge(s_jp, used)
                act.activation(aoT, banks[0:HD, 7, :].rearrange("p (k n) -> p k n", k=2), ACT.Identity).then_inc(s_ao, 1)

            def att(g, par, base, jobs):
                for u in range(UN):
                    exps(UN * g + u, u % 2)
                    for k in range(2):
                        if (u, k) in jobs:
                            kind, item, n = jobs[u, k]
                            if kind == "qk":
                                qk_out(1 - par, item, base + n)
                            elif kind == "hT":
                                half_hT(item, base + n)
                    if u == 1 and not (isinstance(g, int) and g == 0):
                        keep_output(GB * g - 1, base)
                    if u == 5:
                        keep_output(GB * g, base + (jobs[3, 1][2] + 1 if (3, 1) in jobs else 0))
            for k in range(2):
                half_hT(k, k)
            act.wait_ge(s_cres, 2 * NG)
            act.wait_ge(s_qb, 1)
            for i in range(2 * QC):
                qk_out(0, i, 2 + i, turn(2 + i))
            for k in range(2):
                half_hT(k, JOBS_FIRST - 2 + k)
            run_attention(act, att)
            keep_output(GB * NG - 1, JOBS_TAIL)

            def ffn(g, par, cur, prev):
                if cur:
                    wait(act, s_f2, g - 1)
                    for c in range(FC):
                        act.wait_ge(s_f1, FC * g + c + 1)
                        act.activation(hid[par][:, c, :], banks[:, 2 + (FC * par + c) % 4, :], ACT.Gelu,
                                       bias=b1f[:, c:c + 1], scale=1.0).then_inc(s_gf, 1)
                    if not (isinstance(g, int) and g == NG - 1):
                        plain_hT(Q_ATT + g + 1, s_f1, FC * (g + 1))
                if isinstance(g, int) and g == 0:
                    act.wait_ge(s_cls, CLS_VAR + 1)
                    act.activation(csq[:, 0, :], cls_n, ACT.Square, accum_out=cpw[:, 1:2]).then_inc(s_csq, 1)
                    for r in range(2):
                        act.activation(csq[:, 1 + r, :], gates[:, r, :], ACT.Square,
                                       accum_out=cpw[:, 2 + r:3 + r]).then_inc(s_csq, 1)
                    act.wait_ge(s_clT, 1)
                    act.activation(cls_T, banks[0:HD, 6, 0:2 * CT_N].rearrange("p (k n) -> p k n", k=2),
                                   ACT.Identity).then_inc(s_clTe, 1)
                    for a in range(NATOMS):
                        role, which = ATOM_ROLE[a]
                        w = len(range(NCLS)[which]) * B
                        act.wait_ge(s_ain, a + 1)
                        for c in range(FC):
                            act.activation(classes(cls_h[role][:, c, :], which),
                                           banks[:, 7 - a % 2, c * w:(c + 1) * w].rearrange("p (n b) -> p n b", b=B),
                                           ACT.Gelu, bias=atom_b1[:, a, c:c + 1], scale=1.0).then_inc(s_ag, 1)
                    act.wait_ge(s_cls, CLS_NORMS + 5)
                    act.activation(prob, lg1, ACT.Exp).then_inc(s_cexp2, 1)
            plain_hT(Q_ATT, s_jp, JOBS_TAIL)
            act.wait_ge(s_je, JOBS_TAIL + 1)
            act.wait_ge(s_fw, FW)
            run_mix(ffn)(act)

        @block.tensor
        def _(pe):
            pe.wait_ge(s_const, 6)
            pe.wait_ge(s_sl, 2)
            for k in range(2):
                ins = pe.transpose(banks[0:HD, 0, k * SLOTS:(k + 1) * SLOTS], slots[:, k * HD:(k + 1) * HD],
                                   ident[0:SLOTS, 0:SLOTS])
            ins.then_inc(s_slp, 1)
            pe.wait_ge(s_slT, 1)

            def two_halves(o, w, x):
                pe.matmul(o, w(0), x(0), start=True, stop=False)
                return pe.matmul(o, w(1), x(1), start=False, stop=True)

            def wo_part(j, par):
                pe.wait_ge(s_wout, (j // NG + 1) * 16)
                pe.wait_ge(s_uve, 4 * j + 4)
                pe.wait_ge(s_res, GT * j)
                for i in range(GT):
                    ins = two_halves(banks[:, 2 + i // 2, (i % 2) * D:(i % 2 + 1) * D],
                                     lambda k: sv[par][:, k, i * P:(i + 1) * P], lambda k: wout[:, k, :])
                ins.then_inc(s_wop, 1)

            def y_part(j, transposed):
                pe.wait_ge(s_hsum, j + 1)
                if transposed:
                    pe.wait_ge(s_hT, 2 * (j + 4))
                for i in range(GT):
                    ins = pe.transpose(banks[:, 0, i * HD:(i + 1) * HD], hsum[:, i * P:(i + 1) * P], ident[0:HD, 0:HD])
                ins.then_inc(s_yp, 1)

            def uv_part(j):
                pe.wait_ge(s_win, (j // NG + 1) * 16)
                pe.wait_ge(s_hT, 2 * j + 2)
                for c in range(4):
                    if not isinstance(j, int) or j >= 2:
                        pe.wait_ge(s_ze, 6 * (j - 2) + (5, 6, 3, 4)[c])
                    two_halves(banks[0:HD, 4 + c, :], lambda k: win[:, k, c * HD:(c + 1) * HD],
                               lambda k: hT[:, k, :]).then_inc(s_uvp, 1)

            def zbc_part(j, uv_between, between):
                pe.wait_ge(s_wzbc, (j // NG + 1) * 16)
                pe.wait_ge(s_conv, 8 * j + 8)
                for c in range(6):
                    if c == 2:
                        between()
                    if c >= 4:
                        pe.wait_ge(s_ze, 6 * j + c - 3)
                    elif uv_between:
                        pe.wait_ge(s_uve, 4 * (j + 1) + c + 1)
                    else:
                        pe.wait_ge(s_ze, 6 * (j - 1) + (5, 6, 3, 4)[c])
                    two_halves(banks[0:HD, 4 + c % 4, :], lambda k: wzbc[:, k, c * HD:(c + 1) * HD],
                               lambda k: uc[:, k, :]).then_inc(s_zp, 1)

            def step(j, par, on):
                if 2 in on:
                    wo_part(j - 2, par)
                if 0 in on:
                    uv_part(j)
                if -1 in on:
                    wait(pe, s_ysum, j - 2)
                    transpose_group(pe, j + 1)

                def y_between():
                    if 2 in on:
                        y_part(j - 2, -1 in on)
                if 1 in on:
                    zbc_part(j - 1, 0 in on, y_between)
                else:
                    y_between()
            run_tok(pe, step)

            def vg(g, n):
                pe.wait_ge(s_vge, 7 * g + n)
                if n < GT:
                    two_halves(banks[:, 4, 0:HV], lambda k: hT[:, k, n * P:(n + 1) * P],
                               lambda k: wv[:, k, :]).then_inc(s_vgp, 1)
                else:
                    c = n - GT
                    two_halves(banks[:, 4, :], lambda k: wg[:, k, c * P:(c + 1) * P],
                               lambda k: hT[:, k, :]).then_inc(s_vgp, 1)

            def qk_item(g, h, w):
                n = 12 * g + 2 * h + w
                if not isinstance(g, int) or n >= 2:
                    pe.wait_ge(s_rot, 3 * (n - 1))
                two_halves(banks[:, 2 + w, :], lambda k: (wq, wk)[w][:, k, h * P:(h + 1) * P],
                           lambda k: hT[:, k, :]).then_inc(s_qkp, 1)

            def scores(g, h):
                head = H0 * g + h
                q, k = qk[0][h % 2], qk[1][h % 2]
                pe.wait_ge(s_radd, 2 * (head + 1))
                for b in range(GB):
                    if not isinstance(g, int) or head >= 1:
                        pe.wait_ge(s_pm, 2 * (head - 1) + b + 1)
                    pe.matmul(banks[:, 6 + b, 0:S], k[:, b * S:b * S + P], q[:, b * S:(b + 1) * S],
                              start=True, stop=True)
                    pe.matmul(banks[:, 6 + b, S:MW], k[:, b * S + P:(b + 1) * S], q[:, b * S + P:(b + 1) * S],
                              start=True, stop=True).then_inc(s_sp, 1)

            def pv(g, h):
                head = H0 * g + h
                if h % 2 == 0:
                    pe.wait_ge(s_oT, NCH * g + h // 2)
                pe.wait_ge(s_pm, 2 * head + 2)
                pe.wait_ge(s_vge, 7 * g + GT)
                r = (h % 2) * DV
                for b in range(GB):
                    pe.matmul(banks[r:r + DV, 5, b * S:(b + 1) * S], vt[:, 2 * b, h * DV:(h + 1) * DV],
                              pm[h % 2][:, b, 0:S], start=True, stop=False)
                    ins = pe.matmul(banks[r:r + DV, 5, b * S + P:(b + 1) * S], vt[:, 2 * b + 1, h * DV:(h + 1) * DV],
                                    pm[h % 2][:, b, S:MW], start=False, stop=True)
                ins.then_inc(s_pv, 1)

            def gn_sums(g):
                pe.wait_ge(s_gn, GN_STEPS * g + 14)
                pe.wait_ge(s_hT, 2 * (NT + g + 1) if not isinstance(g, int) or g < NG - 1 else 2 * (NT + NG))
                pe.matmul(banks[:, 0, 400:400 + 4 * NCH], blk, gmv.rearrange("p n s -> p (n s)"),
                          start=True, stop=True).then_inc(s_gstat, 1)

            def ret_out(g):
                pe.wait_ge(s_ng, g + 1)
                for i in range(GT):
                    for c in range(NCH):
                        ins = pe.matmul(banks[:, i // 2, (i % 2) * D:(i % 2 + 1) * D], ng[:, c, i * P:(i + 1) * P],
                                        wo[:, c, :], start=c == 0, stop=c == NCH - 1)
                ins.then_inc(s_rop, 1)

            def ret(g, cur, prev):
                if cur:
                    pe.wait_ge(s_hT, 2 * (NT + g) + 2)
                for h in range(H0):
                    if cur:
                        for w in range(2):
                            if 2 * h + w < GT:
                                vg(g, 2 * h + w)
                            elif w == 0 and h >= 3:
                                vg(g, GT + h - 3)
                            qk_item(g, h, w)
                    if prev and h == 1:
                        gn_sums(g - 1)
                    if cur and h >= 2:
                        pv(g, h - 2)
                    if cur and h >= 1:
                        scores(g, h - 1)
                if prev:
                    ret_out(g - 1)
                if cur:
                    pv(g, H0 - 2)
                    scores(g, H0 - 1)
                    if not (isinstance(g, int) and g == NG - 1):
                        pe.wait_ge(s_rres, 2 * g)
                        transpose_group(pe, NT + g + 1)
                    pv(g, H0 - 1)
            pe.wait_ge(s_rw, RET_W)
            pe.wait_ge(s_ysum, NT)
            transpose_group(pe, NT)
            pe.wait_ge(s_res, TOK_DONE)
            run_groups(pe, ret)

            def mix(i, par, cur, prev):
                g = i - 1
                if prev:
                    pe.wait_ge(s_E, 2 * g + 2)
                    wait(pe, s_eT, g)
                    for t in range(GT):
                        ins = flip(pe, banks[:, 4, t * SLOTS:(t + 1) * SLOTS], E_[:, t * P:(t + 1) * P],
                                   ident[0:SLOTS, 0:SLOTS], t == 0)
                    ins.then_inc(s_tre, 1)
                    pe.wait_ge(s_eT, g + 1)
                    wait(pe, s_yv, 2 * g)
                    for b in range(GB):
                        ins = two_halves(banks[0:SLOTS, 6, b * D:(b + 1) * D], lambda k: eT[:, 2 * b + k, :],
                                         lambda k: xw[1 - par][:, 2 * b + k, :])
                    ins.then_inc(s_y, 1)
                if cur:
                    pe.wait_ge(s_tokn, GT * (i + 1))
                    pe.wait_ge(s_hT, 2 * (Q_MIX + i))
                    for k in range(2):
                        for t in range(GT):
                            ins = pe.transpose(banks[0:HD, k, t * P:(t + 1) * P], tokn[:, t, k * HD:(k + 1) * HD],
                                               ident[:, :])
                        ins.then_inc(s_tr, 1)
                if prev:
                    pe.wait_ge(s_cn, g + 1)
                    wait(pe, s_CT, g)
                    for t in range(GT):
                        ins = flip(pe, banks[0:SLOTS, 5, t * P:(t + 1) * P], Cl[:, t, :], ident[:, :], t == 0)
                    ins.then_inc(s_trc, 1)
                if cur:
                    pe.wait_ge(s_hT, 2 * (Q_MIX + i) + 2)
                    wait(pe, s_E, 2 * i)
                    two_halves(banks[0:SLOTS, 2, :], lambda k: slT[:, k, :], lambda k: hT[:, k, :]).then_inc(s_lt, 1)
                    wait(pe, s_sub, i)
                    for t in range(GT):
                        ins = two_halves(banks[:, 3, t * SLOTS:(t + 1) * SLOTS],
                                         lambda k: hT[:, k, t * P:(t + 1) * P], lambda k: slT[:, k, :])
                    ins.then_inc(s_lt, 1)
                if prev:
                    pe.wait_ge(s_yv, 2 * g + 2)
                    wait(pe, s_YT, 2 * g)
                    for b in range(GB):
                        for k in range(2):
                            c = (2 * b + k) * SLOTS
                            ins = flip(pe, banks[0:HD, 7, c:c + SLOTS], yv[:, b, k * HD:(k + 1) * HD],
                                       ident[0:SLOTS, 0:SLOTS], b + k == 0)
                    ins.then_inc(s_trY, 1)
            pe.wait_ge(s_rres, 2 * NG)
            run_mix(mix)(pe)

            def fc1(n, r, k):
                pe.wait_ge(s_w1[r], 16 * (k + 1))
                pe.wait_ge(s_ys, n + 1)
                wait(pe, s_hr, n - 1)
                for a, w in ((0, 512), (1, FF - 512)):
                    ins = two_halves(banks[0:B, 2 * (r % 2) + a, 0:w], lambda h: ys[r % 2][:, h, :],
                                     lambda h: ring1[r][:, h, 512 * a:512 * a + w])
                ins.then_inc(s_fc1, 1)

            def transpose_hidden(n, r):
                wait(pe, s_hb, n - 1)
                pe.wait_ge(s_hr, n + 1)
                for c in range(FC):
                    ins = flip(pe, banks[:, 4 + r % 2, c * B:(c + 1) * B], hraw[r % 2][:, c * P:(c + 1) * P],
                               ident[0:B, 0:B], c == 0)
                ins.then_inc(s_ht, 1)

            def fc2(n, r, k):
                pe.wait_ge(s_w2[r], 16 * (k + 1))
                wait(pe, s_y2c, n - 1)
                pe.wait_ge(s_gl, n + 1)
                for c in range(FC):
                    ins = pe.matmul(banks[0:B, 6 + r % 2, 0:D], gl[r % 2][:, c * B:(c + 1) * B], ring2[r][:, c, :],
                                    start=c == 0, stop=c == FC - 1)
                ins.then_inc(s_fc2, 1)

            def slot(n, r, k):
                if isinstance(n, int) and n == 0:
                    fc1(n, r, k)
                    return
                before = (r - 1) % RING
                transpose_hidden(n - 1, before)
                fc1(n, r, k)
                fc2(n - 1, before, k if r else k - 1)
            pe.wait_ge(s_YT, GB * NG)
            run_slots(pe, slot)
            transpose_hidden(SLOTS - 1, RING - 1)
            fc2(SLOTS - 1, RING - 1, SLOTS // RING - 1)

            def combine(g, par, cur, prev):
                if cur:
                    pe.wait_ge(s_y2, g + 1)
                    pe.wait_ge(s_cp, g + 1)
                    wait(pe, s_cres, 2 * (g - 1))
                    for t in range(GT):
                        ins = pe.matmul(banks[:, 2 * par + t // 2, (t % 2) * D:(t % 2 + 1) * D],
                                        CTs[par][:, t * P:(t + 1) * P], y2[par][:, t // 2, :], start=True, stop=True)
                    ins.then_inc(s_co, 1)
            run_combine(pe, combine)

            def task(n):
                lax = isinstance(n, int) and 2 < n < JOBS_FIRST - 2 and n != 2 + 2 * QC
                wait(pe, s_je, n - lax)

            def half_transpose(q, k, n):
                task(n)
                pe.wait_ge(s_xn, GT * (q + 1))
                for t in range(GT):
                    ins = pe.transpose(banks[0:HD, 6, t * P:(t + 1) * P], xn[:, t, k * HD:(k + 1) * HD], ident[:, :])
                ins.then_inc(s_jp, 1)

            def qk_in(i, n, bank=6):
                task(n)
                m = ((i % 2) * QC + i // 2) * QT
                two_halves(banks[0:QT, bank, :], lambda k: wqk[:, k, m:m + QT], lambda k: hT[:, k, :]).then_inc(s_jp, 1)

            def v_in(t, n, bank=6):
                task(n)
                two_halves(banks[:, bank, 0:D], lambda k: hT[:, k, t * P:(t + 1) * P],
                           lambda k: wv1[:, k, :]).then_inc(s_jp, 1)

            def project(n_b, n):
                task(n)
                pe.wait_ge(s_ao, n_b + 1)
                for t in range(2):
                    ins = two_halves(banks[:, 6, t * D:(t + 1) * D], lambda k: aoT[:, k, t * P:(t + 1) * P],
                                     lambda k: wp1[:, k, :])
                ins.then_inc(s_jp, 1)

            def scores(U, u, par):
                b, c = u // QG, u % QG
                q, k = qkT[par][c * HG // TH], kd[u % 2]
                pe.wait_ge(s_kd, U + 1)
                for h in range(HG):
                    if not isinstance(U, int) or U:
                        pe.wait_ge(s_ex, 2 * (HG * (U - 1) + h + 1))
                    for m in range(2):
                        ins = pe.matmul(banks[:, h, m * S:(m + 1) * S], q[:, b * S + m * P:b * S + (m + 1) * P],
                                        k[:, h, :], start=True, stop=True)
                    ins.then_inc(s_p1, 1)

            def transpose_probs(U, par):
                pe.wait_ge(s_pn, U + 1)
                wait(pe, s_pe, U)
                for h in range(HG):
                    for n in range(2):
                        for m in range(2):
                            c = (2 * m + n) * P
                            ins = pe.transpose(banks[:, HG + h, c:c + P], probs[par][:, h, n, m * P:(m + 1) * P], ident[:, :])
                ins.then_inc(s_pt, 1)

            def values_out(U, u, par):
                b, c = u // QG, u % QG
                pe.wait_ge(s_pe, U + 1)
                if c == 0:
                    wait(pe, s_ao, U // QG if isinstance(U, int) else (U - u) // QG + b)
                for h in range(HG):
                    head = HG * c + h
                    half, row = head // TH, head % TH // 2 * 2 * HD1
                    odd = head % 2
                    v = va[par].rearrange("p t a x d -> p t a (x d)")
                    for m in range(2):
                        ins = pe.matmul(banks[row:row + 2 * HD1, 7, half * S:(half + 1) * S],
                                        v[:, 2 * b + m, head // 2, odd * HD1:(odd + 2) * HD1], pT[u % 2][:, h, m, :],
                                        start=not odd and m == 0, stop=bool(odd and m == 1))
                ins.then_inc(s_av, 1)

            def run_job(g, base, job):
                kind, item, n = job
                n = base + n
                if kind == "qk":
                    qk_in(item, n)
                elif kind == "v":
                    v_in(item, n)
                elif kind == "proj":
                    project(GB * g - 1 if item else GB * g, n)
                elif kind == "hT":
                    half_transpose(Q_ATT + g + 2, item, n)

            def att(g, par, base, jobs):
                for u in range(UN):
                    U = UN * g + u
                    scores(U, u, par)
                    if u or not isinstance(g, int) or g:
                        transpose_probs(U - 1, (u - 1) % 2)
                    if (u, 0) in jobs:
                        run_job(g, base, jobs[u, 0])
                    if u >= 2 or not isinstance(g, int) or g:
                        values_out(U - 2, (u - 2) % UN, par if u >= 2 else 1 - par)
                    if (u, 1) in jobs:
                        run_job(g, base, jobs[u, 1])
            pe.wait_ge(s_aw, AW)
            for k in range(2):
                half_transpose(Q_ATT, k, k)
            for i in range(2 * QC):
                qk_in(i, 2 + i, turn(2 + i))
            for t in range(GT):
                v_in(t, 2 + 2 * QC + t, turn(2 + 2 * QC + t))
            for k in range(2):
                half_transpose(Q_ATT + 1, k, JOBS_FIRST - 2 + k)
            run_attention(pe, att)
            last = UN * NG
            transpose_probs(last - 1, 1)
            values_out(last - 2, UN - 2, 1)
            values_out(last - 1, UN - 1, 1)
            project(GB * NG - 1, JOBS_TAIL)
            def ffn(g, par, cur, prev):
                if cur:
                    pe.wait_ge(s_hT, 2 * (Q_ATT + g) + 2)
                    for c in range(FC):
                        wait(pe, s_gf, FC * g + c - 3)
                        two_halves(banks[:, 2 + (FC * par + c) % 4, :], lambda k: w1f[:, k, c * P:(c + 1) * P],
                                   lambda k: hT[:, k, :]).then_inc(s_f1, 1)
                    if not (isinstance(g, int) and g == NG - 1):
                        transpose_group(pe, Q_FFN + g + 1, Q_ATT + g + 1)
                if prev:
                    pe.wait_ge(s_gf, FC * g)
                    wait(pe, s_eres, 2 * (g - 1))
                    if isinstance(g, int) and g == 1:
                        pe.wait_ge(s_ag, FC * NATOMS)
                    if isinstance(g, int) and g == NG:
                        pe.wait_ge(s_fin, 2)
                    for t in range(GT):
                        for c in range(FC):
                            ins = pe.matmul(banks[:, 6 + t // 2, (t % 2) * D:(t % 2 + 1) * D],
                                            hid[1 - par][:, c, t * P:(t + 1) * P], w2f[:, c, :],
                                            start=c == 0, stop=c == FC - 1)
                    ins.then_inc(s_f2, 1)
                if isinstance(g, int) and g == 0:
                    class_in()
                if isinstance(g, int) and g == NG - 1:
                    class_candidates()

            def class_in():
                pe.wait_ge(s_cls, CLS_VAR + 1)
                for k in range(2):
                    ins = pe.transpose(banks[0:HD, 6, k * CT_N:(k + 1) * CT_N], cls_n[:, k * HD:(k + 1) * HD],
                                       ident[0:CT_N, 0:CT_N])
                ins.then_inc(s_clT, 1)
                pe.wait_ge(s_clTe, 1)
                pe.wait_ge(s_atom, ATOMS_W)
                for a in range(NATOMS):
                    which = ATOM_ROLE[a][1]
                    w = len(range(NCLS)[which]) * B
                    wait(pe, s_ag, FC * (a - 1))
                    for c in range(FC):
                        ins = two_halves(banks[:, 7 - a % 2, c * w:(c + 1) * w].rearrange("p (n b) -> p n b", b=B),
                                         lambda k: atom_in[a][:, k, c * P:(c + 1) * P],
                                         lambda k: classes(cls_T[:, k, :], which))
                    ins.then_inc(s_ain, 1)

            def class_candidates():
                pe.wait_ge(s_ag, FC * NATOMS)
                pe.wait_ge(s_eres, 2 * (NG - 1))
                for a in range(NATOMS):
                    role, which = ATOM_ROLE[a]
                    w = len(range(NCLS)[which]) * B
                    wait(pe, s_cand, 2 * (a - 1))
                    for k in range(2):
                        for c in range(FC):
                            ins = pe.matmul(banks[0:HD, 6 + a % 2, k * w:(k + 1) * w].rearrange("p (n b) -> p n b", b=B),
                                            atom_out[a][:, c, k * HD:(k + 1) * HD],
                                            classes(cls_h[1 - role][:, c, :], which), start=c == 0, stop=c == FC - 1)
                    ins.then_inc(s_aout, 1)
                pe.wait_ge(s_cand, 2 * NATOMS)
                for r in range(2):
                    for k in range(2):
                        ins = pe.transpose(banks[0:CT_N, 7, r * D + k * HD:r * D + (k + 1) * HD], cand[r][:, k, :],
                                           ident[0:HD, 0:HD])
                ins.then_inc(s_candT, 1)

            transpose_group(pe, Q_FFN, Q_ATT)
            pe.wait_ge(s_je, JOBS_TAIL + 1)
            pe.wait_ge(s_fw, FW)
            run_mix(ffn)(pe)


def halves(w):
    w = np.swapaxes(np.asarray(w), -1, -2)
    return np.ascontiguousarray(np.moveaxis(w.reshape(*w.shape[:-2], 2, HD, w.shape[-1]), -3, -2))


def columns(v):
    v = np.asarray(v)
    return np.moveaxis(v.reshape(*v.shape[:-1], -1, HD), -1, 0)


def rows(w, n):
    return w.reshape(-1, n, w.shape[1]).transpose(1, 0, 2)


def retention_tables():
    f = np.float32
    half = DQK // 2
    t = np.arange(S, dtype=f)
    angles = t[:, None] * (f(1) / f(10000) ** (np.arange(half, dtype=f) / f(half)))[None, :]
    zeta = (np.arange(half, dtype=f) + f(half)) / f(DQK)
    tables = {}
    for name, sign in (("q", f(1)), ("k", f(-1))):
        decay = zeta[None, :] ** (sign * t[:, None] / f(512))
        cos, sin = (np.cos(angles) * decay).T, (np.sin(angles) * decay).T
        tables["cos_" + name] = np.concatenate([cos, cos])
        tables["sin_" + name] = np.concatenate([sin, -sin])
    gammas = np.array([1.0 - 2.0 ** (-(5 + h)) for h in range(H0)], f)
    diff = t[:, None] - t[None, :]
    m = gammas[:, None, None] ** np.maximum(diff, f(0))[None] * (diff >= 0).astype(f)[None]
    m = m / np.sqrt(np.maximum(m.sum(-1, keepdims=True, dtype=f), f(1e-6))) * f(DQK ** -0.5)
    keys = m.transpose(2, 0, 1)
    tables["mask"] = np.concatenate([keys[:P], keys[P:, :, P:]], axis=2).astype(f)
    tables["blk"] = np.kron(np.eye(P // DV, dtype=f), np.full((DV, DV), 1 / DV, f))
    return tables


def kernel(**a):
    import concourse.bacc as bacc
    from concourse.bass_utils import run_bass_kernel_spmd

    a = {k: np.asarray(v) for k, v in a.items()}
    t = {k[len("L0_tok_"):]: v for k, v in a.items() if k.startswith("L0_tok_")}
    data = {
        "tok_idx": a["x"].reshape(TILES, P).T,
        "emb": t["embedding"],
        "pos": t["pos_enc"].reshape(2, P, D).transpose(1, 0, 2),
        "win": halves(t["Win"]),
        "wzbc": halves(np.concatenate([t["Wd"], t["WB"], t["WC"]], axis=1)),
        "wout": halves(t["Wout"]),
        "vec": np.concatenate([columns(v) for v in (
            t["ln_g"], t["ln_b"], t["b_in"], *[t["convw"][:, :, k] for k in range(TAPS)], t["convb"],
            t["bd"], t["bB"], t["bC"])], axis=2),
        "bout": t["bout"],
    }
    r = {k[len("L0_attn_"):]: v for k, v in a.items() if k.startswith("L0_attn_")}
    data.update(rq=rows(r["Wq"], HD), rk=rows(r["Wk"], HD), rv=rows(r["Wv"], HD), rg=rows(r["Wg"], HD),
                ro=rows(r["Wo"], P), gnw=r["gn_weight"].reshape(NCH, P).T, gnb=r["gn_bias"].reshape(NCH, P).T,
                **retention_tables())
    f = {k[len("L0_ffn_"):]: v for k, v in a.items() if k.startswith("L0_ffn_")}
    data.update(slots=f["slots"], slot_scale=f["scale"][:, None], normw=f["norm_weight"], b2=f["fc2_bias"],
                b1=f["fc1_bias"].reshape(SLOTS, FC, P).transpose(2, 0, 1),
                fc1=f["fc1_weight"].reshape(SLOTS, 2, HD, FF).transpose(0, 2, 1, 3),
                fc2=f["fc2_weight"].reshape(SLOTS, FC, P, D).transpose(0, 2, 1, 3))
    m = {k[len("L1_attn_"):]: v for k, v in a.items() if k.startswith("L1_attn_")}
    wq, wk, wv = np.split(m["qkv_w"], 3)
    bq, bk, bv = np.split(m["qkv_b"], 3)
    data.update(wqk=halves(np.concatenate([wq, wk])), wv1=halves(wv), wp1=halves(m["proj_w"]),
                qkb=np.concatenate([bq, bk]).reshape(2 * QC, QT).T, vb1=bv, pb1=m["proj_b"])
    e = {k[len("L1_ffn_"):]: v for k, v in a.items() if k.startswith("L1_ffn_")}
    data.update(w1f=halves(e["fc1_w"]), w2f=rows(e["fc2_w"].T, P), b1f=e["fc1_b"].reshape(FC, P).T, b2f=e["fc2_b"],
                atom_in=halves(e["atom_in_w"]),
                atom_out=e["atom_out_w"].transpose(0, 2, 1).reshape(NATOMS, FC, P, D).transpose(0, 2, 1, 3),
                atom_b1=e["atom_in_b"].reshape(NATOMS, FC, P).transpose(2, 0, 1),
                atom_b2=e["atom_out_b"].reshape(NATOMS, 2, HD).transpose(2, 0, 1),
                gates=np.repeat(e["gate_pair"], B, axis=0), balance=np.repeat(e["balance_bias"], B, axis=0))
    nc = bacc.Bacc("TRN2", target_bir_lowering=False, num_devices=1)
    data = {f"in_{k}": np.ascontiguousarray(v) for k, v in data.items()}
    A = {k[3:]: nc.dram_tensor(k, v.shape, mybir.dt.from_np(v.dtype), kind="ExternalInput").ap()
         for k, v in data.items()}
    out = nc.dram_tensor("out", (B * S, D), F32, kind="ExternalOutput").ap()
    slot_out = nc.dram_tensor("slot_out", (SLOTS, B, D), F32, kind="Internal").ap()
    build(nc, A, out, slot_out)
    r = run_bass_kernel_spmd(nc, [data], core_ids=[0])
    return r.results[0]["out"].reshape(B, S, D)
```
